# Optimizing a Trainium2 kernel written in Bass

```python
import numpy as np
import jax
import jax.numpy as jnp

def _softmax(x, axis=-1):
    return jax.nn.softmax(x, axis=axis)

def _gelu(x):
    return jax.nn.gelu(x, approximate=True)

def _silu(x):
    return jax.nn.silu(x)

def _sigmoid(x):
    return jax.nn.sigmoid(x)

def _layernorm(x, axis=-1, eps=1e-05):
    m = jnp.mean(x, axis=axis, keepdims=True)
    v = jnp.var(x, axis=axis, keepdims=True)
    return (x - m) / jnp.sqrt(v + eps)

def _scatter_add(tgt, idx, src, axis=0):
    return tgt.at[idx].add(src)

def _segment_sum(src, seg, n):
    return jax.ops.segment_sum(src, seg, n)
kernel_name = 'mk_lm_tower_d2_tok_ids512_r4_747af0'

def setup_inputs(seed: int=0):
    np.random.seed(seed)
    _w = jnp.asarray

    def _rec_inputs():
        import jax
        import jax.numpy as jnp
        _rk = jax.random.key(seed)
        x = jax.random.randint(jax.random.fold_in(_rk, 1), (32, 128), 0, 22, jnp.int32)
        itok_BS_0_21 = jax.random.randint(jax.random.fold_in(_rk, 21), (32, 128), 0, 22, jnp.int32)
        return (x, itok_BS_0_21)
    x, itok_BS_0_21 = _rec_inputs()

    def _L0_tok_setup():
        import jax, jax.numpy as jnp
        import numpy as np
        NEG = -100000000.0

        def nw_value(theta, A):
            N, M = theta.shape
            ii = jnp.arange(N + 1)
            neg1 = jnp.full((1,), NEG, theta.dtype)
            prev2 = jnp.full((N + 1,), NEG, theta.dtype).at[0].set(0.0)
            prev = jnp.full((N + 1,), NEG, theta.dtype)

            def step(carry, d):
                prev, prev2 = carry
                jj = d - ii
                valid = (ii >= 1) & (ii <= N) & (jj >= 1) & (jj <= M)
                th = theta[jnp.clip(ii - 1, 0, N - 1), jnp.clip(jj - 1, 0, M - 1)]
                diag = jnp.concatenate([neg1, prev2[:-1]])
                up = jnp.concatenate([neg1, prev[:-1]]) + A
                left = prev + A
                v = jax.nn.logsumexp(jnp.stack([diag, up, left]), axis=0)
                new = jnp.where(valid, th + v, NEG)
                return ((new, prev), None)
            (last, _), _ = jax.lax.scan(step, (prev, prev2), jnp.arange(2, N + M + 1))
            return last[N]
        key = jax.random.key(seed)
        ks = jax.random.split(key, 7)
        B, N, M = (16, 128, 128)
        n_alpha, n_input, n_embed = (22, 128, 128)
        return {'x': jax.random.randint(ks[0], (B, N), 0, n_alpha, dtype=jnp.int32), 'y': jax.random.randint(ks[1], (B, M), 0, n_alpha, dtype=jnp.int32), 'W_embed': jax.random.normal(ks[2], (n_alpha, n_input), jnp.float32) * 0.1, 'W_proj': jax.random.normal(ks[3], (n_input, n_embed), jnp.float32) * 0.05, 'b_proj': jax.random.normal(ks[4], (n_embed,), jnp.float32) * 0.01, 'W_gap': jax.random.normal(ks[5], (2 * n_embed,), jnp.float32) * 0.05, 'b_gap': jax.random.normal(ks[6], (1,), jnp.float32) * 0.01}
    _L0_tok_all = _L0_tok_setup()
    _L0_tok_in = {k: v for k, v in _L0_tok_all.items() if k in ('W_embed', 'W_proj', 'b_proj', 'W_gap', 'b_gap')}
    del _L0_tok_all

    def _L0_attn_setup():
        import jax, jax.numpy as jnp
        import numpy as np
        GAMMA = 0.96875
        HIDDEN = 128
        key = jax.random.key(seed)
        kx, kq, kk, kv = jax.random.split(key, 4)
        B, S, H = (8, 512, HIDDEN)
        X = jax.random.normal(kx, (B, S, H), dtype=jnp.float32)
        W_Q = jax.random.normal(kq, (H, H), dtype=jnp.float32) / H
        W_K = jax.random.normal(kk, (H, H), dtype=jnp.float32) / H
        W_V = jax.random.normal(kv, (H, H), dtype=jnp.float32) / H
        return {'X': X, 'W_Q': W_Q, 'W_K': W_K, 'W_V': W_V}
    _L0_attn_all = _L0_attn_setup()
    _L0_attn_in = {k: v for k, v in _L0_attn_all.items() if k in ('W_Q', 'W_K', 'W_V')}
    del _L0_attn_all

    def _L0_ffn_setup():
        import jax, jax.numpy as jnp
        import numpy as np
        D_MODEL = 128
        N_HEADS = 8
        KV_OPTS = (8, 4, 1)
        D_K = D_MODEL // N_HEADS

        def gqa(x, wq, wk, wv, wo, n_kv):
            B, S, _ = x.shape
            groups = N_HEADS // n_kv
            q = (x @ wq).reshape(B, S, N_HEADS, D_K).transpose(0, 2, 1, 3)
            k = (x @ wk).reshape(B, S, n_kv, D_K).transpose(0, 2, 1, 3)
            v = (x @ wv).reshape(B, S, n_kv, D_K).transpose(0, 2, 1, 3)
            k = jnp.repeat(k, groups, axis=1)
            v = jnp.repeat(v, groups, axis=1)
            scores = jnp.einsum('bhqd,bhkd->bhqk', q, k) / jnp.sqrt(jnp.float32(D_K))
            attn = jax.nn.softmax(scores, axis=-1)
            out = jnp.einsum('bhqk,bhkd->bhqd', attn, v)
            out = out.transpose(0, 2, 1, 3).reshape(B, S, D_MODEL)
            return out @ wo
        key = jax.random.key(seed)
        ks = jax.random.split(key, 32)
        it = iter(ks)
        s = 0.02
        inp = {'x': jax.random.normal(next(it), (64, 256, D_MODEL), dtype=jnp.float32)}
        inp['r_w1'] = jax.random.normal(next(it), (D_MODEL, D_MODEL // 4), jnp.float32) * s
        inp['r_b1'] = jnp.zeros((D_MODEL // 4,), jnp.float32)
        inp['r_w2'] = jax.random.normal(next(it), (D_MODEL // 4, len(KV_OPTS)), jnp.float32) * s
        inp['r_b2'] = jnp.zeros((len(KV_OPTS),), jnp.float32)
        for i, nkv in enumerate(KV_OPTS):
            inp[f'wq{i}'] = jax.random.normal(next(it), (D_MODEL, D_MODEL), jnp.float32) * s
            inp[f'wk{i}'] = jax.random.normal(next(it), (D_MODEL, nkv * D_K), jnp.float32) * s
            inp[f'wv{i}'] = jax.random.normal(next(it), (D_MODEL, nkv * D_K), jnp.float32) * s
            inp[f'wo{i}'] = jax.random.normal(next(it), (D_MODEL, D_MODEL), jnp.float32) * s
        return inp
    _L0_ffn_all = _L0_ffn_setup()
    _L0_ffn_in = {k: v for k, v in _L0_ffn_all.items() if k in ('r_w1', 'r_b1', 'r_w2', 'r_b2', 'wq0', 'wk0', 'wv0', 'wo0', 'wq1', 'wk1', 'wv1', 'wo1', 'wq2', 'wk2', 'wv2', 'wo2')}
    del _L0_ffn_all

    def _L1_attn_setup():
        import jax, jax.numpy as jnp
        import numpy as np
        B, S, D = (8, 256, 128)
        K, H = (64, 8)
        key = jax.random.key(seed)
        ks = jax.random.split(key, 8)
        s = lambda fan_in: 1.0 / np.sqrt(fan_in)
        return {'x': jax.random.normal(ks[0], (B, S, D), dtype=jnp.float32), 'Wq': jax.random.uniform(ks[1], (D, K * H), jnp.float32, -s(D), s(D)), 'Wk': jax.random.uniform(ks[2], (D, K * H), jnp.float32, -s(D), s(D)), 'Wv': jax.random.uniform(ks[3], (D, D * H), jnp.float32, -s(D), s(D)), 'Wo': jax.random.uniform(ks[4], (D * H, D), jnp.float32, -s(D * H), s(D * H)), 'bo': jax.random.uniform(ks[5], (D,), jnp.float32, -s(D * H), s(D * H)), 'gamma': jnp.ones((D,), jnp.float32), 'beta': jnp.zeros((D,), jnp.float32)}
    _L1_attn_all = _L1_attn_setup()
    _L1_attn_in = {k: v for k, v in _L1_attn_all.items() if k in ('Wq', 'Wk', 'Wv', 'Wo', 'bo', 'gamma', 'beta')}
    del _L1_attn_all

    def _L1_ffn_setup():
        import jax, jax.numpy as jnp
        import numpy as np
        B, T, D = (4, 2048, 128)
        E, F, CAP = (8, 512, 1024)
        key = jax.random.key(seed)
        ks = jax.random.split(key, 6)
        s = 0.02
        return {'x': jax.random.normal(ks[0], (B, T, D), dtype=jnp.float32), 'Wr': jax.random.normal(ks[1], (D, E), dtype=jnp.float32) * s, 'W1': jax.random.normal(ks[2], (E, D, F), dtype=jnp.float32) * s, 'b1': jax.random.normal(ks[3], (E, F), dtype=jnp.float32) * s, 'W2': jax.random.normal(ks[4], (E, F, D), dtype=jnp.float32) * s, 'b2': jax.random.normal(ks[5], (E, D), dtype=jnp.float32) * s}
    _L1_ffn_all = _L1_ffn_setup()
    _L1_ffn_in = {k: v for k, v in _L1_ffn_all.items() if k in ('Wr', 'W1', 'b1', 'W2', 'b2')}
    del _L1_ffn_all
    return {'x': x, 'itok_BS_0_21': itok_BS_0_21, 'L0_tok_W_embed': _L0_tok_in['W_embed'], 'L0_tok_W_proj': _L0_tok_in['W_proj'], 'L0_tok_b_proj': _L0_tok_in['b_proj'], 'L0_tok_W_gap': _L0_tok_in['W_gap'], 'L0_tok_b_gap': _L0_tok_in['b_gap'], 'L0_attn_W_Q': _L0_attn_in['W_Q'], 'L0_attn_W_K': _L0_attn_in['W_K'], 'L0_attn_W_V': _L0_attn_in['W_V'], 'L0_ffn_r_w1': _L0_ffn_in['r_w1'], 'L0_ffn_r_b1': _L0_ffn_in['r_b1'], 'L0_ffn_r_w2': _L0_ffn_in['r_w2'], 'L0_ffn_r_b2': _L0_ffn_in['r_b2'], 'L0_ffn_wq0': _L0_ffn_in['wq0'], 'L0_ffn_wk0': _L0_ffn_in['wk0'], 'L0_ffn_wv0': _L0_ffn_in['wv0'], 'L0_ffn_wo0': _L0_ffn_in['wo0'], 'L0_ffn_wq1': _L0_ffn_in['wq1'], 'L0_ffn_wk1': _L0_ffn_in['wk1'], 'L0_ffn_wv1': _L0_ffn_in['wv1'], 'L0_ffn_wo1': _L0_ffn_in['wo1'], 'L0_ffn_wq2': _L0_ffn_in['wq2'], 'L0_ffn_wk2': _L0_ffn_in['wk2'], 'L0_ffn_wv2': _L0_ffn_in['wv2'], 'L0_ffn_wo2': _L0_ffn_in['wo2'], 'L1_attn_Wq': _L1_attn_in['Wq'], 'L1_attn_Wk': _L1_attn_in['Wk'], 'L1_attn_Wv': _L1_attn_in['Wv'], 'L1_attn_Wo': _L1_attn_in['Wo'], 'L1_attn_bo': _L1_attn_in['bo'], 'L1_attn_gamma': _L1_attn_in['gamma'], 'L1_attn_beta': _L1_attn_in['beta'], 'L1_ffn_Wr': _L1_ffn_in['Wr'], 'L1_ffn_W1': _L1_ffn_in['W1'], 'L1_ffn_b1': _L1_ffn_in['b1'], 'L1_ffn_W2': _L1_ffn_in['W2'], 'L1_ffn_b2': _L1_ffn_in['b2']}

def reference(x, itok_BS_0_21, L0_tok_W_embed, L0_tok_W_proj, L0_tok_b_proj, L0_tok_W_gap, L0_tok_b_gap, L0_attn_W_Q, L0_attn_W_K, L0_attn_W_V, L0_ffn_r_w1, L0_ffn_r_b1, L0_ffn_r_w2, L0_ffn_r_b2, L0_ffn_wq0, L0_ffn_wk0, L0_ffn_wv0, L0_ffn_wo0, L0_ffn_wq1, L0_ffn_wk1, L0_ffn_wv1, L0_ffn_wo1, L0_ffn_wq2, L0_ffn_wk2, L0_ffn_wv2, L0_ffn_wo2, L1_attn_Wq, L1_attn_Wk, L1_attn_Wv, L1_attn_Wo, L1_attn_bo, L1_attn_gamma, L1_attn_beta, L1_ffn_Wr, L1_ffn_W1, L1_ffn_b1, L1_ffn_W2, L1_ffn_b2):
    import jax
    import jax.numpy as jnp

    def _L0_tok_ref(x, y, W_embed, W_proj, b_proj, W_gap, b_gap):
        import jax, jax.numpy as jnp
        import numpy as np
        NEG = -100000000.0

        def nw_value(theta, A):
            N, M = theta.shape
            ii = jnp.arange(N + 1)
            neg1 = jnp.full((1,), NEG, theta.dtype)
            prev2 = jnp.full((N + 1,), NEG, theta.dtype).at[0].set(0.0)
            prev = jnp.full((N + 1,), NEG, theta.dtype)

            def step(carry, d):
                prev, prev2 = carry
                jj = d - ii
                valid = (ii >= 1) & (ii <= N) & (jj >= 1) & (jj <= M)
                th = theta[jnp.clip(ii - 1, 0, N - 1), jnp.clip(jj - 1, 0, M - 1)]
                diag = jnp.concatenate([neg1, prev2[:-1]])
                up = jnp.concatenate([neg1, prev[:-1]]) + A
                left = prev + A
                v = jax.nn.logsumexp(jnp.stack([diag, up, left]), axis=0)
                new = jnp.where(valid, th + v, NEG)
                return ((new, prev), None)
            (last, _), _ = jax.lax.scan(step, (prev, prev2), jnp.arange(2, N + M + 1))
            return last[N]
        zx = jnp.take(W_embed, x, axis=0) @ W_proj + b_proj
        zy = jnp.take(W_embed, y, axis=0) @ W_proj + b_proj
        theta = jnp.einsum('bid,bjd->bij', zx, zy)
        merged = jnp.concatenate([zx.mean(axis=1), zy.mean(axis=1)], axis=1)
        A = merged @ W_gap + b_gap[0]
        aln = jax.vmap(jax.grad(nw_value, argnums=0))(theta, A)
        return aln

    def _L0_attn_ref(X, W_Q, W_K, W_V):
        import jax, jax.numpy as jnp
        import numpy as np
        GAMMA = 0.96875
        HIDDEN = 128
        Q = X @ W_Q
        K = X @ W_K
        V = X @ W_V
        S_len = X.shape[1]
        idx = jnp.arange(S_len)
        D = GAMMA ** jnp.abs(idx[None, :] - idx[:, None]).astype(X.dtype)
        scores = jnp.einsum('bsh,bth->bst', Q, K) * D
        ret = jnp.einsum('bst,bth->bsh', scores * jax.nn.sigmoid(scores), V)
        return ret

    def _L0_ffn_ref(x, r_w1, r_b1, r_w2, r_b2, wq0, wk0, wv0, wo0, wq1, wk1, wv1, wo1, wq2, wk2, wv2, wo2):
        import jax, jax.numpy as jnp
        import numpy as np
        D_MODEL = 128
        N_HEADS = 8
        KV_OPTS = (8, 4, 1)
        D_K = D_MODEL // N_HEADS

        def gqa(x, wq, wk, wv, wo, n_kv):
            B, S, _ = x.shape
            groups = N_HEADS // n_kv
            q = (x @ wq).reshape(B, S, N_HEADS, D_K).transpose(0, 2, 1, 3)
            k = (x @ wk).reshape(B, S, n_kv, D_K).transpose(0, 2, 1, 3)
            v = (x @ wv).reshape(B, S, n_kv, D_K).transpose(0, 2, 1, 3)
            k = jnp.repeat(k, groups, axis=1)
            v = jnp.repeat(v, groups, axis=1)
            scores = jnp.einsum('bhqd,bhkd->bhqk', q, k) / jnp.sqrt(jnp.float32(D_K))
            attn = jax.nn.softmax(scores, axis=-1)
            out = jnp.einsum('bhqk,bhkd->bhqd', attn, v)
            out = out.transpose(0, 2, 1, 3).reshape(B, S, D_MODEL)
            return out @ wo
        routing_input = x.mean(axis=1)
        logits = jax.nn.relu(routing_input @ r_w1 + r_b1) @ r_w2 + r_b2
        sel = jnp.argmax(jax.nn.softmax(logits, axis=-1), axis=-1)
        params = [(wq0, wk0, wv0, wo0), (wq1, wk1, wv1, wo1), (wq2, wk2, wv2, wo2)]
        out = jnp.zeros_like(x)
        for i, nkv in enumerate(KV_OPTS):
            yi = gqa(x, *params[i], nkv)
            mask = (sel == i)[:, None, None]
            out = jnp.where(mask, yi, out)
        return out

    def _L1_attn_ref(x, Wq, Wk, Wv, Wo, bo, gamma, beta):
        import jax, jax.numpy as jnp
        import numpy as np
        B, S, D = (8, 256, 128)
        K, H = (64, 8)
        b, s, d = x.shape
        q = (x @ Wq).reshape(b, s, H, K)
        k = (x @ Wk).reshape(b, s, H, K)
        v = (x @ Wv).reshape(b, s, H, D)
        scores = jnp.einsum('bqhk,bshk->hbqs', q, k) / np.sqrt(K).astype(np.float32)
        scores = jnp.where(scores == 0, jnp.float32(-1000000000.0), scores)
        att = jax.nn.softmax(scores, axis=-1)
        o = jnp.einsum('hbqs,bshd->bqhd', att, v).reshape(b, s, H * D)
        o = o @ Wo + bo
        y = o + x
        mu = jnp.mean(y, axis=-1, keepdims=True)
        var = jnp.mean(jnp.square(y - mu), axis=-1, keepdims=True)
        return (y - mu) * jax.lax.rsqrt(var + 1e-06) * gamma + beta

    def _L1_ffn_ref(x, Wr, W1, b1, W2, b2):
        import jax, jax.numpy as jnp
        import numpy as np
        B, T, D = (4, 2048, 128)
        E, F, CAP = (8, 512, 1024)
        Bb, Tt, Dd = x.shape
        N = Bb * Tt
        C = min(CAP, N)
        x_flat = x.reshape(N, Dd)
        logits = x_flat @ Wr
        probs = jax.nn.softmax(logits, axis=0)
        vals, idx = jax.lax.top_k(probs.T, C)
        selected = x_flat[idx]
        h = jax.nn.gelu(jnp.einsum('ecd,edf->ecf', selected, W1) + b1[:, None, :], approximate=False)
        out_e = jnp.einsum('ecf,efd->ecd', h, W2) + b2[:, None, :]
        weighted = vals[..., None] * out_e
        output = jnp.zeros_like(x_flat).at[idx.reshape(-1)].add(weighted.reshape(-1, Dd))
        return output.reshape(Bb, Tt, Dd)
    h = _L0_tok_ref(x, itok_BS_0_21, L0_tok_W_embed, L0_tok_W_proj, L0_tok_b_proj, L0_tok_W_gap, L0_tok_b_gap)
    h = h + _L0_attn_ref(_layernorm(h, axis=-1), L0_attn_W_Q, L0_attn_W_K, L0_attn_W_V)
    h = h + _L0_ffn_ref(_layernorm(h, axis=-1), L0_ffn_r_w1, L0_ffn_r_b1, L0_ffn_r_w2, L0_ffn_r_b2, L0_ffn_wq0, L0_ffn_wk0, L0_ffn_wv0, L0_ffn_wo0, L0_ffn_wq1, L0_ffn_wk1, L0_ffn_wv1, L0_ffn_wo1, L0_ffn_wq2, L0_ffn_wk2, L0_ffn_wv2, L0_ffn_wo2)
    h = h + _L1_attn_ref(_layernorm(h, axis=-1), L1_attn_Wq, L1_attn_Wk, L1_attn_Wv, L1_attn_Wo, L1_attn_bo, L1_attn_gamma, L1_attn_beta)
    h = h + _L1_ffn_ref(_layernorm(h, axis=-1), L1_ffn_Wr, L1_ffn_W1, L1_ffn_b1, L1_ffn_W2, L1_ffn_b2)
    return h

_drawn_inputs = setup_inputs


def setup_inputs(seed=0):
    import zlib

    import numpy as np

    out = dict(_drawn_inputs(seed))
    spreads = {'L0_ffn_r_b1': (0.0, 0.1),
     'L0_ffn_r_b2': (0.0, 0.1),
     'L1_attn_gamma': (1.0, 0.2),
     'L1_attn_beta': (0.0, 0.1)}
    factors = {'L0_tok_b_proj': 4.745,
     'L0_tok_W_gap': 8.0,
     'L0_ffn_wq2': 2.891,
     'L1_attn_bo': 3.062,
     'L1_ffn_Wr': 64.0,
     'L1_ffn_W1': 64.0,
     'L1_ffn_b1': 64.0,
     'L1_ffn_W2': 55.813,
     'L1_ffn_b2': 64.0}
    for name, (base, spread) in spreads.items():
        noise = np.random.default_rng([zlib.crc32(name.encode()), seed]).standard_normal(out[name].shape)
        drawn = base * np.exp(spread * noise) if base else spread * noise
        out[name] = jnp.asarray(drawn.astype(out[name].dtype))
    for name, factor in factors.items():
        out[name] = (out[name] * factor).astype(out[name].dtype)
    return out
```

```python
import math
from contextlib import ExitStack

import concourse.bass as bass
from concourse import mybir

F32 = mybir.dt.float32
I32 = mybir.dt.int32
BF16 = mybir.dt.bfloat16
ALU = mybir.AluOpType
ACT = mybir.ActivationFunctionType
AX = mybir.AxisListType

B, S, D = 32, 128, 128
P = 128
V = 22
VP = 33
G = 4
NG = B // G
HALF = S // 2
CH = 16
NCH = S // CH


def alignment_stage(nc, used, A, H, ident, psum):
    w_dram = nc.dram_tensor("w_dram", (2, 2, B, S, HALF), F32, kind="Internal").ap()
    r_dram = nc.dram_tensor("r_dram", (2, 2 * B, S, HALF), F32, kind="Internal").ap()
    with ExitStack() as ctx:
        sb = lambda name, shape, dt=F32: ctx.enter_context(nc.sbuf_tensor(name, shape, dt))
        sem = lambda name: used.append(nc.alloc_semaphore(name)) or used[-1]
        onehot = sb("onehot", [VP, 3, B * S])
        letter = sb("letter", [VP, 1])
        emb = sb("emb", [V, P])
        wproj = sb("wproj", [P, P])
        bproj = sb("bproj", [P, 1])
        wgap = sb("wgap", [P, 2])
        bgap = sb("bgap", [V, 1])
        embT = sb("embT", [P, V])
        zT = sb("zT", [P, V])
        pair = sb("pair", [VP, VP])
        gap = sb("gap", [V, 2])
        gapcol = sb("gapcol", [V, 2, VP])
        counts = sb("counts", [V, 2, 4, B])
        gapscore = sb("gapscore", [VP, B])
        crow = sb("crow", [P, 1])
        pairY = sb("pairY", [VP, B * S])
        theta = sb("theta", [P, B, S])
        w_rows = sb("w_rows", [P, 2, B, S])
        w_dp = sb("w_dp", [P, S + 2, HALF])
        tok = w_dp[0:VP, 0:S, :].rearrange("v i j -> v (i j)").bitcast(I32).rearrange("v (k t) -> v k t", k=2)
        hist = sb("hist", [P, S + 2, HALF + 1])
        R = sb("R", [P, HALF])
        bb = sb("bb", [P, HALF])
        aa = sb("aa", [P, HALF])
        rH = sb("rH", [P, HALF])
        mm_ = sb("mm_", [P, HALF])
        ratios = w_rows
        tri = sb("tri", [P, 2, P])
        th1 = sb("th1", [B, S])
        bfin = sb("bfin", [P, HALF])
        last = sb("last", [B, S])
        ones_bs = sb("ones_bs", [B, S])
        path1 = sb("path1", [B, S])
        lnlast = sb("lnlast", [B, S])
        dd = sb("dd", [P, 2, G * S])

        s_tok = sem("s_tok"); s_w = sem("s_w"); s_const = sem("s_const"); s_pc = sem("s_pc")
        s_embT = sem("s_embT"); s_embTc = sem("s_embTc"); s_z = sem("s_z"); s_zc = sem("s_zc")
        s_pair = sem("s_pair"); s_pairc = sem("s_pairc"); s_gc = sem("s_gc")
        s_hot = sem("s_hot"); s_one = sem("s_one"); s_cnt = sem("s_cnt"); s_A = sem("s_A"); s_Ac = sem("s_Ac")
        s_c = sem("s_c")
        s_y = sem("s_y"); s_yc = sem("s_yc"); s_yA = sem("s_yA")
        s_th = sem("s_th"); s_exp = sem("s_exp"); s_thc = sem("s_thc")
        s_wdp = [sem(f"s_wdp{q}") for q in range(NCH)]
        s_wst = sem("s_wst")
        s_rst = [sem(f"s_rst{q}") for q in range(NCH)]
        s_dve = sem("s_dve"); s_scan = sem("s_scan"); s_hand = sem("s_hand")
        s_rat = [sem(f"s_rathalf{q}") for q in range(2)]
        s_rat0 = sem("s_rat0"); s_th1 = sem("s_th1"); s_bf = sem("s_bf"); s_last = sem("s_last"); s_lnl = sem("s_lnl")
        s_p1 = sem("s_p1"); s_row1 = sem("s_row1"); s_ln = sem("s_ln"); s_D = sem("s_D"); s_dd = sem("s_dd"); s_h = sem("s_h")
        s_dch = sem("s_dch")
        block = ctx.enter_context(nc.Block())

        tokens = (A["x"], A["itok_BS_0_21"])

        @block.sync
        def _(sp):
            for k in range(2):
                src = tokens[k].rearrange("b s -> (b s)").unsqueeze(0).broadcast_to([VP, B * S])
                sp.dma_start(tok[:, k, :], src).then_inc(s_tok, 16)
            for n in range(2 * NG):
                m, d = n // 2, n % 2
                sp.wait_ge(s_exp, n + 1)
                for half in range(2):
                    dst = w_dram[half, d, m * G:(m + 1) * G, :, :].rearrange("b i j -> i b j")
                    sp.dma_start(dst, w_rows[:, d, m * G:(m + 1) * G, half * HALF:(half + 1) * HALF]).then_inc(s_wst, 16)
            sp.wait_ge(s_wst, 64 * NG)
            for q in range(NCH):
                for half in range(2):
                    r0 = 1 + q * CH + half
                    sp.dma_start(w_dp[half * 64:half * 64 + 64, r0:r0 + CH, :],
                                 w_dram[half, :, :, q * CH:(q + 1) * CH, :].rearrange("d b i j -> (d b) i j")).then_inc(s_wdp[q], 16)
            sp.wait_ge(s_thc, NG)
            sp.dma_start(th1[:, :], theta[0:1, :, :]).then_inc(s_th1, 16)
            sp.wait_ge(s_rat0, 1)
            for q in range(NCH + 1):
                for half in range(2):
                    if q < NCH:
                        lo = q * CH + (q == 0)
                        sp.wait_ge(s_scan, (q + 1) * CH + half)
                        src = hist[half * 64:half * 64 + 64, 1 + lo + half:1 + (q + 1) * CH + half, 1:]
                        sp.dma_start(r_dram[half, :, lo:(q + 1) * CH, :], src).then_inc(s_rst[q], 16)
                    if q == NCH - 1:
                        sp.wait_ge(s_bf, 1 + half)
                        sp.dma_start(last[:, half * HALF:(half + 1) * HALF], bfin[half * 64 + 32:half * 64 + 64, :]).then_inc(s_last, 16)
                if q:
                    lo = (q - 1) * CH + (q == 1)
                    sp.wait_ge(s_rst[q - 1], 32)
                    for half in range(2):
                        dst = ratios[lo:q * CH, :, :, half * HALF:(half + 1) * HALF].rearrange("i d b j -> i (d b) j")
                        sp.dma_start(dst, r_dram[half, :, lo:q * CH, :].rearrange("p i j -> i p j")).then_inc(s_rat[half], 16)
            sp.wait_ge(s_p1, 1)
            sp.wait_ge(s_ln, 1)
            sp.dma_start(ratios[0:1, 0, :, :], path1[:, :]).then_inc(s_row1, 16)

        @block.gpsimd
        def _(pool):
            pool.dma_start(emb[:, :], A["L0_tok_W_embed"]).then_inc(s_w, 16)
            pool.dma_start(wproj[:, :], A["L0_tok_W_proj"]).then_inc(s_w, 16)
            pool.dma_start(bproj[:, :], A["L0_tok_b_proj"].unsqueeze(1)).then_inc(s_w, 16)
            with nc.allow_non_contiguous_dma("two short columns"):
                pool.dma_start(wgap[:, :], A["L0_tok_W_gap"].rearrange("(k p) -> p k", k=2)).then_inc(s_w, 16)
            pool.dma_start(bgap[:, :], A["L0_tok_b_gap"].unsqueeze(1).broadcast_to([V, 1])).then_inc(s_w, 16)
            pool.memset(ident[:, :], 0.0).then_inc(s_pc, 1)
            pool.iota(letter[:, :], pattern=[[0, 1]], base=0, channel_multiplier=1, allow_small_or_imprecise_dtypes=True).then_inc(s_const, 1)
            pool.memset(pair[:, :], 0.0).then_inc(s_const, 1)
            pool.memset(gapcol[:, :, :], 0.0).then_inc(s_const, 1)
            pool.memset(R[:, :], 1.0).then_inc(s_const, 1)
            pool.memset(ones_bs[:, :], 1.0).then_inc(s_const, 1)
            pool.memset(hist[:, :, 0:1], 0.0).then_inc(s_const, 1)
            pool.memset(tri[:, :, :], 0.0).then_inc(s_pc, 1)
            pool.wait_ge(s_pc, 1)
            pool.affine_select(out=ident[:, :], in_=ident[:, :], compare_op=ALU.not_equal, fill=1.0, base=0,
                               pattern=[[-1, P]], channel_multiplier=1).then_inc(s_const, 1)
            pool.wait_ge(s_pc, 2)
            pool.affine_select(out=tri[:, 0, :], in_=tri[:, 0, :], compare_op=ALU.is_gt, fill=1.0, base=0,
                               pattern=[[-1, P]], channel_multiplier=1).then_inc(s_const, 1)
            pool.affine_select(out=tri[:, 1, :], in_=tri[:, 1, :], compare_op=ALU.is_gt, fill=-1.0, base=P,
                               pattern=[[-1, P]], channel_multiplier=-1).then_inc(s_const, 1)
            pool.wait_ge(s_const, 9)
            pool.wait_ge(s_hot, 3)
            for k in (0, 2):
                pool.memset(onehot[32:33, k, :], 1.0).then_inc(s_one, 1)
            for q in range(NCH):
                pool.wait_ge(s_wdp[q], 32)
            pool.wait_ge(s_one, 2)
            pool.memset(ratios[0:1, :, :, :], 1.0).then_inc(s_rat0, 1)

        @block.tensor
        def _(pe):
            pe.wait_ge(s_w, 80)
            pe.wait_ge(s_const, 7)
            pe.transpose(psum[0][:, 0:V], emb[:, :], ident[0:V, 0:V]).then_inc(s_embT, 1)
            pe.wait_ge(s_embTc, 1)
            pe.matmul(psum[1][:, 0:V], wproj[:, :], embT[:, :], start=True, stop=True).then_inc(s_z, 1)
            pe.wait_ge(s_zc, 1)
            pe.matmul(psum[2][0:V, 0:V], zT[:, :], zT[:, :], start=True, stop=True).then_inc(s_pair, 1)
            pe.matmul(psum[3][0:V, 0:2], zT[:, :], wgap[:, :], start=True, stop=True).then_inc(s_pair, 1)
            pe.wait_ge(s_gc, 4)
            pe.wait_ge(s_cnt, 2)
            pe.matmul(psum[0][0:VP, 0:B], gapcol[:, 0, :], counts[:, 0, 0, :], start=True, stop=False)
            pe.matmul(psum[0][0:VP, 0:B], gapcol[:, 1, :], counts[:, 1, 0, :], start=False, stop=True).then_inc(s_A, 1)
            pe.matmul(psum[1][:, 0:1], counts[:, 0, :, :].rearrange("v r b -> v (r b)"), gap[:, 0:1], start=True, stop=False)
            pe.matmul(psum[1][:, 0:1], counts[:, 1, :, :].rearrange("v r b -> v (r b)"), gap[:, 1:2], start=False, stop=True).then_inc(s_A, 1)
            pe.wait_ge(s_pairc, 1)
            for m in range(NG):
                bank = psum[2 + m % 4]
                if m >= 4:
                    pe.wait_ge(s_yc, m - 3)
                pe.matmul(bank[0:VP, :], pair[:, :], onehot[:, 1, m * 512:(m + 1) * 512], start=True, stop=True).then_inc(s_y, 1)
            pe.wait_ge(s_one, 2)
            pe.wait_ge(s_yA, 1)
            pe.wait_ge(s_c, 1)
            for m in range(NG):
                for d in range(2):
                    n = 2 * m + d
                    bank = psum[n % 8]
                    if n >= 8:
                        pe.wait_ge(s_exp, n - 7)
                    if d == 0 and m >= 4:
                        pe.wait_ge(s_thc, m - 3)
                    for k in range(G):
                        b = m * G + k
                        X = onehot[:, 2 * d, b * S:(b + 1) * S]
                        Y = pairY[:, b * S:(b + 1) * S]
                        if d:
                            Y = Y[:, ::-1]
                        mm = pe.matmul(bank[:, k * S:(k + 1) * S], X, Y, start=True, stop=True)
                    mm.then_inc(s_th, 1)
            pe.wait_ge(s_row1, 16)
            for m in range(NG):
                pe.wait_ge(s_ln, 2)
                if m >= 4:
                    pe.wait_ge(s_dd, m - 3)
                pe.matmul(psum[m % 4][:, :], tri[:, 0, :], ratios[:, 0, m * G:(m + 1) * G, :], start=True, stop=False)
                pe.matmul(psum[m % 4][:, :], tri[:, 1, :], ratios[:, 1, m * G:(m + 1) * G, ::-1], start=False, stop=True).then_inc(s_D, 1)

        @block.scalar
        def _(act):
            act.wait_ge(s_embT, 1)
            act.activation(embT[:, :], psum[0][:, 0:V], ACT.Copy).then_inc(s_embTc, 1)
            act.wait_ge(s_z, 1)
            act.activation(zT[:, :], psum[1][:, 0:V], ACT.Identity, bias=bproj[:, :]).then_inc(s_zc, 1)
            act.wait_ge(s_pair, 1)
            act.activation(pair[0:V, 0:V], psum[2][0:V, 0:V], ACT.Copy).then_inc(s_pairc, 1)
            act.wait_ge(s_A, 2)
            act.activation(crow[:, :], psum[1][:, 0:1], ACT.Exp, scale=-1.0).then_inc(s_c, 1)
            for n in range(2 * NG):
                group = slice((n // 2) * G, (n // 2 + 1) * G)
                if n % 2 == 0:
                    act.wait_ge(s_thc, n // 2 + 1)
                    act.activation(w_rows[:, 0, group, :], theta[:, group, :], ACT.Exp).then_inc(s_exp, 1)
                else:
                    act.wait_ge(s_th, n + 1)
                    act.activation(w_rows[:, 1, group, :], psum[n % 8][:, :], ACT.Exp).then_inc(s_exp, 1)
            def hand(s):
                act.wait_ge(s_scan, s - 1 if not isinstance(s, int) else s - 1)
                act.activation(hist[64:128, bass.ds(s, 1), 0:1], hist[0:64, bass.ds(s - 1, 1), HALF:HALF + 1], ACT.Copy).then_inc(s_hand, 1)
            with act.Fori(3, S + 2) as s:
                hand(s)
            act.wait_ge(s_last, 32)
            act.activation(lnlast[:, 1:S], last[:, 1:S], ACT.Ln).then_inc(s_lnl, 1)
            for half in range(2):
                act.wait_ge(s_rat[half], 16 * NCH)
            for d in range(2):
                act.activation(ratios[:, d, :, :], ratios[:, d, :, :], ACT.Ln).then_inc(s_ln, 1)
            for m in range(NG):
                act.wait_ge(s_dd, m + 1)
                act.activation(H[:, m * G:(m + 1) * G, :], dd[:, m % 2, :], ACT.Exp).then_inc(s_h, 1)

        @block.vector
        def _(dve):
            dve.wait_ge(s_const, 1)
            for k in (1, 0):
                dve.wait_ge(s_tok, 32)
                dve.tensor_scalar(onehot[:, k, :], tok[:, k, :], letter[:, :], None, ALU.is_equal).then_inc(s_hot, 1)
            dve.tensor_scalar(onehot[:, 2, :].rearrange("v (b s) -> v b s", b=B), tok[:, 0, :].rearrange("v (b s) -> v b s", b=B)[:, :, ::-1],
                              letter[:, :], None, ALU.is_equal).then_inc(s_hot, 1)
            dve.wait_ge(s_w, 80)
            dve.wait_ge(s_hot, 2)
            for k in range(2):
                dve.tensor_reduce(counts[:, k, 0, :], onehot[0:V, k, :].rearrange("v (b s) -> v b s", b=B), AX.X, ALU.add).then_inc(s_dch, 1)
            dve.wait_ge(s_dch, 2)
            for k in range(2):
                dve.tensor_copy(counts[:, k, 1:4, :], counts[:, k, 0:1, :].broadcast_to([V, 3, B])).then_inc(s_cnt, 1)
            dve.wait_ge(s_pair, 2)
            dve.tensor_scalar(gap[:, 0:1], psum[3][0:V, 0:1], bgap[:, :], 1.0 / S, ALU.add, ALU.mult).then_inc(s_gc, 1)
            dve.tensor_scalar(gap[:, 1:2], psum[3][0:V, 1:2], 1.0 / S, None, ALU.mult).then_inc(s_gc, 1)
            dve.wait_ge(s_gc, 2)
            for k in range(2):
                dve.tensor_copy(gapcol[:, k, 32:33], gap[:, k:k + 1]).then_inc(s_gc, 1)
            dve.wait_ge(s_A, 1)
            dve.tensor_copy(gapscore[:, :], psum[0][0:VP, 0:B]).then_inc(s_Ac, 1)
            for m in range(NG):
                dve.wait_ge(s_y, m + 1)
                dve.tensor_copy(pairY[:, m * 512:(m + 1) * 512], psum[2 + m % 4][0:VP, :]).then_inc(s_yc, 1)
            dve.wait_ge(s_yc, NG)
            dve.wait_ge(s_Ac, 1)
            dve.tensor_copy(pairY[32:33, :].rearrange("v (b s) -> v b s", b=B),
                            gapscore[32:33, :].unsqueeze(2).broadcast_to([1, B, S])).then_inc(s_yA, 1)
            for m in range(NG):
                dve.wait_ge(s_th, 2 * m + 1)
                dve.tensor_copy(theta[:, m * G:(m + 1) * G, :], psum[(2 * m) % 8][:, :]).then_inc(s_thc, 1)

            dve.wait_ge(s_c, 1)
            done = 0

            def chained(ins):
                ins.then_inc(s_dve, 1)

            def step(s, before, p=slice(0, P)):
                w = w_dp[p, bass.ds(s, 1), :].squeeze(1)
                h = hist[p, bass.ds(s, 1), 1:HALF + 1].squeeze(1)
                hs = hist[p, bass.ds(s, 1), 0:HALF].squeeze(1)
                dve.wait_ge(s_dve, before)
                chained(dve.tensor_tensor(bb[p, :], w, R[p, :], ALU.mult))
                dve.wait_ge(s_dve, before + 1)
                chained(dve.scalar_tensor_tensor(aa[p, :], bb[p, :], crow[p, :], w, ALU.mult, ALU.add))
                dve.wait_ge(s_dve, before + 2)
                dve.wait_ge(s_hand, s - 2)
                dve.tensor_tensor_scan(h, bb[p, :], aa[p, :], hist[p, bass.ds(s, 1), 0:1].squeeze(1), ALU.mult, ALU.add).then_inc(s_scan, 1)
                dve.wait_ge(s_c, 1)
                dve.wait_ge(s_scan, s)
                chained(dve.reciprocal(rH[p, :], h))
                dve.wait_ge(s_dve, before + 3)
                chained(dve.tensor_tensor(mm_[p, :], rH[p, :], hs, ALU.mult))
                dve.wait_ge(s_dve, before + 4)
                chained(dve.tensor_tensor(R[p, :], R[p, :], mm_[p, :], ALU.mult))

            dve.wait_ge(s_wdp[0], 32)
            dve.wait_ge(s_const, 9)
            chained(dve.reciprocal(R[0:64, :], w_dp[0:64, 1, :]))
            dve.wait_ge(s_dve, 1)
            chained(dve.memset(R[0:64, 0:1], 0.0))
            w, h, hs = w_dp[0:64, 2, :], hist[0:64, 2, 1:HALF + 1], hist[0:64, 2, 0:HALF]
            dve.wait_ge(s_dve, 2)
            chained(dve.tensor_tensor(bb[0:64, :], w, R[0:64, :], ALU.mult))
            dve.wait_ge(s_dve, 3)
            chained(dve.scalar_tensor_tensor(aa[0:64, :], bb[0:64, :], crow[0:64, :], w, ALU.mult, ALU.add))
            dve.wait_ge(s_dve, 4)
            dve.tensor_tensor_scan(h, bb[0:64, :], aa[0:64, :], 0.0, ALU.mult, ALU.add).then_inc(s_scan, 2)
            dve.wait_ge(s_scan, 2)
            chained(dve.reciprocal(rH[0:64, :], h))
            dve.wait_ge(s_dve, 5)
            chained(dve.tensor_tensor(mm_[0:64, :], rH[0:64, :], hs, ALU.mult))
            dve.wait_ge(s_dve, 6)
            chained(dve.tensor_tensor(R[0:64, :], R[0:64, :], mm_[0:64, :], ALU.mult))
            chained(dve.reciprocal(R[64:128, :], w_dp[64:128, 2, :]))
            for q in range(NCH):
                first = max(3, q * CH + 1)
                dve.wait_ge(s_wdp[q], 32)
                with dve.Fori(first, (q + 1) * CH + 1) as s:
                    step(s, 8 + (s - 3) * 5)
            before = 8 + (S - 2) * 5
            dve.wait_ge(s_dve, before)
            dve.tensor_tensor(bfin[0:64, :], w_dp[0:64, S, :], R[0:64, :], ALU.mult).then_inc(s_bf, 1)
            step(S + 1, before, slice(64, 128))
            dve.wait_ge(s_dve, before + 5)
            dve.tensor_tensor(bfin[64:128, :], w_dp[64:128, S + 1, :], R[64:128, :], ALU.mult).then_inc(s_bf, 1)

            dve.wait_ge(s_lnl, 1)
            dve.tensor_tensor_scan(path1[:, 1:S], ones_bs[:, 1:S], lnlast[:, 1:S][:, ::-1], 0.0, ALU.mult, ALU.add).then_inc(s_dch, 1)
            dve.memset(path1[:, 0:1], 0.0).then_inc(s_dch, 1)
            dve.wait_ge(s_dch, 4)
            dve.wait_ge(s_th1, 16)
            dve.tensor_tensor(path1[:, :], path1[:, :], th1[:, :], ALU.add).then_inc(s_p1, 1)
            for m in range(NG):
                dve.wait_ge(s_D, m + 1)
                if m >= 2:
                    dve.wait_ge(s_h, m - 1)
                dve.tensor_tensor(dd[:, m % 2, :], psum[m % 4][:, :], theta[:, m * G:(m + 1) * G, :].rearrange("p b s -> p (b s)"),
                                  ALU.subtract).then_inc(s_dd, 1)


HEADS = 8
DK = D // HEADS
KV_HEADS = (8, 4, 1)
PADK = 32
K1 = 64
E = 8
TABW = D + E
DECAY = 0.96875
WQ, WK, WV, WO, WALL = 0, HEADS * PADK, 2 * HEADS * PADK, 2 * HEADS * PADK + D, 2 * HEADS * PADK + 2 * D


def layers_stage(nc, used, A, H, ident, psall, table, logitsT, w1, w2, s_weights):
    psum = [psall[:, i, :] for i in range(8)]
    with ExitStack() as ctx:
        sb = lambda name, shape, dt=F32: ctx.enter_context(nc.sbuf_tensor(name, shape, dt))
        sem = lambda name: used.append(nc.alloc_semaphore(name)) or used[-1]
        wq0 = sb("wq0", [P, P]); wk0 = sb("wk0", [P, P]); wv0 = sb("wv0", [P, P])
        wqT = sb("wqT", [P, P]); wkT = sb("wkT", [P, P]); wkq = sb("wkq", [P, P])
        decay = sb("decay", [P, P])
        rw1 = sb("rw1", [P, 32]); rb1 = sb("rb1", [32, 1]); rw2 = sb("rw2", [32, 3]); rb2 = sb("rb2", [1, 3])
        variants = sb("variants", [P, 3, WALL])
        chosen = sb("chosen", [P, G, WALL])
        wq1 = sb("wq1", [P, HEADS * K1]); wk1 = sb("wk1", [P, HEADS * K1])
        wv1 = sb("wv1", [P, HEADS, D]); wo1 = sb("wo1", [P, HEADS, D])
        wvT = sb("wvT", [P, HEADS, D]); wvo = sb("wvo", [P, HEADS, D])
        bo = sb("bo", [P, D]); gamma = sb("gamma", [P, D]); beta = sb("beta", [P, D])
        wr = sb("wr", [P, E])
        power = sb("power", [P, G])
        stats = sb("stats", [P, G, 6]); mv = sb("mv", [P, G, 2]); ve = sb("ve", [P, G]); rstd = sb("rstd", [P, G])
        xh = sb("xh", [P, G, D]); xT = sb("xT", [P, G, S])
        pT = sb("pT", [P, G, S]); v0 = sb("v0", [P, G, D])
        sd = sb("sd", [P, G, S]); th = sb("th", [P, G, S]); act0 = sb("act0", [P, G, S])
        msum = sb("msum", [P, G]); r1 = sb("r1", [32, G]); lg = sb("lg", [1, G, 3]); c1 = sb("c1", [1, G]); mx1 = sb("mx1", [1, G])
        c2 = sb("c2", [1, G]); sel = sb("sel", [1, G], I32)
        qk = sb("qk", [P, G, 4, S]); v17 = sb("v17", [P, G, HEADS, DK + 1])
        smax = sb("smax", [P, 2, HEADS]); ex = sb("ex", [P, 2, HEADS, S]); exT = sb("exT", [P, 2, HEADS, S])
        rden = sb("rden", [P, 2, HEADS]); o0 = sb("o0", [P, G, D]); oT = sb("oT", [P, G, S])
        qT1 = sb("qT1", [P, 4, G * S]); kT1 = sb("kT1", [P, 4, G * S]); vo = sb("vo", [P, G, HEADS, D])
        s2_ = sb("s2_", [P, HEADS, S]); den = sb("den", [P, 2, HEADS])
        y1 = sb("y1", [P, G, D]); y2 = sb("y2", [P, G, D])

        L = 5
        s_in = sem("s_in"); s_pc = sem("s2_pc"); s_var0 = sem("s_var0")
        s_iota = sem("s_iota"); s_abs = sem("s_abs"); s_dec = sem("s_dec")
        s_wt = sem("s_wt"); s_wtc = sem("s_wtc"); s_m0 = sem("s_m0"); s_m0c = sem("s_m0c")
        s_bn = [sem(f"s_bn{i}") for i in range(L)]; s_mv = [sem(f"s_mv{i}") for i in range(L)]
        s_ve = sem("s_ve"); s_rstd = sem("s_rstd"); s_xh = [sem(f"s_xh{i}") for i in range(L)]
        s_xT = [sem(f"s_xT{i}") for i in range(4)]; s_xTc = [sem(f"s_xTc{i}") for i in range(4)]
        s_p = sem("s_p"); s_pT = sem("s_pT"); s_v0 = sem("s_v0"); s_v0c = sem("s_v0c"); s_s0 = sem("s_s0"); s_sd = sem("s_sd")
        s_th = sem("s2_th"); s_act0 = sem("s_act0"); s_o = sem("s_o"); s_h = [sem(f"s_h{i}") for i in range(3)]
        s_ms = sem("s_ms"); s_r1 = sem("s_r1"); s_r1c = sem("s_r1c"); s_lg = sem("s_lg"); s_rt = sem("s_rt"); s_sel = sem("s_sel")
        s_ch = sem("s_ch"); s_qk = sem("s_qk"); s_qkc = sem("s_qkc"); s_v = sem("s_v"); s_vc = sem("s_vc")
        s_sc = [sem(f"s_sc{i}") for i in range(2)]; s_mx = [sem(f"s_mx{i}") for i in range(2)]; s_sub = [sem(f"s_sub{i}") for i in range(2)]
        s_ex = [sem(f"s_ex{i}") for i in range(2)]; s_eT = [sem(f"s_eT{i}") for i in range(2)]
        s_eTa = [sem(f"s_eTa{i}") for i in range(2)]; s_eTv = [sem(f"s_eTv{i}") for i in range(2)]
        s_av = [sem(f"s_av{i}") for i in range(2)]
        s_rd = sem("s_rd"); s_o0 = sem("s_o0"); s_oT = sem("s_oT"); s_oTc = sem("s_oTc"); s_wo = sem("s_wo")
        s_q1 = sem("s_q1"); s_q1c = sem("s_q1c"); s_vo = sem("s_vo"); s_voc = sem("s_voc")
        s_zero = sem("s_zero"); s_msk = sem("s_msk"); s_den = sem("s_den"); s_rd1 = sem("s_rd1"); s_nrm = sem("s_nrm")
        s_xb = sem("s_xb"); s_y = sem("s_y2"); s_gm = sem("s_gm"); s_lt = sem("s_lt"); s_ltc = sem("s_ltc"); s_tab = sem("s_tab")
        s_one = sem("s2_one")
        block = ctx.enter_context(nc.Block())
        rows = lambda g, k: H[:, bass.ds(g * G + k, 1), :].squeeze(1)

        def wait_alone(eng, signal, value):
            value = eng.to_reg(value)
            eng.wait_ge(s_in, IN)
            eng.wait_ge(signal, value)

        def ln_stats(dve, g, i, src):
            for k in range(G):
                dve.bn_stats(stats[:, k, :], src(k)).then_inc(s_bn[i], 1)
            for k in range(G):
                wait_alone(dve, s_bn[i], g * G + k + 1)
                dve.bn_aggr(mv[:, k, :], stats[:, k, :]).then_inc(s_mv[i], 1)

        def ln_apply(dve, g, i, src, dst):
            dve.wait_ge(s_rstd, g * L + RANK[i] + 1)
            for k in range(G):
                dve.tensor_scalar(dst(k), src(k), mv[:, k, 0:1], rstd[:, k:k + 1], ALU.subtract, ALU.mult).then_inc(s_xh[i], 1)

        RANK = {0: 0, 1: 1, 2: 2, 4: 3, 3: 4}

        def ln_rstd(pool, g, i, eps):
            wait_alone(pool, s_mv[i], g * G + G)
            pool.tensor_scalar(ve[:, :], mv[:, :, 1], eps, None, ALU.add).then_inc(s_ve, 1)
            pool.wait_ge(s_ve, g * L + RANK[i] + 1)
            pool.tensor_tensor(rstd[:, :], ve[:, :], power[:, :], ALU.pow).then_inc(s_rstd, 1)

        IN = 16 * (15 + 3 * 2 + 2 * sum(HEADS // n for n in KV_HEADS))

        @block.sync
        def _(sp):
            sp.dma_start(wq0[:, :], A["L0_attn_W_Q"]).then_inc(s_in, 16)
            sp.dma_start(wk0[:, :], A["L0_attn_W_K"]).then_inc(s_in, 16)
            sp.dma_start(wv0[:, :], A["L0_attn_W_V"]).then_inc(s_in, 16)
            sp.dma_start(wv1[:, :, :], A["L1_attn_Wv"].rearrange("d (h n) -> d h n", h=HEADS)).then_inc(s_in, 16)
            sp.dma_start(wo1[:, :, :], A["L1_attn_Wo"].rearrange("(h p) n -> p h n", h=HEADS)).then_inc(s_in, 16)
            sp.dma_start(wq1[:, :], A["L1_attn_Wq"]).then_inc(s_in, 16)
            sp.dma_start(wk1[:, :], A["L1_attn_Wk"]).then_inc(s_in, 16)
            sp.dma_start(rw1[:, :], A["L0_ffn_r_w1"]).then_inc(s_in, 16)
            sp.dma_start(rb1[:, :], A["L0_ffn_r_b1"].unsqueeze(1)).then_inc(s_in, 16)
            sp.dma_start(rw2[:, :], A["L0_ffn_r_w2"]).then_inc(s_in, 16)
            sp.dma_start(rb2[:, :], A["L0_ffn_r_b2"].unsqueeze(0)).then_inc(s_in, 16)
            sp.dma_start(wr[:, :], A["L1_ffn_Wr"]).then_inc(s_in, 16)
            for t, name in ((bo, "L1_attn_bo"), (gamma, "L1_attn_gamma"), (beta, "L1_attn_beta")):
                sp.dma_start(t[:, :], A[name].unsqueeze(0).broadcast_to([P, D])).then_inc(s_in, 16)
            sp.wait_ge(s_var0, 1)
            with nc.allow_non_contiguous_dma("a head's columns, set apart"):
                for i, n in enumerate(KV_HEADS):
                    padded = lambda c: variants[:, i, c:c + HEADS * PADK].rearrange("p (h c) -> p h c", c=PADK)[:, :, 0:DK]
                    sp.dma_start(padded(WQ), A[f"L0_ffn_wq{i}"].rearrange("p (h c) -> p h c", c=DK)).then_inc(s_in, 16)
                    for r in range(HEADS // n):
                        for c, name in ((WK, "wk"), (WV, "wv")):
                            src = A[f"L0_ffn_{name}{i}"].rearrange("p (h c) -> p h c", c=DK)
                            dst = padded(WK) if c == WK else variants[:, i, WV:WV + D].rearrange("p (h c) -> p h c", c=DK)
                            sp.dma_start(dst[:, r::HEADS // n, :], src).then_inc(s_in, 16)
                    sp.dma_start(variants[:, i, WO:WALL], A[f"L0_ffn_wo{i}"]).then_inc(s_in, 16)
            sp.dma_start(w1[:, :, :], A["L1_ffn_W1"].rearrange("e d f -> d e f")).then_inc(s_weights, 16)
            for e in range(E):
                sp.dma_start(w2[:, e, :, :], A["L1_ffn_W2"][e].rearrange("(c p) d -> p c d", p=P)).then_inc(s_weights, 16)
            sp.wait_ge(s_in, IN)
            sp.sem_inc(s_tab, 16)
            with sp.Fori(0, NG) as g:
                wait_alone(sp, s_sel, g + 1)
                for k in range(G):
                    v = sp.value_load(sel[0:1, k:k + 1], min_val=0, max_val=2)
                    sp.dma_start(chosen[:, k, :], variants[:, bass.ds(v, 1), :].squeeze(1)).then_inc(s_ch, 16)
                sp.wait_ge(s_xh[3], g * G + G)
                sp.dma_start(table[bass.ds(g * G * S, G * S), 0:D].rearrange("(k s) d -> s k d", k=G), xh[:, :, :]).then_inc(s_tab, 16)
            sp.wait_ge(s_tab, 16 * NG + 16)

        @block.gpsimd
        def _(pool):
            pool.memset(variants[:, :, :], 0.0).then_inc(s_var0, 1)
            pool.iota(decay[:, :], pattern=[[1, P]], base=0, channel_multiplier=-1, allow_small_or_imprecise_dtypes=True).then_inc(s_iota, 1)
            pool.memset(power[:, :], -0.5).then_inc(s_pc, 1)
            pool.memset(v17[:, :, :, DK:DK + 1], 1.0).then_inc(s_one, 1)
            pool.wait_ge(s_in, IN)
            pool.wait_ge(s_pc, 1)
            with pool.Fori(0, NG) as g:
                ln_rstd(pool, g, 0, 1e-5)
                ln_rstd(pool, g, 1, 1e-5)
                ln_rstd(pool, g, 2, 1e-5)
                pool.wait_ge(s_xh[2], g * G + G)
                pool.tensor_tensor(y1[:, :, :], xh[:, :, :], bo[:, :].unsqueeze(1).broadcast_to([P, G, D]), ALU.add).then_inc(s_xb, 1)
                for k in range(G):
                    pool.wait_ge(s_rd1, g * G + k + 1)
                    pool.tensor_tensor(ex[:, k % 2, :, :], ex[:, k % 2, :, :],
                                       rden[:, k % 2, :].unsqueeze(2).broadcast_to([P, HEADS, S]), ALU.mult).then_inc(s_nrm, 1)
                ln_rstd(pool, g, 4, 1e-6)
                pool.wait_ge(s_xh[4], g * G + G)
                pool.tensor_tensor(y2[:, :, :], y2[:, :, :], gamma[:, :].unsqueeze(1).broadcast_to([P, G, D]), ALU.mult).then_inc(s_gm, 1)
                pool.wait_ge(s_gm, 2 * g + 1)
                pool.tensor_tensor(y2[:, :, :], y2[:, :, :], beta[:, :].unsqueeze(1).broadcast_to([P, G, D]), ALU.add).then_inc(s_gm, 1)
                ln_rstd(pool, g, 3, 1e-5)

        @block.tensor
        def _(pe):
            pe.wait_ge(s_in, IN)
            pe.transpose(psum[0][:, 0:P], wk0[:, :], ident[:, :])
            pe.transpose(psum[0][:, P:2 * P], wq0[:, :], ident[:, :]).then_inc(s_wt, 1)
            for n in range(2):
                for h in range(4):
                    mm = pe.transpose(psum[1 + n][:, h * P:(h + 1) * P], wv1[:, 4 * n + h, :], ident[:, :])
                mm.then_inc(s_wt, 1)
            pe.wait_ge(s_wtc, 4)
            pe.matmul(psum[3][:, 0:P], wkT[:, :], wqT[:, :], start=True, stop=True).then_inc(s_m0, 1)
            for n in range(2):
                for h in range(4):
                    mm = pe.matmul(psum[4 + n][:, h * P:(h + 1) * P], wvT[:, 4 * n + h, :], wo1[:, 4 * n + h, :], start=True, stop=True)
                mm.then_inc(s_m0, 1)
            pe.wait_ge(s_m0c, 3)

            def turn_x(g, i):
                pe.wait_ge(s_xh[i], g * G + G)
                for k in range(G):
                    mm = pe.transpose(psum[0][:, k * S:(k + 1) * S], xh[:, k, :], ident[:, :])
                mm.then_inc(s_xT[i], 1)
                pe.wait_ge(s_xTc[i], g + 1)

            def turn_ex(g, i, k):
                n = g * G + k
                pe.wait_ge(s_ex[0] if i == 0 else s_nrm, n + 1)
                if k:
                    pe.wait_ge(s_eTa[i], n)
                    pe.wait_ge(s_eTv[i], n)
                for h in range(HEADS):
                    mm = pe.transpose(psum[1 + h // 4][:, (h % 4) * S:(h % 4 + 1) * S], ex[:, k % 2, h, :], ident[:, :])
                mm.then_inc(s_eT[i], 1)

            with pe.Fori(0, NG) as g:
                turn_x(g, 0)
                pe.matmul(psum[1][:, :], wkq[:, :], xT[:, :, :], start=True, stop=True).then_inc(s_p, 1)
                for k in range(G):
                    mm = pe.matmul(psum[2][:, k * D:(k + 1) * D], xT[:, k, :], wv0[:, :], start=True, stop=True)
                mm.then_inc(s_v0, 1)
                pe.wait_ge(s_pT, g + 1)
                for k in range(G):
                    mm = pe.matmul(psum[3][:, k * S:(k + 1) * S], pT[:, k, :], xT[:, k, :], start=True, stop=True)
                mm.then_inc(s_s0, 1)
                pe.wait_ge(s_act0, g + 1)
                pe.wait_ge(s_v0c, g + 1)
                for k in range(G):
                    mm = pe.matmul(psum[1][:, k * D:(k + 1) * D], act0[:, k, :], v0[:, k, :], start=True, stop=True)
                mm.then_inc(s_o, 1)
                turn_x(g, 1)
                pe.wait_ge(s_ms, g + 1)
                pe.matmul(psum[2][0:32, 0:G], rw1[:, :], msum[:, :], start=True, stop=True).then_inc(s_r1, 1)
                wait_alone(pe, s_r1c, g + 1)
                for k in range(G):
                    mm = pe.matmul(psum[3][0:1, 3 * k:3 * k + 3], r1[:, k:k + 1], rw2[:, :], start=True, stop=True)
                mm.then_inc(s_lg, 1)
                pe.wait_ge(s_ch, (g + 1) * 16 * G)
                pe.wait_ge(s_rt, g * 5 + 1)

                for k in range(G):
                    mm = pe.matmul(psum[3][:, k * D:(k + 1) * D], xT[:, k, :], chosen[:, k, WV:WV + D], start=True, stop=True)
                mm.then_inc(s_v, 1)
                for k in range(G):
                    if k >= 2:
                        pe.wait_ge(s_qkc, g * G + k - 1)
                    for c in range(4):
                        mm = pe.matmul(psum[1 + k % 2][:, c * S:(c + 1) * S], chosen[:, k, c * P:(c + 1) * P], xT[:, k, :], start=True, stop=True)
                    mm.then_inc(s_qk, 1)

                def scores(k):
                    pe.wait_ge(s_qkc, g * G + k + 2)
                    if k:
                        pe.wait_ge(s_sub[0], g * G + k)
                    for h in range(HEADS):
                        for kk in range(2):
                            r = slice((h // 2) * PADK, (h // 2 + 1) * PADK)
                            c = (2 * kk + h % 2) * S
                            mm = pe.matmul(psum[4 + h // 2][:, c:c + S], qk[r, k + kk, h % 2, :], qk[r, k + kk, 2 + h % 2, :],
                                           start=True, stop=True)
                    mm.then_inc(s_sc[0], 1)

                def weigh(k):
                    n = g * G + k
                    pe.wait_ge(s_vc, g + 1)
                    pe.wait_ge(s_eTa[0], n + 1)
                    pe.wait_ge(s_eTv[0], n + 1)
                    if k:
                        pe.wait_ge(s_o0, n)
                    for n in range(HEADS):
                        h = n // 2 + 4 * (n % 2)
                        mm = pe.matmul(psum[3][:, h * (DK + 1):(h + 1) * (DK + 1)], exT[:, k % 2, n, :], v17[:, k, h, :], start=True, stop=True)
                    mm.then_inc(s_av[0], 1)

                pe.wait_ge(s_qkc, g * G + G)
                scores(0)
                turn_ex(g, 0, 0)
                weigh(0)
                scores(2)
                for k in range(1, G):
                    turn_ex(g, 0, k)
                    weigh(k)
                pe.wait_ge(s_o0, g * G + G)
                for k in range(G):
                    mm = pe.transpose(psum[0][:, k * S:(k + 1) * S], o0[:, k, :], ident[:, :])
                mm.then_inc(s_oT, 1)
                pe.wait_ge(s_oTc, g + 1)
                for k in range(G):
                    mm = pe.matmul(psum[1][:, k * D:(k + 1) * D], oT[:, k, :], chosen[:, k, WO:WALL], start=True, stop=True)
                mm.then_inc(s_wo, 1)
                turn_x(g, 2)
                for c in range(8):
                    if c >= 4:
                        pe.wait_ge(s_q1c, g * 8 + c - 3)
                    w = wq1 if c < 4 else wk1
                    pe.matmul(psum[c % 4][:, :], w[:, (c % 4) * P:(c % 4 + 1) * P], xT[:, :, :], start=True, stop=True).then_inc(s_q1, 1)
                pe.wait_ge(s_q1c, g * 8 + 8)

                def proj1(k, c):
                    n = g * 2 * G + 2 * k + c
                    if k or c:
                        pe.wait_ge(s_voc, n)
                    pe.matmul(psum[0][:, :], xT[:, k, :], wvo[:, 4 * c:4 * c + 4, :], start=True, stop=True).then_inc(s_vo, 1)

                def scores1(k):
                    if k >= 2:
                        pe.wait_ge(s_msk, 2 * (g * G + k - 1))
                    for h in range(HEADS):
                        r = slice((h % 2) * K1, (h % 2 + 1) * K1)
                        mm = pe.matmul(psum[4 + 2 * (k % 2) + h % 2][:, (h // 2) * S:(h // 2 + 1) * S], qT1[r, h // 2, k * S:(k + 1) * S],
                                       kT1[r, h // 2, k * S:(k + 1) * S], start=True, stop=True)
                    mm.then_inc(s_sc[1], 1)

                def weigh1(k):
                    n = g * G + k
                    pe.wait_ge(s_voc, 2 * n + 2)
                    pe.wait_ge(s_eTa[1], n + 1)
                    pe.wait_ge(s_eTv[1], n + 1)
                    for h in range(HEADS):
                        mm = pe.matmul(psum[3][:, k * D:(k + 1) * D], exT[:, k % 2, h, :], vo[:, k, h, :], start=(h == 0), stop=(h == HEADS - 1))
                    if k == G - 1:
                        mm.then_inc(s_av[1], 1)

                proj1(0, 0)
                scores1(0)
                proj1(0, 1)
                scores1(1)
                for k in range(1, G):
                    proj1(k, 0)
                    turn_ex(g, 1, k - 1)
                    weigh1(k - 1)
                    proj1(k, 1)
                    if k + 1 < G:
                        scores1(k + 1)
                turn_ex(g, 1, G - 1)
                weigh1(G - 1)
                turn_x(g, 3)
                pe.matmul(psum[1][0:E, :], wr[:, :], xT[:, :, :], start=True, stop=True).then_inc(s_lt, 1)
                pe.wait_ge(s_ltc, g + 2)

        @block.scalar
        def _(act):
            act.wait_ge(s_wt, 1)
            act.activation(wkT[:, :], psum[0][:, 0:P], ACT.Copy).then_inc(s_wtc, 1)
            act.activation(wqT[:, :], psum[0][:, P:2 * P], ACT.Copy).then_inc(s_wtc, 1)
            for n in range(2):
                act.wait_ge(s_wt, 2 + n)
                act.activation(wvT[:, 4 * n:4 * n + 4, :], psum[1 + n][:, :], ACT.Copy).then_inc(s_wtc, 1)
            act.wait_ge(s_m0, 1)
            act.activation(wkq[:, :], psum[3][:, 0:P], ACT.Copy).then_inc(s_m0c, 1)
            for n in range(2):
                act.wait_ge(s_m0, 2 + n)
                act.activation(wvo[:, 4 * n:4 * n + 4, :], psum[4 + n][:, :], ACT.Copy).then_inc(s_m0c, 1)
            act.wait_ge(s_abs, 1)
            act.activation(decay[:, :], decay[:, :], ACT.Exp, scale=math.log(DECAY)).then_inc(s_dec, 1)
            act.wait_ge(s_in, IN)

            def copy_x(g, i):
                act.wait_ge(s_xT[i], g + 1)
                act.activation(xT[:, :, :], psum[0][:, :], ACT.Copy).then_inc(s_xTc[i], 1)

            def exps(g, i, k, scale):
                n = g * G + k
                act.wait_ge(s_sub[i], n + 1)
                act.activation(ex[:, k % 2, :, :], ex[:, k % 2, :, :], ACT.Exp, scale=scale).then_inc(s_ex[i], 1)

            def copy_ex(g, i, k):
                n = g * G + k
                act.wait_ge(s_eT[i], n + 1)
                act.activation(exT[:, k % 2, 0:4, :], psum[1][:, :], ACT.Copy).then_inc(s_eTa[i], 1)

            act.sem_inc(s_ltc, 1)
            with act.Fori(0, NG) as g:
                copy_x(g, 0)
                act.wait_ge(s_p, g + 1)
                act.activation(pT[:, :, :], psum[1][:, :], ACT.Copy).then_inc(s_pT, 1)
                act.wait_ge(s_v0, g + 1)
                act.activation(v0[:, :, :], psum[2][:, :], ACT.Copy, scale=0.5).then_inc(s_v0c, 1)
                act.wait_ge(s_sd, g + 1)
                act.activation(th[:, :, :], sd[:, :, :], ACT.Tanh, scale=0.5).then_inc(s_th, 1)
                copy_x(g, 1)
                act.wait_ge(s_r1, g + 1)
                act.activation(r1[:, :], psum[2][0:32, 0:G], ACT.Relu, bias=rb1[:, :], scale=1.0 / S).then_inc(s_r1c, 1)

                for k in range(G):
                    act.wait_ge(s_qk, g * G + k + 1)
                    act.activation(qk[:, k, :, :], psum[1 + k % 2][:, :], ACT.Copy).then_inc(s_qkc, 1)
                for k in range(G):
                    exps(g, 0, k, 1.0 / math.sqrt(DK))
                    if k:
                        copy_ex(g, 0, k - 1)
                copy_ex(g, 0, G - 1)
                act.wait_ge(s_oT, g + 1)
                act.activation(oT[:, :, :], psum[0][:, :], ACT.Copy).then_inc(s_oTc, 1)
                copy_x(g, 2)
                for c in range(8):
                    act.wait_ge(s_q1, g * 8 + c + 1)
                    act.activation((qT1 if c < 4 else kT1)[:, c % 4, :], psum[c % 4][:, :], ACT.Copy).then_inc(s_q1c, 1)
                def copy_vo(k, c):
                    n = g * 2 * G + 2 * k + c
                    act.wait_ge(s_vo, n + 1)
                    act.activation(vo[:, k, 4 * c:4 * c + 4, :], psum[0][:, :], ACT.Copy).then_inc(s_voc, 1)

                copy_vo(0, 0)
                copy_vo(0, 1)
                exps(g, 1, 0, 1.0 / math.sqrt(K1))
                for k in range(1, G):
                    copy_vo(k, 0)
                    exps(g, 1, k, 1.0 / math.sqrt(K1))
                    copy_ex(g, 1, k - 1)
                    copy_vo(k, 1)
                copy_ex(g, 1, G - 1)
                copy_x(g, 3)
                act.wait_ge(s_lt, g + 1)
                act.activation(logitsT[:, bass.ds(g * G * S, G * S)], psum[1][0:E, :], ACT.Copy).then_inc(s_ltc, 1)

        @block.vector
        def _(dve):
            dve.wait_ge(s_iota, 1)
            dve.scalar_tensor_tensor(decay[:, :], decay[:, :], -1.0, decay[:, :], ALU.mult, ALU.max).then_inc(s_abs, 1)
            dve.wait_ge(s_in, IN)
            dve.wait_ge(s_dec, 1)
            dve.wait_ge(s_one, 1)
            with dve.Fori(0, NG) as g:
                row = lambda k: rows(g, k)
                hgroup = H[:, bass.ds(g * G, G), :]
                xk = lambda k: xh[:, k, :]

                def copy_ex(i, k):
                    n = g * G + k
                    dve.wait_ge(s_eT[i], n + 1)
                    dve.tensor_copy(exT[:, k % 2, 4:8, :].rearrange("p h s -> p (h s)"), psum[2][:, :]).then_inc(s_eTv[i], 1)

                ln_stats(dve, g, 0, row)
                dve.wait_ge(s_ltc, g + 1)
                dve.wait_ge(s_tab, 16 * g + 16)
                ln_apply(dve, g, 0, row, xk)
                dve.wait_ge(s_s0, g + 1)
                dve.tensor_tensor(sd[:, :, :], psum[3][:, :].rearrange("p (k s) -> p k s", k=G),
                                  decay[:, :].unsqueeze(1).broadcast_to([P, G, S]), ALU.mult).then_inc(s_sd, 1)
                dve.wait_ge(s_th, g + 1)
                dve.scalar_tensor_tensor(act0[:, :, :], th[:, :, :], 1.0, sd[:, :, :], ALU.add, ALU.mult).then_inc(s_act0, 1)
                dve.wait_ge(s_o, g + 1)
                dve.tensor_tensor(hgroup, hgroup, psum[1][:, :].rearrange("p (k s) -> p k s", k=G), ALU.add).then_inc(s_h[0], 1)
                wait_alone(dve, s_h[0], g + 1)
                ln_stats(dve, g, 1, row)
                ln_apply(dve, g, 1, row, xk)
                dve.wait_ge(s_xTc[1], g + 1)
                dve.tensor_reduce(msum[:, :], xT[:, :, :], AX.X, ALU.add).then_inc(s_ms, 1)
                dve.wait_ge(s_lg, g + 1)
                dve.tensor_tensor(lg[:, :, :], psum[3][0:1, 0:3 * G].rearrange("p (k c) -> p k c", k=G),
                                  rb2[:, :].unsqueeze(1).broadcast_to([1, G, 3]), ALU.add).then_inc(s_rt, 1)
                dve.wait_ge(s_rt, g * 5 + 1)
                dve.tensor_tensor(c1[:, :], lg[:, :, 1], lg[:, :, 0], ALU.is_gt).then_inc(s_rt, 1)
                dve.tensor_tensor(mx1[:, :], lg[:, :, 1], lg[:, :, 0], ALU.max).then_inc(s_rt, 1)
                dve.wait_ge(s_rt, g * 5 + 3)
                dve.tensor_tensor(c2[:, :], lg[:, :, 2], mx1[:, :], ALU.is_gt).then_inc(s_rt, 2)
                dve.wait_ge(s_rt, g * 5 + 5)
                dve.scalar_tensor_tensor(sel[:, :], c2[:, :], 2.0, c1[:, :], ALU.mult, ALU.max).then_inc(s_sel, 1)

                dve.wait_ge(s_v, g + 1)
                dve.tensor_copy(v17[:, :, :, 0:DK], psum[3][:, :].rearrange("p (k h c) -> p k h c", k=G, h=HEADS)).then_inc(s_vc, 1)

                def normalise(k):
                    n = g * G + k
                    av = psum[3][:, 0:HEADS * (DK + 1)].rearrange("p (h c) -> p h c", h=HEADS)
                    dve.wait_ge(s_av[0], n + 1)
                    dve.reciprocal(rden[:, k % 2, :], av[:, :, DK]).then_inc(s_rd, 1)
                    dve.wait_ge(s_rd, n + 1)
                    dve.tensor_tensor(o0[:, k, :].rearrange("p (h c) -> p h c", h=HEADS), av[:, :, 0:DK],
                                      rden[:, k % 2, :].unsqueeze(2).broadcast_to([P, HEADS, DK]), ALU.mult).then_inc(s_o0, 1)

                for k in range(G):
                    n = g * G + k
                    if k % 2 == 0:
                        dve.wait_ge(s_sc[0], g * 2 + k // 2 + 1)
                    part = psall[:, 4:8, (k % 2) * 2 * S:(k % 2 + 1) * 2 * S].rearrange("p r (c s) -> p r c s", c=2)
                    dve.tensor_reduce(smax[:, k % 2, :].rearrange("p (r c) -> p r c", c=2), part, AX.X, ALU.max).then_inc(s_mx[0], 1)
                    dve.wait_ge(s_mx[0], n + 1)
                    if k >= 2:
                        dve.wait_ge(s_eT[0], n - 1)
                    dve.tensor_tensor(ex[:, k % 2, :, :].rearrange("p (r c) s -> p r c s", c=2), part,
                                      smax[:, k % 2, :].rearrange("p (r c) -> p r c", c=2).unsqueeze(3).broadcast_to([P, 4, 2, S]),
                                      ALU.subtract).then_inc(s_sub[0], 1)
                    if k:
                        copy_ex(0, k - 1)
                        normalise(k - 1)
                copy_ex(0, G - 1)
                normalise(G - 1)
                dve.wait_ge(s_wo, g + 1)
                dve.tensor_tensor(hgroup, hgroup, psum[1][:, :].rearrange("p (k s) -> p k s", k=G), ALU.add).then_inc(s_h[1], 1)
                wait_alone(dve, s_h[1], g + 1)
                ln_stats(dve, g, 2, row)
                ln_apply(dve, g, 2, row, xk)
                for k in range(G):
                    n = g * G + k
                    dve.wait_ge(s_sc[1], n + 1)
                    for c in range(2):
                        dve.tensor_scalar(s2_[:, 4 * c:4 * c + 4, :].rearrange("p h s -> p (h s)"), psum[4 + 2 * (k % 2) + c][:, :], 0.0,
                                          -1e9 * math.sqrt(K1), ALU.is_equal, ALU.mult).then_inc(s_zero, 1)
                    for c in range(2):
                        dve.wait_ge(s_zero, 2 * n + 1 + c)
                        part = s2_[:, 4 * c:4 * c + 4, :].rearrange("p h s -> p (h s)")
                        dve.tensor_tensor(part, psum[4 + 2 * (k % 2) + c][:, :], part, ALU.add).then_inc(s_msk, 1)
                    dve.wait_ge(s_msk, 2 * n + 2)
                    dve.tensor_reduce(smax[:, k % 2, :], s2_[:, :, :], AX.X, ALU.max).then_inc(s_mx[1], 1)
                    dve.wait_ge(s_mx[1], n + 1)
                    dve.tensor_tensor(ex[:, k % 2, :, :].rearrange("p (q c) s -> p c q s", c=2), s2_[:, :, :].rearrange("p (c q) s -> p c q s", c=2),
                                      smax[:, k % 2, :].rearrange("p (c q) -> p c q", c=2).unsqueeze(3).broadcast_to([P, 2, 4, S]),
                                      ALU.subtract).then_inc(s_sub[1], 1)
                    if k:
                        copy_ex(1, k - 1)
                    dve.wait_ge(s_ex[1], n + 1)
                    dve.tensor_reduce(den[:, k % 2, :], ex[:, k % 2, :, :], AX.X, ALU.add).then_inc(s_den, 1)
                    dve.wait_ge(s_den, n + 1)
                    dve.reciprocal(rden[:, k % 2, :], den[:, k % 2, :]).then_inc(s_rd1, 1)
                copy_ex(1, G - 1)
                dve.wait_ge(s_av[1], g + 1)
                dve.wait_ge(s_xb, g + 1)
                dve.tensor_tensor(y1[:, :, :], y1[:, :, :], psum[3][:, :].rearrange("p (k s) -> p k s", k=G), ALU.add).then_inc(s_y, 1)
                dve.wait_ge(s_y, g + 1)
                ln_stats(dve, g, 4, lambda k: y1[:, k, :])
                ln_apply(dve, g, 4, lambda k: y1[:, k, :], lambda k: y2[:, k, :])
                dve.wait_ge(s_gm, 2 * g + 2)
                dve.tensor_tensor(hgroup, hgroup, y2[:, :, :], ALU.add).then_inc(s_h[2], 1)
                wait_alone(dve, s_h[2], g + 1)
                ln_stats(dve, g, 3, row)
                ln_apply(dve, g, 3, row, xk)


U32 = mybir.dt.uint32
N = B * S
CAP = 1024
F = 512
FC = F // P
CHUNKS = P // E
CW = N // CHUNKS
TILES = CAP // P
HB = 4


def experts_stage(nc, used, A, H, ident, psall, table, logitsT, w1, w2, s_weights, WEIGHTS, out):
    psum = [psall[:, i, :] for i in range(8)]
    logits_dram = nc.dram_tensor("logits_dram", (E, N), F32, kind="Internal").ap()
    out_rows = out.rearrange("b s d -> (b s) d")
    with ExitStack() as ctx:
        sb = lambda name, shape, dt=F32: ctx.enter_context(nc.sbuf_tensor(name, shape, dt))
        sem = lambda name: used.append(nc.alloc_semaphore(name)) or used[-1]
        b1rows = sb("b1rows", [E * FC, P]); b1 = sb("b1", [P, E, FC]); b2 = sb("b2", [P, E, D])
        prob = sb("prob", [P, CW]); rowmax = sb("rowmax", [P, 1]); m8 = sb("m8", [1, E]); mrow = sb("mrow", [1, P])
        one1 = sb("one1", [1, 1]); negmax = sb("negmax", [P, 1]); rowsum = sb("rowsum", [P, 1]); rsum = sb("rsum", [P, 1])
        same = sb("same", [P, E, CHUNKS]); before = sb("before", [P, E, CHUNKS])
        thr = sb("thr", [P, 1]); cand = sb("cand", [P, 1]); bit = sb("bit", [P, 1], I32); take = sb("take", [P, 1])
        count = sb("count", [P, 2]); hits = sb("hits", [P, CW])
        above = sb("above", [P, CW]); equal = sb("equal", [P, CW]); rank = sb("rank", [P, CW]); ones = sb("ones", [P, CW])
        need = sb("need", [P, 1]); offs = sb("offs", [P, 1]); picked = sb("picked", [P, CW]); slot = sb("slot", [P, CW])
        sloti = sb("sloti", [P, CW], I32); hii = sb("hii", [P, CW], I32); loi = sb("loi", [P, CW], I32)
        hl = sb("hl", [P, 2, CW])
        turned = sb("turned", [P, 3, 2, E, CHUNKS])
        iota_p = sb("iota_p", [P, P]); iota_t = sb("iota_t", [P, TILES]); tokid = sb("tokid", [P, 2, CHUNKS])
        hot_t = sb("hot_t", [P, 2, E, CHUNKS, TILES]); rhs = sb("rhs", [P, E, 2, CHUNKS, 2, TILES])
        hot_p = sb("hot_p", [P, 2, CHUNKS, P])
        idx = sb("idx", [P, E, TILES], U32); vals = sb("vals", [P, E, TILES])
        xg = sb("xg", [P, 2, TILES, D]); xgT = sb("xgT", [P, 2, HB * P]); hT = sb("hT", [P, 2, FC, HB * P])
        y = sb("y", [P, 2, TILES, D])

        s_lo = sem("s3_lo"); s_pr = sem("s3_pr"); s_b = sem("s3_b"); s_c = sem("s3_c"); s_cc = sem("s3_cc")
        s_rm = sem("s3_rm"); s_rmT = sem("s3_rmT"); s_m8 = sem("s3_m8"); s_mr = sem("s3_mr"); s_nm = sem("s3_nm"); s_nmc = sem("s3_nmc")
        s_e = sem("s3_e"); s_sum = sem("s3_sum"); s_rs = sem("s3_rs"); s_p = sem("s3_p")
        s_thr = sem("s3_thr"); s_cand = sem("s3_cand"); s_cnt = sem("s3_cnt"); s_tot = sem("s3_tot"); s_take = sem("s3_take"); s_bit = sem("s3_bit")
        s_sel = sem("s3_sel"); s_g = sem("s3_g"); s_off = sem("s3_off"); s_hl = sem("s3_hl"); s_tn = sem("s3_tn"); s_tnc = sem("s3_tnc")
        s_ht = sem("s3_ht"); s_rhs = sem("s3_rhs"); s_hp = sem("s3_hp"); s_ix = sem("s3_ix"); s_ixc = sem("s3_ixc"); s_b1 = sem("s3_b1"); s_b1c = sem("s3_b1c")
        s_out0 = sem("s3_out0"); s_ga = [sem(f"s3_ga{i}") for i in range(2)]; s_sc = sem("s3_sc")
        s_xt = sem("s3_xt"); s_xtc = sem("s3_xtc"); s_h1 = sem("s3_h1"); s_h1c = sem("s3_h1c"); s_y = sem("s3_y"); s_yb = sem("s3_yb"); s_yc = sem("s3_yc")
        block = ctx.enter_context(nc.Block())
        BITS = 30
        flat = lambda t: t.rearrange("p a b -> p (a b)")

        @block.sync
        def _(sp):
            sp.dma_start(logits_dram, logitsT[:, :]).then_inc(s_lo, 16)
            sp.dma_start(b1rows[:, :], A["L1_ffn_b1"].rearrange("e (c f) -> (e c) f", f=P)).then_inc(s_b, 16)
            sp.dma_start(b2[:, :, :], A["L1_ffn_b2"].unsqueeze(0).broadcast_to([P, E, D])).then_inc(s_b, 16)
            sp.dma_start(out.rearrange("b s d -> s b d"), H[:, :, :]).then_inc(s_out0, 16)
            sp.wait_ge(s_lo, 16)
            sp.dma_start(prob[:, :], logits_dram.rearrange("e (c f) -> (e c) f", f=CW)).then_inc(s_pr, 16)

        @block.gpsimd
        def _(pool):
            pool.memset(ones[:, :], 1.0).then_inc(s_c, 1)
            pool.memset(flat(same[:, :, :]), 1.0).then_inc(s_cc, 1)
            pool.memset(thr[:, :], 0.0).then_inc(s_c, 1)
            pool.memset(bit[:, :], 1 << (BITS - 1)).then_inc(s_c, 1)
            pool.memset(one1[:, :], 1.0).then_inc(s_c, 1)
            pool.iota(iota_p[:, :], pattern=[[1, P]], base=0, channel_multiplier=0, allow_small_or_imprecise_dtypes=True).then_inc(s_c, 1)
            pool.iota(iota_t[:, :], pattern=[[1, TILES]], base=0, channel_multiplier=0, allow_small_or_imprecise_dtypes=True).then_inc(s_c, 1)
            pool.iota(tokid[:, :, :], pattern=[[P, 2], [CW, CHUNKS]], base=0, channel_multiplier=1, allow_small_or_imprecise_dtypes=True).then_inc(s_c, 1)
            pool.wait_ge(s_cc, 1)
            pool.affine_select(out=same[:, :, :], in_=same[:, :, :], compare_op=ALU.is_ge, fill=0.0, base=0,
                               pattern=[[-CHUNKS, E], [0, CHUNKS]], channel_multiplier=1).then_inc(s_cc, 1)
            pool.wait_ge(s_cc, 2)
            pool.affine_select(out=same[:, :, :], in_=same[:, :, :], compare_op=ALU.is_ge, fill=0.0, base=CHUNKS - 1,
                               pattern=[[CHUNKS, E], [0, CHUNKS]], channel_multiplier=-1).then_inc(s_cc, 1)
            pool.wait_ge(s_cc, 3)
            pool.affine_select(out=flat(before[:, :, :]), in_=flat(same[:, :, :]), compare_op=ALU.is_gt, fill=0.0, base=0,
                               pattern=[[1, P]], channel_multiplier=-1).then_inc(s_cc, 1)

            def gather(e):
                pool.wait_ge(s_ixc, 2 * e + 2)
                if e >= 2:
                    pool.wait_ge(s_xt, 2 * (e - 1))
                for j in range(TILES):
                    pool.indirect_dma_start(out=xg[:, e % 2, j, :], out_offset=None, in_=table,
                                            in_offset=bass.IndirectOffsetOnAxis(ap=idx[:, e, j:j + 1], axis=0)).then_inc(s_ga[e % 2], 16)

            def scatter(e):
                pool.wait_ge(s_out0, 16)
                if e:
                    pool.wait_ge(s_sc, 16 * TILES * e)
                for j in range(TILES):
                    if j % HB == 0:
                        pool.wait_ge(s_yc, 2 * e + j // HB + 1)
                    pool.indirect_dma_start(out=out_rows, out_offset=bass.IndirectOffsetOnAxis(ap=idx[:, e, j:j + 1], axis=0),
                                            in_=y[:, e % 2, j, :], in_offset=None, compute_op=ALU.add).then_inc(s_sc, 16)

            gather(0)
            for e in range(E):
                if e + 1 < E:
                    gather(e + 1)
                scatter(e)
            pool.wait_ge(s_sc, 16 * TILES * E)

        @block.tensor
        def _(pe):
            pe.wait_ge(s_b, 32)
            pe.transpose(psum[0][:, 0:E * FC], b1rows[:, :], ident[0:E * FC, 0:E * FC]).then_inc(s_b1, 1)
            pe.wait_ge(s_rm, 1)
            pe.transpose(psum[1][0:1, 0:P], rowmax[:, :], ident[:, :]).then_inc(s_rmT, 1)
            pe.wait_ge(s_mr, 1)
            pe.matmul(psum[2][:, 0:1], mrow[:, :], one1[:, :], start=True, stop=True).then_inc(s_nm, 1)
            pe.wait_ge(s_cc, 4)
            pe.wait_ge(s_e, 1)
            pe.matmul(psum[3][:, 0:1], flat(same[:, :, :]), rowsum[:, :], start=True, stop=True).then_inc(s_sum, 1)
            with pe.Fori(0, BITS) as i:
                pe.wait_ge(s_cnt, i + 1)
                pe.matmul(psum[4][:, 0:1], flat(same[:, :, :]), count[:, 0:1], start=True, stop=True).then_inc(s_tot, 1)
            pe.wait_ge(s_g, 2)
            pe.matmul(psum[5][:, 0:1], flat(same[:, :, :]), count[:, 0:1], start=True, stop=True)
            pe.matmul(psum[5][:, 1:2], flat(before[:, :, :]), count[:, 1:2], start=True, stop=True).then_inc(s_off, 1)
            pe.wait_ge(s_g, 3)
            pe.matmul(psum[6][:, 0:1], flat(before[:, :, :]), count[:, 0:1], start=True, stop=True).then_inc(s_off, 1)
            pe.wait_ge(s_hl, 2)
            for q, t in enumerate((hl[:, 0, :], hl[:, 1, :], prob[:, :])):
                for half in range(2):
                    mm = pe.transpose(psum[q][:, half * P:(half + 1) * P], t[:, half * P:(half + 1) * P], ident[:, :])
                mm.then_inc(s_tn, 1)

            def slots(e):
                for half in range(2):
                    pe.wait_ge(s_hp, 2 * e + half + 1)
                    for c in range(CHUNKS):
                        mm = pe.matmul(psum[7][:, 0:2 * TILES], hot_p[:, half, c, :], rhs[:, e, half, c, :, :],
                                       start=(half == 0 and c == 0), stop=(half == 1 and c == CHUNKS - 1))
                    mm.then_inc(s_ix, 1)

            def expert(e):
                for u in range(2):
                    n = 2 * e + u
                    pe.wait_ge(s_ga[e % 2], 16 * TILES * (e // 2 + 1))
                    if n >= 2:
                        pe.wait_ge(s_xtc, n - 1)
                    for j in range(HB):
                        mm = pe.transpose(psum[u][:, j * P:(j + 1) * P], xg[:, e % 2, u * HB + j, :], ident[:, :])
                    mm.then_inc(s_xt, 1)
                for u in range(2):
                    n = 2 * e + u
                    pe.wait_ge(s_xtc, n + 1)
                    for c in range(FC):
                        m = n * FC + c
                        if m >= 4:
                            pe.wait_ge(s_h1c, m - 3)
                        pe.matmul(psum[2 + c][:, :], w1[:, e, c * P:(c + 1) * P], xgT[:, u, :], start=True, stop=True).then_inc(s_h1, 1)
                for u in range(2):
                    n = 2 * e + u
                    pe.wait_ge(s_h1c, FC * (n + 1))
                    if n:
                        pe.wait_ge(s_yb, n)
                    for j in range(HB):
                        for c in range(FC):
                            mm = pe.matmul(psum[6][:, j * D:(j + 1) * D], hT[:, u, c, j * P:(j + 1) * P], w2[:, e, c, :],
                                           start=(c == 0), stop=(c == FC - 1))
                    mm.then_inc(s_y, 1)

            pe.wait_ge(s_rhs, 2)
            pe.wait_ge(s_weights, WEIGHTS)
            pe.wait_ge(s_tnc, 3)
            slots(0)
            for e in range(E):
                if e + 1 < E:
                    pe.wait_ge(s_ixc, 2 * e + 2)
                    slots(e + 1)
                expert(e)

        @block.scalar
        def _(act):
            act.wait_ge(s_b1, 1)
            act.activation(b1[:, :, :].rearrange("p e c -> p (e c)"), psum[0][:, 0:E * FC], ACT.Copy).then_inc(s_b1c, 1)
            act.wait_ge(s_nm, 1)
            act.activation(negmax[:, :], psum[2][:, 0:1], ACT.Copy, scale=-1.0).then_inc(s_nmc, 1)
            act.wait_ge(s_nmc, 1)
            act.wait_ge(s_pr, 16)
            act.activation(prob[:, :], prob[:, :], ACT.Exp, bias=negmax[:, :], accum_out=rowsum[:, :]).then_inc(s_e, 1)
            act.wait_ge(s_b1c, 1)
            for e in range(E):
                for u in range(2):
                    n = 2 * e + u
                    act.wait_ge(s_xt, n + 1)
                    act.activation(xgT[:, u, :], psum[u][:, :], ACT.Copy).then_inc(s_xtc, 1)
                for u in range(2):
                    n = 2 * e + u
                    if n >= 2:
                        act.wait_ge(s_y, n - 1)
                    for c in range(FC):
                        act.wait_ge(s_h1, n * FC + c + 1)
                        act.activation(hT[:, u, c, :], psum[2 + c][:, :], ACT.Gelu, bias=b1[:, e, c:c + 1]).then_inc(s_h1c, 1)

        @block.vector
        def _(dve):
            dve.wait_ge(s_pr, 16)
            dve.wait_ge(s_c, 7)
            dve.tensor_reduce(rowmax[:, :], prob[:, :], AX.X, ALU.max).then_inc(s_rm, 1)
            dve.wait_ge(s_rmT, 1)
            dve.tensor_reduce(m8[:, :], psum[1][0:1, 0:P].rearrange("p (e c) -> p e c", e=E), AX.X, ALU.max).then_inc(s_m8, 1)
            dve.wait_ge(s_m8, 1)
            dve.tensor_copy(mrow[:, :].rearrange("p (e c) -> p e c", e=E), m8[:, :].unsqueeze(2).broadcast_to([1, E, CHUNKS])).then_inc(s_mr, 1)
            dve.wait_ge(s_sum, 1)
            dve.reciprocal(rsum[:, :], psum[3][:, 0:1]).then_inc(s_rs, 1)
            dve.wait_ge(s_rs, 1)
            dve.tensor_scalar(prob[:, :], prob[:, :], rsum[:, :], None, ALU.mult).then_inc(s_p, 1)
            dve.wait_ge(s_p, 1)
            with dve.Fori(0, BITS) as i:
                dve.wait_ge(s_thr, i + 1) if False else None
                dve.tensor_tensor(cand[:, :].bitcast(I32), thr[:, :].bitcast(I32), bit[:, :], ALU.bitwise_or).then_inc(s_cand, 1)
                dve.wait_ge(s_cand, i + 1)
                dve.tensor_scalar(hits[:, :], prob[:, :], cand[:, :], 0.0, ALU.is_ge, ALU.add, accum_out=count[:, 0:1]).then_inc(s_cnt, 1)
                dve.tensor_scalar(bit[:, :], bit[:, :], 1, None, ALU.logical_shift_right).then_inc(s_bit, 1)
                dve.wait_ge(s_tot, i + 1)
                dve.scalar_tensor_tensor(take[:, :], psum[4][:, 0:1], CAP - 0.5, cand[:, :], ALU.is_ge, ALU.mult).then_inc(s_take, 1)
                dve.wait_ge(s_take, i + 1)
                dve.wait_ge(s_bit, i + 1)
                dve.tensor_tensor(thr[:, :], thr[:, :], take[:, :], ALU.max).then_inc(s_thr, 1)
                dve.wait_ge(s_thr, i + 1)
            dve.tensor_scalar(above[:, :], prob[:, :], thr[:, :], 0.0, ALU.is_gt, ALU.add, accum_out=count[:, 0:1]).then_inc(s_g, 1)
            dve.tensor_scalar(equal[:, :], prob[:, :], thr[:, :], 0.0, ALU.is_equal, ALU.add, accum_out=count[:, 1:2]).then_inc(s_g, 1)
            dve.wait_ge(s_g, 2)
            dve.tensor_tensor_scan(rank[:, :], ones[:, :], equal[:, :], 0.0, ALU.mult, ALU.add).then_inc(s_sel, 1)
            dve.wait_ge(s_off, 1)
            dve.tensor_scalar(offs[:, :], psum[5][:, 0:1], -1.0, float(CAP), ALU.mult, ALU.add).then_inc(s_sel, 1)
            dve.wait_ge(s_sel, 2)
            dve.tensor_tensor(need[:, :], offs[:, :], psum[5][:, 1:2], ALU.subtract).then_inc(s_sel, 1)
            dve.wait_ge(s_sel, 3)
            dve.scalar_tensor_tensor(picked[:, :], rank[:, :], need[:, :], equal[:, :], ALU.is_le, ALU.mult).then_inc(s_sel, 1)
            dve.wait_ge(s_sel, 4)
            dve.tensor_tensor(picked[:, :], picked[:, :], above[:, :], ALU.add).then_inc(s_sel, 1)
            dve.wait_ge(s_sel, 5)
            dve.tensor_tensor_scan(rank[:, :], ones[:, :], picked[:, :], 0.0, ALU.mult, ALU.add).then_inc(s_sel, 1)
            dve.wait_ge(s_sel, 6)
            dve.tensor_copy(count[:, 0:1], rank[:, CW - 1:CW]).then_inc(s_g, 1)
            dve.wait_ge(s_off, 2)
            dve.scalar_tensor_tensor(slot[:, :], rank[:, :], psum[6][:, 0:1], picked[:, :], ALU.add, ALU.mult).then_inc(s_sel, 1)
            dve.wait_ge(s_sel, 7)
            dve.tensor_scalar(sloti[:, :], slot[:, :], -1.0, None, ALU.add).then_inc(s_sel, 1)
            dve.wait_ge(s_sel, 8)
            dve.tensor_scalar(hii[:, :], sloti[:, :], 3, None, ALU.arith_shift_right).then_inc(s_sel, 1)
            dve.tensor_scalar(loi[:, :], sloti[:, :], TILES - 1, None, ALU.bitwise_and).then_inc(s_sel, 1)
            dve.wait_ge(s_sel, 10)
            dve.tensor_copy(hl[:, 0, :], hii[:, :]).then_inc(s_hl, 1)
            dve.tensor_copy(hl[:, 1, :], loi[:, :]).then_inc(s_hl, 1)
            for q in range(3):
                dve.wait_ge(s_tn, q + 1)
                dve.tensor_copy(turned[:, q, :, :, :].rearrange("p h e c -> p (h e c)"), psum[q][:, 0:2 * P]).then_inc(s_tnc, 1)
            dve.wait_ge(s_tnc, 3)
            dve.tensor_tensor(hot_t[:, :, :, :, :].rearrange("p h e c t -> p (h e c) t"),
                              turned[:, 1, :, :, :].rearrange("p h e c -> p (h e c)").unsqueeze(2).broadcast_to([P, 2 * P, TILES]),
                              iota_t[:, :].unsqueeze(1).broadcast_to([P, 2 * P, TILES]), ALU.is_equal).then_inc(s_ht, 1)
            dve.wait_ge(s_ht, 1)
            for half in range(2):
                hot = hot_t[:, half, :, :, :]
                dve.tensor_tensor(rhs[:, :, half, :, 0, :], hot, tokid[:, half, :].unsqueeze(1).unsqueeze(3).broadcast_to([P, E, CHUNKS, TILES]),
                                  ALU.mult)
                ins = dve.tensor_tensor(rhs[:, :, half, :, 1, :], hot, turned[:, 2, half, :, :].unsqueeze(3).broadcast_to([P, E, CHUNKS, TILES]),
                                        ALU.mult)
                ins.then_inc(s_rhs, 1)

            def hots(e):
                for half in range(2):
                    if e:
                        dve.wait_ge(s_ix, 2 * e - 1 + half)
                    dve.tensor_tensor(hot_p[:, half, :, :], turned[:, 0, half, e, :].unsqueeze(2).broadcast_to([P, CHUNKS, P]),
                                      iota_p[:, :].unsqueeze(1).broadcast_to([P, CHUNKS, P]), ALU.is_equal).then_inc(s_hp, 1)
                dve.wait_ge(s_ix, 2 * e + 2)
                dve.tensor_copy(idx[:, e, :], psum[7][:, 0:TILES]).then_inc(s_ixc, 1)
                dve.tensor_copy(vals[:, e, :], psum[7][:, TILES:2 * TILES]).then_inc(s_ixc, 1)

            hots(0)
            hots(1)
            for e in range(E):
                for u in range(2):
                    n = 2 * e + u
                    dve.wait_ge(s_y, n + 1)
                    if e >= 2:
                        dve.wait_ge(s_sc, 16 * TILES * (e - 1))
                    part = y[:, e % 2, u * HB:(u + 1) * HB, :]
                    dve.tensor_tensor(part, psum[6][:, :].rearrange("p (j d) -> p j d", j=HB), b2[:, e:e + 1, :].broadcast_to([P, HB, D]),
                                      ALU.add).then_inc(s_yb, 1)
                    dve.wait_ge(s_yb, n + 1)
                    dve.tensor_tensor(part, part, vals[:, e, u * HB:(u + 1) * HB].unsqueeze(2).broadcast_to([P, HB, D]), ALU.mult).then_inc(s_yc, 1)
                if e + 2 < E:
                    hots(e + 2)


def tower_kernel(nc, A, out):
    table = nc.dram_tensor("token_table", (N, D), F32, kind="Internal").ap()
    with ExitStack() as ctx:
        sb = lambda name, shape, dt=F32: ctx.enter_context(nc.sbuf_tensor(name, shape, dt))
        psall = ctx.enter_context(nc.psum_tensor("banks", [P, 8, 512], F32))
        H = sb("H", [P, B, D])
        ident = sb("ident", [P, P])

        def fresh():
            nc.clear_and_free_semaphores(used)
            nc.all_engine_barrier()
            used.clear()

        used = []
        alignment_stage(nc, used, A, H, ident, [psall[:, i, :] for i in range(8)])
        fresh()
        logitsT = sb("logitsT", [E, N])
        w1 = sb("w1", [P, E, F])
        w2 = sb("w2", [P, E, FC, D])
        s_weights = ctx.enter_context(nc.semaphore("s_weights"))
        layers_stage(nc, used, A, H, ident, psall, table, logitsT, w1, w2, s_weights)
        fresh()
        experts_stage(nc, used, A, H, ident, psall, table, logitsT, w1, w2, s_weights, 16 * (1 + E), out)


_OUT = (B, S, D)


def kernel(**inputs):
    import numpy as _np
    import concourse.bacc as _bacc
    from concourse import mybir as _mybir
    from concourse.bass_utils import run_bass_kernel_spmd as _run

    nc = _bacc.Bacc("TRN2", target_bir_lowering=False, num_devices=1)
    arrays, A = {}, {}
    for name, value in inputs.items():
        a = _np.ascontiguousarray(value)
        arrays[f"in_{name}"] = a
        A[name] = nc.dram_tensor(f"in_{name}", a.shape, _mybir.dt.from_np(a.dtype), kind="ExternalInput").ap()
    out = nc.dram_tensor("out_h", _OUT, F32, kind="ExternalOutput").ap()
    tower_kernel(nc, A, out)
    r = _run(nc, [arrays], core_ids=[0])
    return r.results[0]["out_h"]
```

```python
import math
from contextlib import ExitStack

import concourse.bass as bass
from concourse import mybir

F32 = mybir.dt.float32
I32 = mybir.dt.int32
BF16 = mybir.dt.bfloat16
ALU = mybir.AluOpType
ACT = mybir.ActivationFunctionType
AX = mybir.AxisListType

B, S, D = 32, 128, 128
P = 128
V = 22
VP = 33
G = 4
NG = B // G
HALF = S // 2
CH = 16
NCH = S // CH


def alignment_stage(nc, used, A, H, ident, psum):
    w_dram = nc.dram_tensor("w_dram", (2, 2, B, S, HALF), F32, kind="Internal").ap()
    r_dram = nc.dram_tensor("r_dram", (2, 2 * B, S, HALF), F32, kind="Internal").ap()
    with ExitStack() as ctx:
        sb = lambda name, shape, dt=F32: ctx.enter_context(nc.sbuf_tensor(name, shape, dt))
        sem = lambda name: used.append(nc.alloc_semaphore(name)) or used[-1]
        onehot = sb("onehot", [VP, 3, B * S])
        letter = sb("letter", [VP, 1])
        emb = sb("emb", [V, P])
        wproj = sb("wproj", [P, P])
        bproj = sb("bproj", [P, 1])
        wgap = sb("wgap", [P, 2])
        bgap = sb("bgap", [V, 1])
        embT = sb("embT", [P, V])
        zT = sb("zT", [P, V])
        pair = sb("pair", [VP, VP])
        gap = sb("gap", [V, 2])
        gapcol = sb("gapcol", [V, 2, VP])
        counts = sb("counts", [V, 2, 4, B])
        gapscore = sb("gapscore", [VP, B])
        crow = sb("crow", [P, 1])
        pairY = sb("pairY", [VP, B * S])
        theta = sb("theta", [P, B, S])
        w_rows = sb("w_rows", [P, 2, B, S])
        w_dp = sb("w_dp", [P, S + 2, HALF])
        tok = w_dp[0:VP, 0:S, :].rearrange("v i j -> v (i j)").bitcast(I32).rearrange("v (k t) -> v k t", k=2)
        hist = sb("hist", [P, S + 2, HALF + 1])
        R = sb("R", [P, HALF])
        bb = sb("bb", [P, HALF])
        aa = sb("aa", [P, HALF])
        rH = sb("rH", [P, 2, HALF])
        xx = sb("xx", [P, HALF])
        gg = sb("gg", [P, 2, HALF])
        qq = sb("qq", [P, HALF])
        ratios = w_rows
        tri = sb("tri", [P, 2, P])
        th1 = sb("th1", [B, S])
        bfin = sb("bfin", [P, HALF])
        last = sb("last", [B, S])
        ones_bs = sb("ones_bs", [B, S])
        path1 = sb("path1", [B, S])
        lnlast = sb("lnlast", [B, S])
        dd = sb("dd", [P, 2, G * S])

        s_tok = sem("s_tok"); s_w = sem("s_w"); s_const = sem("s_const"); s_pc = sem("s_pc")
        s_embT = sem("s_embT"); s_embTc = sem("s_embTc"); s_z = sem("s_z"); s_zc = sem("s_zc")
        s_pair = sem("s_pair"); s_pairc = sem("s_pairc"); s_gc = sem("s_gc")
        s_hot = sem("s_hot"); s_one = sem("s_one"); s_cnt = sem("s_cnt"); s_A = sem("s_A"); s_Ac = sem("s_Ac")
        s_c = sem("s_c")
        s_y = sem("s_y"); s_yc = sem("s_yc"); s_yA = sem("s_yA")
        s_th = sem("s_th"); s_exp = sem("s_exp"); s_thc = sem("s_thc")
        s_wdp = [sem(f"s_wdp{q}") for q in range(NCH)]
        s_wst = sem("s_wst")
        s_rst = [sem(f"s_rst{q}") for q in range(NCH)]
        s_dve = sem("s_dve"); s_b = sem("s_b"); s_a = sem("s_a"); s_rh = sem("s_rh"); s_r = sem("s_r"); s_x = sem("s_x"); s_g = sem("s_g"); s_q = sem("s_q"); s_scan = sem("s_scan"); s_hand = sem("s_hand")
        s_rat = [sem(f"s_rathalf{q}") for q in range(2)]
        s_rat0 = sem("s_rat0"); s_th1 = sem("s_th1"); s_bf = sem("s_bf"); s_last = sem("s_last"); s_lnl = sem("s_lnl")
        s_p1 = sem("s_p1"); s_row1 = sem("s_row1"); s_ln = sem("s_ln"); s_D = sem("s_D"); s_dd = sem("s_dd"); s_h = sem("s_h")
        s_dch = sem("s_dch")
        block = ctx.enter_context(nc.Block())

        tokens = (A["x"], A["itok_BS_0_21"])

        @block.sync
        def _(sp):
            for k in range(2):
                src = tokens[k].rearrange("b s -> (b s)").unsqueeze(0).broadcast_to([VP, B * S])
                sp.dma_start(tok[:, k, :], src).then_inc(s_tok, 16)
            for n in range(2 * NG):
                m, d = n // 2, n % 2
                sp.wait_ge(s_exp, n + 1)
                for half in range(2):
                    dst = w_dram[half, d, m * G:(m + 1) * G, :, :].rearrange("b i j -> i b j")
                    sp.dma_start(dst, w_rows[:, d, m * G:(m + 1) * G, half * HALF:(half + 1) * HALF]).then_inc(s_wst, 16)
            sp.wait_ge(s_wst, 64 * NG)
            for q in range(NCH):
                for half in range(2):
                    r0 = 1 + q * CH + half
                    sp.dma_start(w_dp[half * 64:half * 64 + 64, r0:r0 + CH, :],
                                 w_dram[half, :, :, q * CH:(q + 1) * CH, :].rearrange("d b i j -> (d b) i j")).then_inc(s_wdp[q], 16)
            sp.wait_ge(s_thc, NG)
            sp.dma_start(th1[:, :], theta[0:1, :, :]).then_inc(s_th1, 16)
            for d in range(2):
                sp.dma_start(ratios[0:1, d, :, :], ones_bs[:, :]).then_inc(s_rat0, 16)
            for q in range(NCH + 1):
                for half in range(2):
                    if q < NCH:
                        lo = q * CH + (q == 0)
                        sp.wait_ge(s_scan, (q + 1) * CH + half)
                        src = hist[half * 64:half * 64 + 64, 1 + lo + half:1 + (q + 1) * CH + half, 1:]
                        sp.dma_start(r_dram[half, :, lo:(q + 1) * CH, :], src).then_inc(s_rst[q], 16)
                    if q == NCH - 1:
                        sp.wait_ge(s_bf, 1 + half)
                        sp.dma_start(last[:, half * HALF:(half + 1) * HALF], bfin[half * 64 + 32:half * 64 + 64, :]).then_inc(s_last, 16)
                if q:
                    lo = (q - 1) * CH + (q == 1)
                    sp.wait_ge(s_rst[q - 1], 32)
                    for half in range(2):
                        dst = ratios[lo:q * CH, :, :, half * HALF:(half + 1) * HALF].rearrange("i d b j -> i (d b) j")
                        sp.dma_start(dst, r_dram[half, :, lo:q * CH, :].rearrange("p i j -> i p j")).then_inc(s_rat[half], 16)
            sp.wait_ge(s_p1, 1)
            sp.wait_ge(s_ln, 1)
            sp.dma_start(ratios[0:1, 0, :, :], path1[:, :]).then_inc(s_row1, 16)

        @block.gpsimd
        def _(pool):
            pool.dma_start(emb[:, :], A["L0_tok_W_embed"]).then_inc(s_w, 16)
            pool.dma_start(wproj[:, :], A["L0_tok_W_proj"]).then_inc(s_w, 16)
            pool.dma_start(bproj[:, :], A["L0_tok_b_proj"].unsqueeze(1)).then_inc(s_w, 16)
            with nc.allow_non_contiguous_dma("two short columns"):
                pool.dma_start(wgap[:, :], A["L0_tok_W_gap"].rearrange("(k p) -> p k", k=2)).then_inc(s_w, 16)
            pool.dma_start(bgap[:, :], A["L0_tok_b_gap"].unsqueeze(1).broadcast_to([V, 1])).then_inc(s_w, 16)
            pool.memset(ident[:, :], 0.0).then_inc(s_pc, 1)
            pool.iota(letter[:, :], pattern=[[0, 1]], base=0, channel_multiplier=1, allow_small_or_imprecise_dtypes=True).then_inc(s_const, 1)
            pool.memset(pair[:, :], 0.0).then_inc(s_const, 1)
            pool.memset(gapcol[:, :, :], 0.0).then_inc(s_const, 1)
            pool.memset(R[:, :], 1.0).then_inc(s_const, 1)
            pool.memset(ones_bs[:, :], 1.0).then_inc(s_const, 1)
            pool.memset(hist[:, :, 0:1], 0.0).then_inc(s_const, 1)
            pool.memset(tri[:, :, :], 0.0).then_inc(s_pc, 1)
            pool.wait_ge(s_pc, 1)
            pool.affine_select(out=ident[:, :], in_=ident[:, :], compare_op=ALU.not_equal, fill=1.0, base=0,
                               pattern=[[-1, P]], channel_multiplier=1).then_inc(s_const, 1)
            pool.wait_ge(s_pc, 2)
            pool.affine_select(out=tri[:, 0, :], in_=tri[:, 0, :], compare_op=ALU.is_gt, fill=1.0, base=0,
                               pattern=[[-1, P]], channel_multiplier=1).then_inc(s_const, 1)
            pool.affine_select(out=tri[:, 1, :], in_=tri[:, 1, :], compare_op=ALU.is_gt, fill=-1.0, base=P,
                               pattern=[[-1, P]], channel_multiplier=-1).then_inc(s_const, 1)
            pool.wait_ge(s_const, 9)
            pool.wait_ge(s_hot, 3)
            for k in (0, 2):
                pool.memset(onehot[32:33, k, :], 1.0).then_inc(s_one, 1)
            pool.wait_ge(s_one, 2)
            pool.wait_ge(s_dve, 5)
            pool.tensor_tensor(qq[:, :], w_dp[:, 4, :], R[:, :], ALU.mult).then_inc(s_q, 3)
            for s in range(3, S + 2):
                p = slice(0 if s <= S else 64, P)
                pn = slice(0 if s < S else 64, P)
                if s <= S:
                    pool.wait_ge(s_q, s)
                pool.wait_ge(s_scan, s)
                if s <= S:
                    pool.tensor_tensor(gg[pn, (s + 1) % 2, :], qq[pn, :], hist[pn, s, 0:HALF], ALU.mult).then_inc(s_g, 4 if s == 3 else 1)
                if s == S:
                    pool.wait_ge(s_g, S + 1)
                if s > 3:
                    pool.wait_ge(s_r, s - 1)
                pool.tensor_tensor(xx[p, :], R[p, :], hist[p, s, 0:HALF], ALU.mult).then_inc(s_x, 3 if s == 3 else 1)
                pool.wait_ge(s_x, s)
                pool.wait_ge(s_rh, s)
                pool.tensor_tensor(R[p, :], xx[p, :], rH[p, (s + 1) % 2, :], ALU.mult).then_inc(s_r, 3 if s == 3 else 1)
                pool.wait_ge(s_r, s)
                if s < S:
                    pq = slice(0 if s + 2 <= S else 64, P)
                    if (s + 1) % CH == 0 and s + 1 < S:
                        pool.wait_ge(s_wdp[(s + 1) // CH], 32)
                    pool.tensor_tensor(qq[pq, :], w_dp[pq, s + 2, :], R[pq, :], ALU.mult).then_inc(s_q, 1)
                elif s == S:
                    pool.tensor_tensor(bfin[0:64, :], w_dp[0:64, S, :], R[0:64, :], ALU.mult).then_inc(s_bf, 1)
                    pool.wait_ge(s_bf, 1)
                else:
                    pool.tensor_tensor(bfin[64:128, :], w_dp[64:128, S + 1, :], R[64:128, :], ALU.mult).then_inc(s_bf, 1)

        @block.tensor
        def _(pe):
            pe.wait_ge(s_w, 80)
            pe.wait_ge(s_const, 7)
            pe.transpose(psum[0][:, 0:V], emb[:, :], ident[0:V, 0:V]).then_inc(s_embT, 1)
            pe.wait_ge(s_embTc, 1)
            pe.matmul(psum[1][:, 0:V], wproj[:, :], embT[:, :], start=True, stop=True).then_inc(s_z, 1)
            pe.wait_ge(s_zc, 1)
            pe.matmul(psum[2][0:V, 0:V], zT[:, :], zT[:, :], start=True, stop=True).then_inc(s_pair, 1)
            pe.matmul(psum[3][0:V, 0:2], zT[:, :], wgap[:, :], start=True, stop=True).then_inc(s_pair, 1)
            pe.wait_ge(s_gc, 4)
            pe.wait_ge(s_cnt, 2)
            pe.matmul(psum[0][0:VP, 0:B], gapcol[:, 0, :], counts[:, 0, 0, :], start=True, stop=False)
            pe.matmul(psum[0][0:VP, 0:B], gapcol[:, 1, :], counts[:, 1, 0, :], start=False, stop=True).then_inc(s_A, 1)
            pe.matmul(psum[1][:, 0:1], counts[:, 0, :, :].rearrange("v r b -> v (r b)"), gap[:, 0:1], start=True, stop=False)
            pe.matmul(psum[1][:, 0:1], counts[:, 1, :, :].rearrange("v r b -> v (r b)"), gap[:, 1:2], start=False, stop=True).then_inc(s_A, 1)
            pe.wait_ge(s_pairc, 1)
            for m in range(NG):
                bank = psum[2 + m % 4]
                if m >= 4:
                    pe.wait_ge(s_yc, m - 3)
                pe.matmul(bank[0:VP, :], pair[:, :], onehot[:, 1, m * 512:(m + 1) * 512], start=True, stop=True).then_inc(s_y, 1)
            pe.wait_ge(s_one, 2)
            pe.wait_ge(s_yA, 1)
            pe.wait_ge(s_c, 1)
            for m in range(NG):
                for d in range(2):
                    n = 2 * m + d
                    bank = psum[n % 8]
                    if n >= 8:
                        pe.wait_ge(s_exp, n - 7)
                    if d == 0 and m >= 4:
                        pe.wait_ge(s_thc, m - 3)
                    for k in range(G):
                        b = m * G + k
                        X = onehot[:, 2 * d, b * S:(b + 1) * S]
                        Y = pairY[:, b * S:(b + 1) * S]
                        if d:
                            Y = Y[:, ::-1]
                        mm = pe.matmul(bank[:, k * S:(k + 1) * S], X, Y, start=True, stop=True)
                    mm.then_inc(s_th, 1)
            pe.wait_ge(s_row1, 16)
            for m in range(NG):
                pe.wait_ge(s_ln, 2)
                if m >= 4:
                    pe.wait_ge(s_dd, m - 3)
                pe.matmul(psum[m % 4][:, :], tri[:, 0, :], ratios[:, 0, m * G:(m + 1) * G, :], start=True, stop=False)
                pe.matmul(psum[m % 4][:, :], tri[:, 1, :], ratios[:, 1, m * G:(m + 1) * G, ::-1], start=False, stop=True).then_inc(s_D, 1)

        @block.scalar
        def _(act):
            act.wait_ge(s_embT, 1)
            act.activation(embT[:, :], psum[0][:, 0:V], ACT.Copy).then_inc(s_embTc, 1)
            act.wait_ge(s_z, 1)
            act.activation(zT[:, :], psum[1][:, 0:V], ACT.Identity, bias=bproj[:, :]).then_inc(s_zc, 1)
            act.wait_ge(s_pair, 1)
            act.activation(pair[0:V, 0:V], psum[2][0:V, 0:V], ACT.Copy).then_inc(s_pairc, 1)
            act.wait_ge(s_A, 2)
            act.activation(crow[:, :], psum[1][:, 0:1], ACT.Exp, scale=-1.0).then_inc(s_c, 1)
            for n in range(2 * NG):
                group = slice((n // 2) * G, (n // 2 + 1) * G)
                if n % 2 == 0:
                    act.wait_ge(s_thc, n // 2 + 1)
                    act.activation(w_rows[:, 0, group, :], theta[:, group, :], ACT.Exp).then_inc(s_exp, 1)
                else:
                    act.wait_ge(s_th, n + 1)
                    act.activation(w_rows[:, 1, group, :], psum[n % 8][:, :], ACT.Exp).then_inc(s_exp, 1)
            for s in range(3, S + 2):
                act.wait_ge(s_scan, s - 1)
                act.activation(hist[64:128, s, 0:1], hist[0:64, s - 1, HALF:HALF + 1], ACT.Copy).then_inc(s_hand, 3 if s == 3 else 1)
            act.wait_ge(s_last, 32)
            act.activation(lnlast[:, 1:S], last[:, 1:S], ACT.Ln).then_inc(s_lnl, 1)
            act.wait_ge(s_rat0, 32)
            for half in range(2):
                act.wait_ge(s_rat[half], 16 * NCH)
            for d in range(2):
                act.activation(ratios[:, d, :, :], ratios[:, d, :, :], ACT.Ln).then_inc(s_ln, 1)
            for m in range(NG):
                act.wait_ge(s_dd, m + 1)
                act.activation(H[:, m * G:(m + 1) * G, :], dd[:, m % 2, :], ACT.Exp).then_inc(s_h, 1)

        @block.vector
        def _(dve):
            dve.wait_ge(s_const, 1)
            for k in (1, 0):
                dve.wait_ge(s_tok, 32)
                dve.tensor_scalar(onehot[:, k, :], tok[:, k, :], letter[:, :], None, ALU.is_equal).then_inc(s_hot, 1)
            dve.tensor_scalar(onehot[:, 2, :].rearrange("v (b s) -> v b s", b=B), tok[:, 0, :].rearrange("v (b s) -> v b s", b=B)[:, :, ::-1],
                              letter[:, :], None, ALU.is_equal).then_inc(s_hot, 1)
            dve.wait_ge(s_w, 80)
            dve.wait_ge(s_hot, 2)
            for k in range(2):
                dve.tensor_reduce(counts[:, k, 0, :], onehot[0:V, k, :].rearrange("v (b s) -> v b s", b=B), AX.X, ALU.add).then_inc(s_dch, 1)
            dve.wait_ge(s_dch, 2)
            for k in range(2):
                dve.tensor_copy(counts[:, k, 1:4, :], counts[:, k, 0:1, :].broadcast_to([V, 3, B])).then_inc(s_cnt, 1)
            dve.wait_ge(s_pair, 2)
            dve.tensor_scalar(gap[:, 0:1], psum[3][0:V, 0:1], bgap[:, :], 1.0 / S, ALU.add, ALU.mult).then_inc(s_gc, 1)
            dve.tensor_scalar(gap[:, 1:2], psum[3][0:V, 1:2], 1.0 / S, None, ALU.mult).then_inc(s_gc, 1)
            dve.wait_ge(s_gc, 2)
            for k in range(2):
                dve.tensor_copy(gapcol[:, k, 32:33], gap[:, k:k + 1]).then_inc(s_gc, 1)
            dve.wait_ge(s_A, 1)
            dve.tensor_copy(gapscore[:, :], psum[0][0:VP, 0:B]).then_inc(s_Ac, 1)
            for m in range(NG):
                dve.wait_ge(s_y, m + 1)
                dve.tensor_copy(pairY[:, m * 512:(m + 1) * 512], psum[2 + m % 4][0:VP, :]).then_inc(s_yc, 1)
            dve.wait_ge(s_yc, NG)
            dve.wait_ge(s_Ac, 1)
            dve.tensor_copy(pairY[32:33, :].rearrange("v (b s) -> v b s", b=B),
                            gapscore[32:33, :].unsqueeze(2).broadcast_to([1, B, S])).then_inc(s_yA, 1)
            for m in range(NG):
                dve.wait_ge(s_th, 2 * m + 1)
                dve.tensor_copy(theta[:, m * G:(m + 1) * G, :], psum[(2 * m) % 8][:, :]).then_inc(s_thc, 1)

            dve.wait_ge(s_c, 1)
            dve.wait_ge(s_wdp[0], 32)
            dve.wait_ge(s_const, 9)
            dve.reciprocal(R[0:64, :], w_dp[0:64, 1, :]).then_inc(s_dve, 1)
            dve.wait_ge(s_dve, 1)
            dve.memset(R[0:64, 0:1], 0.0).then_inc(s_dve, 1)
            dve.wait_ge(s_dve, 2)
            dve.tensor_tensor(bb[0:64, :], w_dp[0:64, 2, :], R[0:64, :], ALU.mult).then_inc(s_b, 2)
            dve.wait_ge(s_b, 2)
            dve.scalar_tensor_tensor(aa[0:64, :], bb[0:64, :], crow[0:64, :], w_dp[0:64, 2, :], ALU.mult, ALU.add).then_inc(s_a, 2)
            dve.wait_ge(s_a, 2)
            dve.tensor_tensor_scan(hist[0:64, 2, 1:HALF + 1], bb[0:64, :], aa[0:64, :], 0.0, ALU.mult, ALU.add).then_inc(s_scan, 2)
            dve.wait_ge(s_scan, 2)
            dve.reciprocal(rH[0:64, 0, :], hist[0:64, 2, 1:HALF + 1]).then_inc(s_rh, 2)
            dve.wait_ge(s_rh, 2)
            dve.tensor_tensor(xx[0:64, :], rH[0:64, 0, :], hist[0:64, 2, 0:HALF], ALU.mult).then_inc(s_dve, 1)
            dve.wait_ge(s_dve, 3)
            dve.tensor_tensor(R[0:64, :], R[0:64, :], xx[0:64, :], ALU.mult).then_inc(s_dve, 1)
            dve.reciprocal(R[64:128, :], w_dp[64:128, 2, :]).then_inc(s_dve, 1)
            dve.wait_ge(s_dve, 5)
            for s in range(3, S + 2):
                p = slice(0 if s <= S else 64, P)
                w, h = w_dp[p, s, :], hist[p, s, 1:HALF + 1]
                if (s - 1) % CH == 0 and s <= S:
                    dve.wait_ge(s_wdp[(s - 1) // CH], 32)
                if s == 3:
                    dve.tensor_tensor(bb[p, :], w, R[p, :], ALU.mult).then_inc(s_b, 1)
                else:
                    dve.wait_ge(s_rh, s - 1)
                    dve.wait_ge(s_g, s)
                    dve.tensor_tensor(bb[p, :], gg[p, s % 2, :], rH[p, s % 2, :], ALU.mult).then_inc(s_b, 1)
                dve.wait_ge(s_b, s)
                dve.scalar_tensor_tensor(aa[p, :], bb[p, :], crow[p, :], w, ALU.mult, ALU.add).then_inc(s_a, 1)
                dve.wait_ge(s_a, s)
                if s > 3:
                    dve.wait_ge(s_hand, s)
                else:
                    dve.wait_ge(s_hand, 3)
                dve.tensor_tensor_scan(h, bb[p, :], aa[p, :], hist[p, s, 0:1], ALU.mult, ALU.add).then_inc(s_scan, 1)
                dve.wait_ge(s_scan, s)
                dve.reciprocal(rH[p, (s + 1) % 2, :], h).then_inc(s_rh, 1)

            dve.wait_ge(s_lnl, 1)
            dve.wait_ge(s_bf, 2)
            dve.tensor_tensor_scan(path1[:, 1:S], ones_bs[:, 1:S], lnlast[:, 1:S][:, ::-1], 0.0, ALU.mult, ALU.add).then_inc(s_dch, 1)
            dve.memset(path1[:, 0:1], 0.0).then_inc(s_dch, 1)
            dve.wait_ge(s_dch, 4)
            dve.wait_ge(s_th1, 16)
            dve.tensor_tensor(path1[:, :], path1[:, :], th1[:, :], ALU.add).then_inc(s_p1, 1)
            for m in range(NG):
                dve.wait_ge(s_D, m + 1)
                if m >= 2:
                    dve.wait_ge(s_h, m - 1)
                dve.tensor_tensor(dd[:, m % 2, :], psum[m % 4][:, :], theta[:, m * G:(m + 1) * G, :].rearrange("p b s -> p (b s)"),
                                  ALU.subtract).then_inc(s_dd, 1)


HEADS = 8
DK = D // HEADS
KV_HEADS = (8, 4, 1)
PADK = 32
K1 = 64
E = 8
TABW = D + E
DECAY = 0.96875
WQ, WK, WV, WO, WALL = 0, HEADS * PADK, 2 * HEADS * PADK, 2 * HEADS * PADK + D, 2 * HEADS * PADK + 2 * D


def layers_stage(nc, used, A, H, ident, psall, table, logitsT, w1, w2, s_weights):
    psum = [psall[:, i, :] for i in range(8)]
    with ExitStack() as ctx:
        sb = lambda name, shape, dt=F32: ctx.enter_context(nc.sbuf_tensor(name, shape, dt))
        sem = lambda name: used.append(nc.alloc_semaphore(name)) or used[-1]
        wq0 = sb("wq0", [P, P]); wk0 = sb("wk0", [P, P]); wv0 = sb("wv0", [P, P])
        wqT = sb("wqT", [P, P]); wkT = sb("wkT", [P, P]); wkq = sb("wkq", [P, P])
        decay = sb("decay", [P, P])
        rw1 = sb("rw1", [P, 32]); rb1 = sb("rb1", [32, 1]); rw2 = sb("rw2", [32, 3]); rb2 = sb("rb2", [1, 3])
        variants = sb("variants", [P, 3, WALL])
        chosen = sb("chosen", [P, G, WALL])
        wq1 = sb("wq1", [P, HEADS * K1]); wk1 = sb("wk1", [P, HEADS * K1])
        wvo = sb("wvo", [P, HEADS, D])
        bo = sb("bo", [P, D]); gamma = sb("gamma", [P, D]); beta = sb("beta", [P, D])
        wr = sb("wr", [P, E])
        power = sb("power", [P, G])
        stats = sb("stats", [P, 5, G, 6]); mv = sb("mv", [P, 5, G, 2]); ve = sb("ve", [P, 5, G]); rstd = sb("rstd", [P, 5, G])
        xh = [sb(f"xh{i}", [P, G, D]) for i in range(4)]
        xT = [sb(f"xT{i}", [P, G, S]) for i in range(4)]
        pT = sb("pT", [P, G, S]); v0 = sb("v0", [P, G, D])
        sd = sb("sd", [P, G, S]); th = sb("th", [P, G, S]); act0 = sb("act0", [P, G, S])
        msum = sb("msum", [P, G]); r1 = sb("r1", [32, G]); lg = sb("lg", [1, G, 3]); c1 = sb("c1", [1, G]); mx1 = sb("mx1", [1, G])
        c2 = sb("c2", [1, G]); sel = sb("sel", [1, G], I32)
        qk = sb("qk", [P, G, 4, S]); v17 = sb("v17", [P, G, HEADS, DK + 1])
        smax = sb("smax", [P, 2, 2, HEADS]); bias = sb("bias", [P, 2, 2, HEADS])
        ex = [sb(f"ex{i}", [P, 2, HEADS, S]) for i in range(2)]
        wv1, wo1, wvT = ex[0][:, 0, :, :], ex[0][:, 1, :, :], ex[1][:, 0, :, :]
        exT = sb("exT", [P, HEADS, S])
        rden = sb("rden", [P, HEADS]); o0 = sb("o0", [P, G, D]); oT = sb("oT", [P, G, S])
        qT1 = sb("qT1", [P, 4, G * S]); kT1 = sb("kT1", [P, 4, G * S]); vo = sb("vo", [P, G, HEADS, D])
        masked = sb("masked", [P, HEADS, S]); den = sb("den", [P, 2, HEADS]); rden1 = sb("rden1", [P, 2, HEADS])
        y1 = sb("y1", [P, G, D]); y2 = sb("y2", [P, G, D])

        s_in = sem("s_in"); s_pc = sem("s2_pc"); s_var0 = sem("s_var0")
        s_iota = sem("s_iota"); s_abs = sem("s_abs"); s_dec = sem("s_dec")
        s_wt = sem("s_wt"); s_wtc = sem("s_wtc"); s_m0 = sem("s_m0"); s_m0c = sem("s_m0c"); s_one = sem("s2_one")
        s_bn = [sem(f"s_bn{i}") for i in range(5)]; s_mv = [sem(f"s_mv{i}") for i in range(5)]
        s_ve = [sem(f"s_ve{i}") for i in range(5)]; s_rstd = [sem(f"s_rstd{i}") for i in range(5)]
        s_xh = [sem(f"s_xh{i}") for i in range(5)]
        s_xT = [sem(f"s_xT{i}") for i in range(4)]; s_xTc = [sem(f"s_xTc{i}") for i in range(4)]
        s_p = sem("s_p"); s_pT = sem("s_pT"); s_v0 = sem("s_v0"); s_v0c = sem("s_v0c"); s_s0 = sem("s_s0"); s_sd = sem("s_sd")
        s_th = sem("s2_th"); s_act0 = sem("s_act0"); s_o = sem("s_o"); s_h = [sem(f"s_h{i}") for i in range(3)]
        s_ms = sem("s_ms"); s_r1 = sem("s_r1"); s_r1c = sem("s_r1c"); s_lg = sem("s_lg"); s_rt = sem("s_rt"); s_sel = sem("s_sel")
        s_ch = sem("s_ch"); s_chw = sem("s_chw"); s_qk = sem("s_qk"); s_qkc = sem("s_qkc"); s_v = sem("s_v"); s_vc = sem("s_vc")
        s_half = sem("s_half"); s_sc = [sem(f"s_sc{i}") for i in range(2)]; s_mx = [sem(f"s_mx{i}") for i in range(2)]
        s_bias = [sem(f"s_bias{i}") for i in range(2)]
        s_ex = [sem(f"s_ex{i}") for i in range(2)]; s_eT = [sem(f"s_eT{i}") for i in range(2)]
        s_eTa = [sem(f"s_eTa{i}") for i in range(2)]; s_eTv = [sem(f"s_eTv{i}") for i in range(2)]
        s_av = [sem(f"s_av{i}") for i in range(2)]
        s_rd = sem("s_rd"); s_o0 = sem("s_o0"); s_oT = sem("s_oT"); s_oTc = sem("s_oTc"); s_wo = sem("s_wo")
        s_q1 = sem("s_q1"); s_q1a = sem("s_q1a"); s_q1v = sem("s_q1v"); s_vo = sem("s_vo"); s_voa = sem("s_voa"); s_vov = sem("s_vov")
        s_zero = sem("s_zero"); s_rd1 = sem("s_rd1"); s_nrm = sem("s_nrm")
        s_xb = sem("s_xb"); s_y = sem("s_y2"); s_gm = sem("s_gm"); s_lt = sem("s_lt"); s_ltc = sem("s_ltc"); s_tab = sem("s_tab")
        block = ctx.enter_context(nc.Block())
        rows = lambda g, k: H[:, bass.ds(g * G + k, 1), :].squeeze(1)
        group = lambda g: H[:, bass.ds(g * G, G), :]
        bank = lambda i: psum[i].rearrange("p (k s) -> p k s", k=G)
        first = lambda g: isinstance(g, int) and g == 0

        def wait_alone(eng, signal, value):
            if not isinstance(value, int):
                value = eng.to_reg(value)
            eng.wait_ge(s_in, IN)
            eng.wait_ge(signal, value)

        def turns(eng, body):
            for t in range(3):
                body(t, True, t >= 1, t >= 2, False, True)
            with eng.Fori(3, NG - 1) as t:
                body(t, True, True, True, True, True)
            for t in range(NG - 1, NG + 3):
                body(t, t < NG, t < NG + 1, t < NG + 2, True, False)

        IN = 16 * (15 + 3 * 2 + 2 * sum(HEADS // n for n in KV_HEADS))

        @block.sync
        def _(sp):
            sp.dma_start(wq0[:, :], A["L0_attn_W_Q"]).then_inc(s_in, 16)
            sp.dma_start(wk0[:, :], A["L0_attn_W_K"]).then_inc(s_in, 16)
            sp.dma_start(wv0[:, :], A["L0_attn_W_V"]).then_inc(s_in, 16)
            sp.dma_start(wv1[:, :, :], A["L1_attn_Wv"].rearrange("d (h n) -> d h n", h=HEADS)).then_inc(s_in, 16)
            sp.dma_start(wo1[:, :, :], A["L1_attn_Wo"].rearrange("(h p) n -> p h n", h=HEADS)).then_inc(s_in, 16)
            sp.dma_start(wq1[:, :], A["L1_attn_Wq"]).then_inc(s_in, 16)
            sp.dma_start(wk1[:, :], A["L1_attn_Wk"]).then_inc(s_in, 16)
            sp.dma_start(rw1[:, :], A["L0_ffn_r_w1"]).then_inc(s_in, 16)
            sp.dma_start(rb1[:, :], A["L0_ffn_r_b1"].unsqueeze(1)).then_inc(s_in, 16)
            sp.dma_start(rw2[:, :], A["L0_ffn_r_w2"]).then_inc(s_in, 16)
            sp.dma_start(rb2[:, :], A["L0_ffn_r_b2"].unsqueeze(0)).then_inc(s_in, 16)
            sp.dma_start(wr[:, :], A["L1_ffn_Wr"]).then_inc(s_in, 16)
            for t, name in ((bo, "L1_attn_bo"), (gamma, "L1_attn_gamma"), (beta, "L1_attn_beta")):
                sp.dma_start(t[:, :], A[name].unsqueeze(0).broadcast_to([P, D])).then_inc(s_in, 16)
            sp.wait_ge(s_var0, 1)
            with nc.allow_non_contiguous_dma("a head's columns, set apart"):
                for i, n in enumerate(KV_HEADS):
                    padded = lambda c: variants[:, i, c:c + HEADS * PADK].rearrange("p (h c) -> p h c", c=PADK)[:, :, 0:DK]
                    sp.dma_start(padded(WQ), A[f"L0_ffn_wq{i}"].rearrange("p (h c) -> p h c", c=DK)).then_inc(s_in, 16)
                    for r in range(HEADS // n):
                        for c, name in ((WK, "wk"), (WV, "wv")):
                            src = A[f"L0_ffn_{name}{i}"].rearrange("p (h c) -> p h c", c=DK)
                            dst = padded(WK) if c == WK else variants[:, i, WV:WV + D].rearrange("p (h c) -> p h c", c=DK)
                            sp.dma_start(dst[:, r::HEADS // n, :], src).then_inc(s_in, 16)
                    sp.dma_start(variants[:, i, WO:WALL], A[f"L0_ffn_wo{i}"]).then_inc(s_in, 16)
            sp.dma_start(w1[:, :, :], A["L1_ffn_W1"].rearrange("e d f -> d e f")).then_inc(s_weights, 16)
            for e in range(E):
                sp.dma_start(w2[:, e, :, :], A["L1_ffn_W2"][e].rearrange("(c p) d -> p c d", p=P)).then_inc(s_weights, 16)
            sp.wait_ge(s_in, IN)

            def body(t, a1, a2, b, c, ahead):
                if a1:
                    wait_alone(sp, s_sel, t + 1)
                    picks = [sp.value_load(sel[0:1, k:k + 1], min_val=0, max_val=2) for k in range(G)]
                    if a2:
                        sp.wait_ge(s_v, t)
                    for k in range(G):
                        sp.dma_start(chosen[:, k, 0:WO], variants[:, bass.ds(picks[k], 1), 0:WO].squeeze(1)).then_inc(s_ch, 16)
                    if a2:
                        sp.wait_ge(s_wo, t)
                    for k in range(G):
                        sp.dma_start(chosen[:, k, WO:WALL], variants[:, bass.ds(picks[k], 1), WO:WALL].squeeze(1)).then_inc(s_chw, 16)
                if c:
                    g = t - 3
                    sp.wait_ge(s_xh[3], g * G + G)
                    sp.dma_start(table[bass.ds(g * G * S, G * S), :].rearrange("(k s) d -> s k d", k=G), xh[3][:, :, :]).then_inc(s_tab, 16)

            turns(sp, body)
            sp.wait_ge(s_tab, 16 * NG)

        @block.gpsimd
        def _(pool):
            pool.memset(variants[:, :, :], 0.0).then_inc(s_var0, 1)
            pool.iota(decay[:, :], pattern=[[1, P]], base=0, channel_multiplier=-1, allow_small_or_imprecise_dtypes=True).then_inc(s_iota, 1)
            pool.memset(power[:, :], -0.5).then_inc(s_pc, 1)
            pool.memset(v17[:, :, :, DK:DK + 1], 1.0).then_inc(s_one, 1)
            pool.wait_ge(s_in, IN)
            pool.wait_ge(s_pc, 1)

            def ln_rstd(g, i, eps):
                wait_alone(pool, s_mv[i], g * G + G)
                pool.tensor_scalar(ve[:, i, :], mv[:, i, :, 1], eps, None, ALU.add).then_inc(s_ve[i], 1)
                pool.wait_ge(s_ve[i], g + 1)
                pool.tensor_tensor(rstd[:, i, :], ve[:, i, :], power[:, :], ALU.pow).then_inc(s_rstd[i], 1)

            def share(g, k):
                pool.wait_ge(s_rd1, g * G + k + 1)
                pool.tensor_tensor(ex[1][:, k % 2, :, :], ex[1][:, k % 2, :, :],
                                   rden1[:, k % 2, :].unsqueeze(2).broadcast_to([P, HEADS, S]), ALU.mult).then_inc(s_nrm, 1)

            def affine(g):
                pool.wait_ge(s_xh[4], g * G + G)
                pool.tensor_tensor(y2[:, :, :], y2[:, :, :], gamma[:, :].unsqueeze(1).broadcast_to([P, G, D]), ALU.mult).then_inc(s_gm, 1)
                pool.wait_ge(s_gm, 2 * g + 1)
                pool.tensor_tensor(y2[:, :, :], y2[:, :, :], beta[:, :].unsqueeze(1).broadcast_to([P, G, D]), ALU.add).then_inc(s_gm, 1)

            def residual(g):
                pool.wait_ge(s_xh[2], g * G + G)
                pool.tensor_tensor(y1[:, :, :], xh[2][:, :, :], bo[:, :].unsqueeze(1).broadcast_to([P, G, D]), ALU.add).then_inc(s_xb, 1)

            ln_rstd(0, 0, 1e-5)

            def body(t, a1, a2, b, c, ahead):
                g2, g3, g4 = t - 1, t - 2, t - 3
                if b:
                    ln_rstd(g3, 2, 1e-5)
                if c:
                    ln_rstd(g4, 4, 1e-6)
                    affine(g4)
                    ln_rstd(g4, 3, 1e-5)
                if b:
                    share(g3, 0)
                    residual(g3)
                if a1:
                    ln_rstd(t, 1, 1e-5)
                if b:
                    share(g3, 1)
                    share(g3, 2)
                if ahead:
                    ln_rstd(t + 1, 0, 1e-5)
                if b:
                    share(g3, 3)

            turns(pool, body)

        @block.tensor
        def _(pe):
            pe.wait_ge(s_in, IN)
            pe.transpose(psum[0][:, 0:P], wk0[:, :], ident[:, :])
            pe.transpose(psum[0][:, P:2 * P], wq0[:, :], ident[:, :]).then_inc(s_wt, 1)
            for n in range(2):
                for h in range(4):
                    mm = pe.transpose(psum[1 + n][:, h * P:(h + 1) * P], wv1[:, 4 * n + h, :], ident[:, :])
                mm.then_inc(s_wt, 1)
            pe.wait_ge(s_wtc, 4)
            pe.matmul(psum[3][:, 0:P], wkT[:, :], wqT[:, :], start=True, stop=True).then_inc(s_m0, 1)
            for n in range(2):
                for h in range(4):
                    mm = pe.matmul(psum[4 + n][:, h * P:(h + 1) * P], wvT[:, 4 * n + h, :], wo1[:, 4 * n + h, :], start=True, stop=True)
                mm.then_inc(s_m0, 1)
            pe.wait_ge(s_m0c, 3)


            def turn_x(g, i, b):
                pe.wait_ge(s_xh[i], g * G + G)
                for k in range(G):
                    mm = pe.transpose(psum[b][:, k * S:(k + 1) * S], xh[i][:, k, :], ident[:, :])
                mm.then_inc(s_xT[i], 1)

            def turn_ex(g, i, k):
                pe.wait_ge(s_ex[0] if i == 0 else s_nrm, g * G + k + 1)
                for n in range(HEADS):
                    mm = pe.transpose(psum[2 + n // 4][:, (n % 4) * S:(n % 4 + 1) * S], ex[i][:, k % 2, n, :], ident[:, :])
                mm.then_inc(s_eT[i], 1)

            def a1_xT(t):
                turn_x(t, 0, 0)

            def a1_p(t):
                pe.wait_ge(s_xTc[0], t + 1)
                pe.matmul(psum[0], wkq[:, :], xT[0][:, :, :], start=True, stop=True).then_inc(s_p, 1)

            def a1_v(t):
                pe.wait_ge(s_pT, t + 1)
                for k in range(G):
                    mm = pe.matmul(psum[0][:, k * D:(k + 1) * D], xT[0][:, k, :], wv0[:, :], start=True, stop=True)
                mm.then_inc(s_v0, 1)

            def a1_s(t):
                pe.wait_ge(s_v0c, t + 1)
                for k in range(G):
                    mm = pe.matmul(psum[0][:, k * S:(k + 1) * S], pT[:, k, :], xT[0][:, k, :], start=True, stop=True)
                mm.then_inc(s_s0, 1)

            def a1_o(t):
                pe.wait_ge(s_act0, t + 1)
                for k in range(G):
                    mm = pe.matmul(psum[0][:, k * D:(k + 1) * D], act0[:, k, :], v0[:, k, :], start=True, stop=True)
                mm.then_inc(s_o, 1)

            def a1_xT2(t):
                turn_x(t, 1, 0)

            def a1_r1(t):
                pe.wait_ge(s_ms, t + 1)
                pe.matmul(psum[0][0:32, 0:G], rw1[:, :], msum[:, :], start=True, stop=True).then_inc(s_r1, 1)

            def a1_lg(t):
                wait_alone(pe, s_r1c, t + 1)
                for k in range(G):
                    mm = pe.matmul(psum[0][0:1, 3 * k:3 * k + 3], r1[:, k:k + 1], rw2[:, :], start=True, stop=True)
                mm.then_inc(s_lg, 1)

            def a2_v(g):
                for k in range(G):
                    mm = pe.matmul(psum[1][:, k * D:(k + 1) * D], xT[1][:, k, :], chosen[:, k, WV:WO], start=True, stop=True)
                mm.then_inc(s_v, 1)

            def a2_qk(g):
                pe.wait_ge(s_ch, (g + 1) * 16 * G)
                pe.wait_ge(s_xTc[1], g + 1)
                for k in range(G):
                    if k >= 2:
                        pe.wait_ge(s_qkc, g * G + k - 1)
                    for c in range(4):
                        mm = pe.matmul(psum[4 + k % 2][:, c * S:(c + 1) * S], chosen[:, k, c * P:(c + 1) * P], xT[1][:, k, :], start=True, stop=True)
                    mm.then_inc(s_qk, 1)

            def a2_scores(g, k, pair):
                n = g * G + k
                if pair == 0:
                    pe.wait_ge(s_qkc, g * G + G)
                    if k:
                        pe.wait_ge(s_ex[0], n)
                else:
                    pe.wait_ge(s_half, n + 1)
                for c in range(2):
                    for r in range(2 * pair, 2 * pair + 2):
                        q = slice(r * PADK, (r + 1) * PADK)
                        col = (2 * pair + c) * S
                        mm = pe.matmul(psum[4 + r % 2][:, col:col + S], qk[q, k, c, :], qk[q, k, 2 + c, :], start=True, stop=True)
                mm.then_inc(s_sc[0] if pair else s_half, 1)

            def a2_weigh(g, k):
                n = g * G + k
                pe.wait_ge(s_vc, g + 1)
                pe.wait_ge(s_eTa[0], n + 1)
                pe.wait_ge(s_eTv[0], n + 1)
                for m in range(HEADS):
                    h = 4 * (m % 2) + m // 4 + 2 * (m % 4 // 2)
                    mm = pe.matmul(psum[1][:, h * (DK + 1):(h + 1) * (DK + 1)], exT[:, m, :], v17[:, k, h, :], start=True, stop=True)
                mm.then_inc(s_av[0], 1)

            def a2_oT(g):
                pe.wait_ge(s_o0, g * G + G)
                pe.wait_ge(s_ex[0], g * G + G)
                for k in range(G):
                    mm = pe.transpose(psum[4][:, k * S:(k + 1) * S], o0[:, k, :], ident[:, :])
                mm.then_inc(s_oT, 1)

            def a2_wo(g):
                pe.wait_ge(s_oTc, g + 1)
                pe.wait_ge(s_chw, (g + 1) * 16 * G)
                for k in range(G):
                    mm = pe.matmul(psum[5][:, k * D:(k + 1) * D], oT[:, k, :], chosen[:, k, WO:WALL], start=True, stop=True)
                mm.then_inc(s_wo, 1)

            def b_qk(g, part):
                for c in range(4 * part, 4 * part + 4):
                    if c == 0:
                        pe.wait_ge(s_xTc[2], g + 1)
                    if 2 <= c < 6:
                        pe.wait_ge(s_q1a, g * 4 + c - 1)
                    if c >= 6:
                        pe.wait_ge(s_q1v, g * 4 + c - 5)
                    w = wq1 if c < 4 else wk1
                    pe.matmul(psum[7 - c % 2], w[:, (c % 4) * P:(c % 4 + 1) * P], xT[2][:, :, :], start=True, stop=True).then_inc(s_q1, 1)

            def b_values(g, n):
                pe.matmul(psum[1], xT[2][:, n // 2, :], wvo[:, 4 * (n % 2):4 * (n % 2) + 4, :], start=True, stop=True).then_inc(s_vo, 1)

            def b_scores(g, k):
                if k:
                    pe.wait_ge(s_mx[1], HEADS * (g * G + k))
                else:
                    pe.wait_ge(s_q1v, g * 4 + 4)
                for h in range(HEADS):
                    r = slice((h % 2) * K1, (h % 2 + 1) * K1)
                    mm = pe.matmul(psum[6 + h % 2][:, (h // 2) * S:(h // 2 + 1) * S], qT1[r, h // 2, k * S:(k + 1) * S],
                                   kT1[r, h // 2, k * S:(k + 1) * S], start=True, stop=True)
                mm.then_inc(s_sc[1], 1)

            def b_weigh(g, k):
                n = g * G + k
                pe.wait_ge(s_eTa[1], n + 1)
                pe.wait_ge(s_eTv[1], n + 1)
                for m in range(HEADS):
                    mm = pe.matmul(psum[1][:, 0:D], exT[:, m, :], vo[:, k, 2 * (m % 4) + m // 4, :], start=(m == 0), stop=(m == HEADS - 1))
                mm.then_inc(s_av[1], 1)

            def c_logits(g):
                pe.wait_ge(s_xTc[3], g + 1)
                pe.matmul(psum[0][0:E, :], wr[:, :], xT[3][:, :, :], start=True, stop=True).then_inc(s_lt, 1)

            def body(t, a1, a2, b, c, ahead):
                g2, g3, g4 = t - 1, t - 2, t - 3
                if c:
                    turn_ex(g4, 1, 3)
                if a2:
                    if not first(g2):
                        pe.wait_ge(s_h[1], g2)
                    a2_qk(g2)
                if c:
                    pe.wait_ge(s_y, g4 * G + 3)
                    b_weigh(g4, 3)
                if a2:
                    if c:
                        pe.wait_ge(s_y, g4 * G + 4)
                    a2_v(g2)
                if a1:
                    if not first(t):
                        pe.wait_ge(s_rt, 5 * t - 4)
                    if c and not first(g4):
                        pe.wait_ge(s_ltc, g4)
                    a1_xT(t)
                if b:
                    turn_x(g3, 2, 6)
                    b_qk(g3, 0)
                if a2:
                    a2_scores(g2, 0, 0)
                    a2_scores(g2, 0, 1)
                if a1:
                    a1_p(t)
                if b:
                    b_qk(g3, 1)
                if a1:
                    a1_v(t)
                if a2:
                    turn_ex(g2, 0, 0)
                if b:
                    b_scores(g3, 0)
                    if a2:
                        pe.wait_ge(s_vc, g2 + 1)
                    else:
                        pe.wait_ge(s_y, g4 * G + 4)
                    b_values(g3, 0)
                if a1:
                    a1_s(t)
                if a2:
                    a2_scores(g2, 1, 0)
                    if b:
                        pe.wait_ge(s_voa, g3 * G + 1)
                    else:
                        pe.wait_ge(s_vc, g2 + 1)
                    a2_weigh(g2, 0)
                    a2_scores(g2, 1, 1)
                if b:
                    if a2:
                        pe.wait_ge(s_o0, g2 * G + 1)
                    else:
                        pe.wait_ge(s_voa, g3 * G + 1)
                    b_values(g3, 1)
                    pe.wait_ge(s_vov, g3 * G + 1)
                    b_values(g3, 2)
                if a1:
                    a1_o(t)
                if a2:
                    turn_ex(g2, 0, 1)
                if b:
                    b_scores(g3, 1)
                if a2:
                    if b:
                        pe.wait_ge(s_voa, g3 * G + 2)
                    else:
                        pe.wait_ge(s_o0, g2 * G + 1)
                    a2_weigh(g2, 1)
                    a2_scores(g2, 2, 0)
                    a2_scores(g2, 2, 1)
                if b:
                    if a2:
                        pe.wait_ge(s_o0, g2 * G + 2)
                    else:
                        pe.wait_ge(s_voa, g3 * G + 2)
                    b_values(g3, 3)
                    turn_ex(g3, 1, 0)
                if c:
                    if a1:
                        pe.wait_ge(s_h[0], t + 1)
                    elif isinstance(t, int) and t == NG:
                        pe.wait_ge(s_rt, 5 * NG - 4)
                    if not a1 and not first(g4):
                        pe.wait_ge(s_ltc, g4)
                    turn_x(g4, 3, 0)
                if b:
                    pe.wait_ge(s_vov, g3 * G + 2)
                    b_values(g3, 4)
                if c:
                    c_logits(g4)
                if b:
                    pe.wait_ge(s_voa, g3 * G + 3)
                    b_weigh(g3, 0)
                if a2:
                    turn_ex(g2, 0, 2)
                if b:
                    b_scores(g3, 2)
                if a2:
                    if b:
                        pe.wait_ge(s_y, g3 * G + 1)
                    else:
                        pe.wait_ge(s_o0, g2 * G + 2)
                    a2_weigh(g2, 2)
                    a2_scores(g2, 3, 0)
                    a2_scores(g2, 3, 1)
                if a1:
                    if c:
                        pe.wait_ge(s_ltc, g4 + 1)
                    a1_xT2(t)
                if b:
                    if a2:
                        pe.wait_ge(s_o0, g2 * G + 3)
                    else:
                        pe.wait_ge(s_y, g3 * G + 1)
                    b_values(g3, 5)
                    turn_ex(g3, 1, 1)
                    pe.wait_ge(s_vov, g3 * G + 3)
                    b_values(g3, 6)
                if a1:
                    a1_r1(t)
                if b:
                    pe.wait_ge(s_voa, g3 * G + 4)
                    b_weigh(g3, 1)
                if a2:
                    turn_ex(g2, 0, 3)
                if b:
                    pe.wait_ge(s_y, g3 * G + 2)
                    b_values(g3, 7)
                if a1:
                    a1_lg(t)
                if b:
                    b_scores(g3, 3)
                if a2:
                    if b:
                        pe.wait_ge(s_vov, g3 * G + 4)
                    else:
                        pe.wait_ge(s_o0, g2 * G + 3)
                    a2_weigh(g2, 3)
                if b:
                    turn_ex(g3, 1, 2)
                if a2:
                    a2_oT(g2)
                if b:
                    if a2:
                        pe.wait_ge(s_o0, g2 * G + 4)
                    else:
                        pe.wait_ge(s_vov, g3 * G + 4)
                    b_weigh(g3, 2)
                if a2:
                    a2_wo(g2)

            turns(pe, body)

        @block.scalar
        def _(act):
            act.wait_ge(s_wt, 1)
            act.activation(wkT[:, :], psum[0][:, 0:P], ACT.Copy).then_inc(s_wtc, 1)
            act.activation(wqT[:, :], psum[0][:, P:2 * P], ACT.Copy).then_inc(s_wtc, 1)
            for n in range(2):
                act.wait_ge(s_wt, 2 + n)
                act.activation(wvT[:, 4 * n:4 * n + 4, :], psum[1 + n][:, :], ACT.Copy).then_inc(s_wtc, 1)
            act.wait_ge(s_m0, 1)
            act.activation(wkq[:, :], psum[3][:, 0:P], ACT.Copy).then_inc(s_m0c, 1)
            for n in range(2):
                act.wait_ge(s_m0, 2 + n)
                act.activation(wvo[:, 4 * n:4 * n + 4, :], psum[4 + n][:, :], ACT.Copy).then_inc(s_m0c, 1)
            act.wait_ge(s_abs, 1)
            act.activation(decay[:, :], decay[:, :], ACT.Exp, scale=math.log(DECAY)).then_inc(s_dec, 1)
            act.wait_ge(s_in, IN)


            def copy_x(g, i, b):
                act.wait_ge(s_xT[i], g + 1)
                act.activation(xT[i][:, :, :], bank(b), ACT.Copy).then_inc(s_xTc[i], 1)

            def copy_ex(g, i, k):
                act.wait_ge(s_eT[i], g * G + k + 1)
                act.activation(exT[:, 0:4, :], psum[2], ACT.Copy).then_inc(s_eTa[i], 1)

            def a2_copy_qk(g, k):
                act.wait_ge(s_qk, g * G + k + 1)
                act.activation(qk[:, k, :, :], bank(4 + k % 2), ACT.Copy).then_inc(s_qkc, 1)

            def b_copy_q(g, n):
                act.wait_ge(s_q1, g * 8 + n + 1)
                act.activation(qT1[:, n, :], psum[7 - n % 2], ACT.Copy).then_inc(s_q1a, 1)

            def a1_copy_p(t):
                act.wait_ge(s_p, t + 1)
                act.activation(pT[:, :, :], bank(0), ACT.Copy).then_inc(s_pT, 1)

            def a1_copy_v(t):
                act.wait_ge(s_v0, t + 1)
                act.activation(v0[:, :, :], bank(0), ACT.Copy, scale=0.5).then_inc(s_v0c, 1)

            def a1_tanh(t):
                act.wait_ge(s_sd, t + 1)
                act.activation(th[:, :, :], sd[:, :, :], ACT.Tanh, scale=0.5).then_inc(s_th, 1)

            def a1_relu(t):
                act.wait_ge(s_r1, t + 1)
                act.activation(r1[:, :], psum[0][0:32, 0:G], ACT.Relu, bias=rb1[:, :], scale=1.0 / S).then_inc(s_r1c, 1)

            def a2_copy_o(g):
                act.wait_ge(s_oT, g + 1)
                act.activation(oT[:, :, :], bank(4), ACT.Copy).then_inc(s_oTc, 1)

            def c_copy_logits(g):
                act.wait_ge(s_lt, g + 1)
                act.activation(logitsT[:, bass.ds(g * G * S, G * S)], psum[0][0:E, :], ACT.Copy).then_inc(s_ltc, 1)

            def a2_exps(g, k):
                n = g * G + k
                act.wait_ge(s_bias[0], n + 1)
                if k >= 2 or not first(g):
                    act.wait_ge(s_eT[0], n - 1)
                for m in range(HEADS):
                    ins = act.activation(ex[0][:, k % 2, m, :], psum[4 + m // 4][:, (m % 4) * S:(m % 4 + 1) * S], ACT.Exp,
                                         bias=bias[:, 0, k % 2, m:m + 1], scale=1.0 / math.sqrt(DK))
                ins.then_inc(s_ex[0], 1)

            def b_exps(g, k):
                n = g * G + k
                act.wait_ge(s_bias[1], n + 1)
                if k >= 2 or not first(g):
                    act.wait_ge(s_eT[1], n - 1)
                for m in range(HEADS):
                    ins = act.activation(ex[1][:, k % 2, m, :], masked[:, m, :], ACT.Exp, bias=bias[:, 1, k % 2, m:m + 1],
                                         scale=1.0 / math.sqrt(K1), accum_out=den[:, k % 2, m:m + 1])
                ins.then_inc(s_ex[1], 1)

            def b_values(g, n):
                act.wait_ge(s_vo, g * 2 * G + n + 1)
                act.activation(vo[:, n // 2, 0:4, :], bank(1), ACT.Copy).then_inc(s_voa, 1)

            def body(t, a1, a2, b, c, ahead):
                g2, g3, g4 = t - 1, t - 2, t - 3
                if a2:
                    a2_copy_qk(g2, 0)
                    a2_copy_qk(g2, 1)
                if c:
                    copy_ex(g4, 1, 3)
                if a2:
                    a2_copy_qk(g2, 2)
                if a1:
                    copy_x(t, 0, 0)
                if b:
                    copy_x(g3, 2, 6)
                    b_copy_q(g3, 0)
                    b_copy_q(g3, 1)
                if a2:
                    a2_copy_qk(g2, 3)
                if b:
                    b_copy_q(g3, 2)
                    b_copy_q(g3, 3)
                if a2:
                    a2_exps(g2, 0)
                if a1:
                    a1_copy_p(t)
                    a1_copy_v(t)
                if a2:
                    copy_ex(g2, 0, 0)
                if b:
                    b_values(g3, 0)
                if a1:
                    a1_tanh(t)
                if b:
                    b_exps(g3, 0)
                if a2:
                    a2_exps(g2, 1)
                if b:
                    b_values(g3, 2)
                if a2:
                    copy_ex(g2, 0, 1)
                    a2_exps(g2, 2)
                if c:
                    copy_x(g4, 3, 0)
                if b:
                    b_values(g3, 4)
                    copy_ex(g3, 1, 0)
                    b_exps(g3, 1)
                if c:
                    c_copy_logits(g4)
                if a2:
                    copy_ex(g2, 0, 2)
                if b:
                    b_exps(g3, 2)
                if a2:
                    a2_exps(g2, 3)
                if a1:
                    copy_x(t, 1, 0)
                if b:
                    copy_ex(g3, 1, 1)
                    b_values(g3, 6)
                if a1:
                    a1_relu(t)
                if a2:
                    copy_ex(g2, 0, 3)
                if b:
                    copy_ex(g3, 1, 2)
                    b_exps(g3, 3)
                if a2:
                    a2_copy_o(g2)

            turns(act, body)

        @block.vector
        def _(dve):
            dve.wait_ge(s_iota, 1)
            dve.scalar_tensor_tensor(decay[:, :], decay[:, :], -1.0, decay[:, :], ALU.mult, ALU.max).then_inc(s_abs, 1)
            dve.wait_ge(s_in, IN)
            dve.wait_ge(s_dec, 1)
            dve.wait_ge(s_one, 1)

            def ln_stats(g, i, src):
                for k in range(G):
                    dve.bn_stats(stats[:, i, k, :], src(k)).then_inc(s_bn[i], 1)
                for k in range(G):
                    wait_alone(dve, s_bn[i], g * G + k + 1)
                    dve.bn_aggr(mv[:, i, k, :], stats[:, i, k, :]).then_inc(s_mv[i], 1)

            def ln_apply(g, i, src, dst):
                dve.wait_ge(s_rstd[i], g + 1)
                for k in range(G):
                    dve.tensor_scalar(dst(k), src(k), mv[:, i, k, 0:1], rstd[:, i, k:k + 1], ALU.subtract, ALU.mult).then_inc(s_xh[i], 1)

            def add_h(g, i, part):
                dve.tensor_tensor(group(g), group(g), part, ALU.add).then_inc(s_h[i], 1)

            def copy_ex(g, i, k):
                dve.wait_ge(s_eT[i], g * G + k + 1)
                dve.tensor_copy(exT[:, 4:8, :].rearrange("p h s -> p (h s)"), psum[3]).then_inc(s_eTv[i], 1)

            def a1_decay(t):
                dve.wait_ge(s_s0, t + 1)
                dve.tensor_tensor(sd[:, :, :], bank(0), decay[:, :].unsqueeze(1).broadcast_to([P, G, S]), ALU.mult).then_inc(s_sd, 1)

            def a1_silu(t):
                dve.wait_ge(s_th, t + 1)
                dve.scalar_tensor_tensor(act0[:, :, :], th[:, :, :], 1.0, sd[:, :, :], ALU.add, ALU.mult).then_inc(s_act0, 1)

            def a1_route(t):
                dve.wait_ge(s_lg, t + 1)
                dve.tensor_tensor(lg[:, :, :], psum[0][0:1, 0:3 * G].rearrange("p (k c) -> p k c", k=G),
                                  rb2[:, :].unsqueeze(1).broadcast_to([1, G, 3]), ALU.add).then_inc(s_rt, 1)
                dve.wait_ge(s_rt, t * 5 + 1)
                dve.tensor_tensor(c1[:, :], lg[:, :, 1], lg[:, :, 0], ALU.is_gt).then_inc(s_rt, 1)
                dve.tensor_tensor(mx1[:, :], lg[:, :, 1], lg[:, :, 0], ALU.max).then_inc(s_rt, 1)
                dve.wait_ge(s_rt, t * 5 + 3)
                dve.tensor_tensor(c2[:, :], lg[:, :, 2], mx1[:, :], ALU.is_gt).then_inc(s_rt, 2)
                dve.wait_ge(s_rt, t * 5 + 5)
                dve.scalar_tensor_tensor(sel[:, :], c2[:, :], 2.0, c1[:, :], ALU.mult, ALU.max).then_inc(s_sel, 1)

            def a2_max(g, k):
                n = g * G + k
                dve.wait_ge(s_sc[0], n + 1)
                dve.tensor_reduce(smax[:, 0, k % 2, :], psall[:, 4:6, :].rearrange("p b (c s) -> p (b c) s", c=4), AX.X, ALU.max).then_inc(s_mx[0], 1)
                dve.wait_ge(s_mx[0], n + 1)
                dve.tensor_scalar(bias[:, 0, k % 2, :], smax[:, 0, k % 2, :], -1.0 / math.sqrt(DK), None, ALU.mult).then_inc(s_bias[0], 1)

            def a2_norm(g, k):
                n = g * G + k
                av = psum[1][:, 0:HEADS * (DK + 1)].rearrange("p (h c) -> p h c", h=HEADS)
                wait_alone(dve, s_av[0], n + 1)
                dve.reciprocal(rden[:, :], av[:, :, DK]).then_inc(s_rd, 1)
                dve.wait_ge(s_rd, n + 1)
                dve.tensor_tensor(o0[:, k, :].rearrange("p (h c) -> p h c", h=HEADS), av[:, :, 0:DK],
                                  rden[:, :].unsqueeze(2).broadcast_to([P, HEADS, DK]), ALU.mult).then_inc(s_o0, 1)

            def b_values(g, n):
                dve.wait_ge(s_vo, g * 2 * G + n + 1)
                dve.tensor_copy(vo[:, n // 2, 4:8, :].rearrange("p h d -> p (h d)"), psum[1]).then_inc(s_vov, 1)

            def b_mask(g, k):
                n = g * G + k
                if k or not first(g):
                    dve.wait_ge(s_ex[1], n)
                wait_alone(dve, s_sc[1], n + 1)
                for c in range(2):
                    dve.tensor_scalar(masked[:, 4 * c:4 * c + 4, :].rearrange("p h s -> p (h s)"), psum[6 + c], 0.0,
                                      -1e9 * math.sqrt(K1), ALU.is_equal, ALU.mult).then_inc(s_zero, 1)
                for m in range(HEADS):
                    if m % 4 == 0:
                        wait_alone(dve, s_zero, 2 * n + 1 + m // 4)
                    dve.tensor_tensor_reduce(out=masked[:, m, :], in0=psum[6 + m // 4][:, (m % 4) * S:(m % 4 + 1) * S], in1=masked[:, m, :],
                                             scale=1.0, scalar=-3.0e38, op0=ALU.add, op1=ALU.max,
                                             accum_out=smax[:, 1, k % 2, m:m + 1]).then_inc(s_mx[1], 1)
                dve.wait_ge(s_mx[1], HEADS * (n + 1))
                dve.tensor_scalar(bias[:, 1, k % 2, :], smax[:, 1, k % 2, :], -1.0 / math.sqrt(K1), None, ALU.mult).then_inc(s_bias[1], 1)

            def b_den(g, k):
                wait_alone(dve, s_ex[1], g * G + k + 1)
                dve.reciprocal(rden1[:, k % 2, :], den[:, k % 2, :]).then_inc(s_rd1, 1)

            def b_add(g, k):
                dve.wait_ge(s_av[1], g * G + k + 1)
                dve.tensor_tensor(y1[:, k, :], y1[:, k, :], psum[1][:, 0:D], ALU.add).then_inc(s_y, 1)

            def a2_copy_v(g):
                dve.wait_ge(s_v, g + 1)
                dve.tensor_copy(v17[:, :, :, 0:DK], psum[1].rearrange("p (k h c) -> p k h c", k=G, h=HEADS)).then_inc(s_vc, 1)

            def b_copy_k(g, n):
                dve.wait_ge(s_q1, g * 8 + n + 5)
                dve.tensor_copy(kT1[:, n, :], psum[7 - n % 2]).then_inc(s_q1v, 1)

            def a1_add(t):
                dve.wait_ge(s_o, t + 1)
                add_h(t, 0, bank(0))

            def a1_mean(t):
                dve.wait_ge(s_xTc[1], t + 1)
                dve.tensor_reduce(msum[:, :], xT[1][:, :, :], AX.X, ALU.add).then_inc(s_ms, 1)

            def a2_add(g):
                dve.wait_ge(s_wo, g + 1)
                add_h(g, 1, bank(5))

            row = lambda g: lambda k: rows(g, k)
            buf = lambda x: lambda k: x[:, k, :]
            ln_stats(0, 0, row(0))
            ln_apply(0, 0, row(0), buf(xh[0]))

            def body(t, a1, a2, b, c, ahead):
                g2, g3, g4 = t - 1, t - 2, t - 3
                if c:
                    copy_ex(g4, 1, 3)
                if b:
                    wait_alone(dve, s_h[1], g3 + 1)
                    ln_stats(g3, 2, row(g3))
                if c:
                    b_add(g4, 3)
                if b:
                    ln_apply(g3, 2, row(g3), buf(xh[2]))
                if c:
                    wait_alone(dve, s_y, G * (g4 + 1))
                    ln_stats(g4, 4, buf(y1))
                if a2:
                    a2_copy_v(g2)
                    a2_max(g2, 0)
                if b:
                    b_copy_k(g3, 0)
                    b_copy_k(g3, 1)
                    b_copy_k(g3, 2)
                    b_copy_k(g3, 3)
                if c:
                    ln_apply(g4, 4, buf(y1), buf(y2))
                if a2:
                    copy_ex(g2, 0, 0)
                if b:
                    b_mask(g3, 0)
                if a2:
                    a2_norm(g2, 0)
                if a1:
                    a1_decay(t)
                if b:
                    b_values(g3, 1)
                if a2:
                    a2_max(g2, 1)
                if a1:
                    a1_silu(t)
                if c:
                    dve.wait_ge(s_gm, 2 * g4 + 2)
                    add_h(g4, 2, y2[:, :, :])
                if a2:
                    copy_ex(g2, 0, 1)
                if a1:
                    a1_add(t)
                if c:
                    wait_alone(dve, s_h[2], g4 + 1)
                    ln_stats(g4, 3, row(g4))
                if b:
                    b_den(g3, 0)
                    b_mask(g3, 1)
                if a2:
                    a2_norm(g2, 1)
                    a2_max(g2, 2)
                if c:
                    if not first(g4):
                        dve.wait_ge(s_tab, 16 * g4)
                    ln_apply(g4, 3, row(g4), buf(xh[3]))
                if b:
                    b_values(g3, 3)
                if a1:
                    wait_alone(dve, s_h[0], t + 1)
                    ln_stats(t, 1, row(t))
                if b:
                    copy_ex(g3, 1, 0)
                if a1:
                    ln_apply(t, 1, row(t), buf(xh[1]))
                if a2:
                    copy_ex(g2, 0, 2)
                if b:
                    b_den(g3, 1)
                    dve.wait_ge(s_xb, g3 + 1)
                    b_add(g3, 0)
                    b_mask(g3, 2)
                if a2:
                    a2_norm(g2, 2)
                    a2_max(g2, 3)
                if b:
                    b_values(g3, 5)
                    copy_ex(g3, 1, 1)
                if a1:
                    a1_mean(t)
                if b:
                    b_add(g3, 1)
                if a2:
                    copy_ex(g2, 0, 3)
                if b:
                    b_values(g3, 7)
                if a1:
                    a1_route(t)
                if b:
                    b_den(g3, 2)
                    b_mask(g3, 3)
                if a2:
                    a2_norm(g2, 3)
                if ahead:
                    ln_stats(t + 1, 0, row(t + 1))
                if b:
                    copy_ex(g3, 1, 2)
                    b_add(g3, 2)
                    b_den(g3, 3)
                if a2:
                    a2_add(g2)
                if ahead:
                    ln_apply(t + 1, 0, row(t + 1), buf(xh[0]))

            turns(dve, body)


U32 = mybir.dt.uint32
N = B * S
CAP = 1024
F = 512
FC = F // P
CHUNKS = P // E
CW = N // CHUNKS
TILES = CAP // P
PARTS = 5
HB = 4


def experts_stage(nc, used, A, H, ident, psall, table, logitsT, w1, w2, s_weights, WEIGHTS, out):
    psum = [psall[:, i, :] for i in range(8)]
    logits_dram = nc.dram_tensor("logits_dram", (E, N), F32, kind="Internal").ap()
    out_rows = out.rearrange("b s d -> (b s) d")
    with ExitStack() as ctx:
        sb = lambda name, shape, dt=F32: ctx.enter_context(nc.sbuf_tensor(name, shape, dt))
        sem = lambda name: used.append(nc.alloc_semaphore(name)) or used[-1]
        b1rows = sb("b1rows", [E * FC, P]); b1 = sb("b1", [P, E, FC]); b2 = sb("b2", [P, E, D])
        prob = sb("prob", [P, CW]); rowmax = sb("rowmax", [P, 1]); m8 = sb("m8", [1, E]); mrow = sb("mrow", [1, P])
        one1 = sb("one1", [1, 1]); negmax = sb("negmax", [P, 1]); rowsum = sb("rowsum", [P, 1]); rsum = sb("rsum", [P, 1])
        same = sb("same", [P, E, CHUNKS]); before = sb("before", [P, E, CHUNKS])
        cand = sb("cand", [P, 3]); bits = sb("bits", [P, 3], I32); take = sb("take", [P, 2, 4])
        count = sb("count", [P, 3]); hits = sb("hits", [P, 3, CW], BF16)
        above = sb("above", [P, CW]); equal = sb("equal", [P, CW]); rank = sb("rank", [P, CW]); ones = sb("ones", [P, CW])
        need = sb("need", [P, 1]); offs = sb("offs", [P, 1]); picked = sb("picked", [P, CW]); slot = sb("slot", [P, CW])
        sloti = sb("sloti", [P, CW], I32); hii = sb("hii", [P, CW], I32); loi = sb("loi", [P, CW], I32)
        hl = sb("hl", [P, 2, CW])
        turned = sb("turned", [P, 3, E, 2, CHUNKS])
        left = sb("left", [P, 2, E, 2, CHUNKS])
        iota_p = sb("iota_p", [P, P]); iota_t = sb("iota_t", [P, TILES]); chunk = sb("chunk", [P, CHUNKS, 2]); lane = sb("lane", [P, 1])
        parts = sb("parts", [P, E, 2 * CHUNKS, PARTS], BF16)
        hot_t = sb("hot_t", [P, 2 * CHUNKS, TILES], BF16); rhs = sb("rhs", [P, 2, 2 * CHUNKS, PARTS, TILES], BF16)
        hot_p = sb("hot_p", [P, 2, 2 * CHUNKS, P], BF16)
        idhi = sb("idhi", [P, TILES]); idx = sb("idx", [P, E, TILES], U32); vals = sb("vals", [P, E, TILES])
        xg = sb("xg", [P, 3, TILES, D]); xgT = sb("xgT", [P, 2, HB * P]); hT = sb("hT", [P, 2, FC, HB * P])
        y = sb("y", [P, 2, TILES, D])

        s_lo = sem("s3_lo"); s_pr = sem("s3_pr"); s_b = sem("s3_b"); s_c = sem("s3_c"); s_cc = sem("s3_cc")
        s_rm = sem("s3_rm"); s_rmT = sem("s3_rmT"); s_m8 = sem("s3_m8"); s_mr = sem("s3_mr"); s_nm = sem("s3_nm"); s_nmc = sem("s3_nmc")
        s_e = sem("s3_e"); s_sum = sem("s3_sum"); s_rs = sem("s3_rs"); s_p = sem("s3_p")
        s_thr = sem("s3_thr"); s_cand = sem("s3_cand"); s_cnt = sem("s3_cnt"); s_tot = sem("s3_tot"); s_take = sem("s3_take"); s_bit = sem("s3_bit")
        s_sel = sem("s3_sel"); s_g = sem("s3_g"); s_off = sem("s3_off"); s_hl = sem("s3_hl"); s_tn = sem("s3_tn"); s_tnc = sem("s3_tnc")
        s_ht = sem("s3_ht"); s_rhs = sem("s3_rhs"); s_hp = sem("s3_hp"); s_ix = sem("s3_ix"); s_id = sem("s3_id"); s_ixc = sem("s3_ixc"); s_b1 = sem("s3_b1"); s_b1c = sem("s3_b1c")
        s_out0 = sem("s3_out0"); s_ga = [sem(f"s3_ga{i}") for i in range(3)]; s_pt = sem("s3_pt"); s_sp = sem("s3_sp"); s_sc = sem("s3_sc")
        s_xt = sem("s3_xt"); s_xtc = sem("s3_xtc"); s_h1 = sem("s3_h1"); s_h1c = sem("s3_h1c"); s_y = sem("s3_y"); s_yb = sem("s3_yb"); s_yc = sem("s3_yc")
        block = ctx.enter_context(nc.Block())
        BITS = 30
        flat = lambda t: t.rearrange("p a b -> p (a b)")

        @block.sync
        def _(sp):
            sp.dma_start(logits_dram, logitsT[:, :]).then_inc(s_lo, 16)
            sp.dma_start(b1rows[:, :], A["L1_ffn_b1"].rearrange("e (c f) -> (e c) f", f=P)).then_inc(s_b, 16)
            sp.dma_start(b2[:, :, :], A["L1_ffn_b2"].unsqueeze(0).broadcast_to([P, E, D])).then_inc(s_b, 16)
            sp.dma_start(out.rearrange("b s d -> s b d"), H[:, :, :]).then_inc(s_out0, 16)
            sp.wait_ge(s_lo, 16)
            sp.dma_start(prob[:, :], logits_dram.rearrange("e (c f) -> (e c) f", f=CW)).then_inc(s_pr, 16)

        @block.gpsimd
        def _(pool):
            pool.memset(ones[:, :], 1.0).then_inc(s_c, 1)
            pool.memset(flat(same[:, :, :]), 1.0).then_inc(s_cc, 1)
            pool.memset(take[:, 0, 3:4], 0.0).then_inc(s_c, 1)
            for k in range(3):
                pool.memset(bits[:, k:k + 1], (k + 1) << (BITS - 2)).then_inc(s_c, 1)
            pool.memset(one1[:, :], 1.0).then_inc(s_c, 1)
            pool.iota(iota_p[:, :], pattern=[[1, P]], base=0, channel_multiplier=0, allow_small_or_imprecise_dtypes=True).then_inc(s_c, 1)
            pool.iota(iota_t[:, :], pattern=[[1, TILES]], base=0, channel_multiplier=0, allow_small_or_imprecise_dtypes=True).then_inc(s_c, 1)
            pool.iota(chunk[:, :, :], pattern=[[2, CHUNKS], [1, 2]], base=0, channel_multiplier=0, allow_small_or_imprecise_dtypes=True).then_inc(s_c, 1)
            pool.iota(lane[:, :], pattern=[[0, 1]], base=0, channel_multiplier=1, allow_small_or_imprecise_dtypes=True).then_inc(s_c, 1)
            pool.wait_ge(s_cc, 1)
            pool.affine_select(out=same[:, :, :], in_=same[:, :, :], compare_op=ALU.is_ge, fill=0.0, base=0,
                               pattern=[[-CHUNKS, E], [0, CHUNKS]], channel_multiplier=1).then_inc(s_cc, 1)
            pool.wait_ge(s_cc, 2)
            pool.affine_select(out=same[:, :, :], in_=same[:, :, :], compare_op=ALU.is_ge, fill=0.0, base=CHUNKS - 1,
                               pattern=[[CHUNKS, E], [0, CHUNKS]], channel_multiplier=-1).then_inc(s_cc, 1)
            pool.wait_ge(s_cc, 3)
            pool.affine_select(out=flat(before[:, :, :]), in_=flat(same[:, :, :]), compare_op=ALU.is_gt, fill=0.0, base=0,
                               pattern=[[1, P]], channel_multiplier=-1).then_inc(s_cc, 1)

            pool.wait_ge(s_c, 10)
            by = lambda q: parts[:, :, :, q]
            for half in range(2):
                pool.tensor_copy(parts[:, :, half * CHUNKS:(half + 1) * CHUNKS, 0],
                                 chunk[:, :, half].unsqueeze(1).broadcast_to([P, E, CHUNKS])).then_inc(s_sp, 1)
            pool.tensor_copy(by(1), lane[:, :].unsqueeze(2).broadcast_to([P, E, 2 * CHUNKS])).then_inc(s_sp, 1)
            rest = turned[:, 2, :, :, :].rearrange("p e h c -> p e (h c)")
            pool.wait_ge(s_pt, 1)
            for q in range(3):
                pool.tensor_copy(by(2 + q), rest).then_inc(s_sp, 1)
                if q < 2:
                    pool.wait_ge(s_sp, 4 + 2 * q)
                    less = left[:, q, :, :, :].rearrange("p e h c -> p e (h c)")
                    pool.tensor_tensor(less, rest, by(2 + q), ALU.subtract).then_inc(s_sp, 1)
                    pool.wait_ge(s_sp, 5 + 2 * q)
                    rest = less

            def gather(e):
                pool.wait_ge(s_ixc, 2 * e + 2)
                if e >= 3:
                    pool.wait_ge(s_xt, 2 * (e - 2))
                for j in range(TILES):
                    pool.indirect_dma_start(out=xg[:, e % 3, j, :], out_offset=None, in_=table,
                                            in_offset=bass.IndirectOffsetOnAxis(ap=idx[:, e, j:j + 1], axis=0)).then_inc(s_ga[e % 3], 16)

            def scatter(e):
                pool.wait_ge(s_out0, 16)
                if e:
                    pool.wait_ge(s_sc, 16 * TILES * e)
                for j in range(TILES):
                    if j % HB == 0:
                        pool.wait_ge(s_yc, 2 * e + j // HB + 1)
                    pool.indirect_dma_start(out=out_rows, out_offset=bass.IndirectOffsetOnAxis(ap=idx[:, e, j:j + 1], axis=0),
                                            in_=y[:, e % 2, j, :], in_offset=None, compute_op=ALU.add).then_inc(s_sc, 16)

            gather(0)
            gather(1)
            for e in range(E):
                if e + 2 < E:
                    gather(e + 2)
                scatter(e)
            pool.wait_ge(s_sc, 16 * TILES * E)

        @block.tensor
        def _(pe):
            pe.wait_ge(s_b, 32)
            pe.transpose(psum[0][:, 0:E * FC], b1rows[:, :], ident[0:E * FC, 0:E * FC]).then_inc(s_b1, 1)
            pe.wait_ge(s_rm, 1)
            pe.transpose(psum[1][0:1, 0:P], rowmax[:, :], ident[:, :]).then_inc(s_rmT, 1)
            pe.wait_ge(s_mr, 1)
            pe.matmul(psum[2][:, 0:1], mrow[:, :], one1[:, :], start=True, stop=True).then_inc(s_nm, 1)
            pe.wait_ge(s_cc, 4)
            pe.wait_ge(s_e, 1)
            pe.matmul(psum[3][:, 0:1], flat(same[:, :, :]), rowsum[:, :], start=True, stop=True).then_inc(s_sum, 1)
            pe.wait_ge(s_p, 1)
            for half in range(2):
                mm = pe.transpose(psum[7][:, half * P:(half + 1) * P], prob[:, half * P:(half + 1) * P], ident[:, :])
            mm.then_inc(s_tn, 1)
            for i in range(BITS // 2):
                pe.wait_ge(s_cnt, 3 * (i + 1))
                pe.matmul(psum[4][:, 0:3], flat(same[:, :, :]), count[:, :], start=True, stop=True).then_inc(s_tot, 1)
            pe.wait_ge(s_g, 2)
            pe.matmul(psum[5][:, 0:1], flat(same[:, :, :]), count[:, 0:1], start=True, stop=True)
            pe.matmul(psum[5][:, 1:2], flat(before[:, :, :]), count[:, 1:2], start=True, stop=True).then_inc(s_off, 1)
            pe.wait_ge(s_g, 3)
            pe.matmul(psum[6][:, 0:1], flat(before[:, :, :]), count[:, 0:1], start=True, stop=True).then_inc(s_off, 1)
            pe.wait_ge(s_hl, 2)
            for q, t in enumerate((hl[:, 0, :], hl[:, 1, :])):
                for half in range(2):
                    mm = pe.transpose(psum[q][:, half * P:(half + 1) * P], t[:, half * P:(half + 1) * P], ident[:, :])
                mm.then_inc(s_tn, 1)

            def slots(e):
                pe.wait_ge(s_rhs, e + 1)
                if e:
                    pe.wait_ge(s_ixc, 2 * e)
                for c in range(2 * CHUNKS):
                    if c % CHUNKS == 0:
                        pe.wait_ge(s_hp, 2 * e + c // CHUNKS + 1)
                    mm = pe.matmul(psum[7][:, 0:PARTS * TILES], hot_p[:, e % 2, c, :], rhs[:, e % 2, c, :, :],
                                   start=(c == 0), stop=(c == 2 * CHUNKS - 1))
                mm.then_inc(s_ix, 1)

            def turn_x(n):
                e, u = n // 2, n % 2
                pe.wait_ge(s_ga[e % 3], 16 * TILES * (e // 3 + 1))
                if n:
                    pe.wait_ge(s_xtc, n)
                for j in range(HB):
                    mm = pe.transpose(psum[0][:, j * P:(j + 1) * P], xg[:, e % 3, u * HB + j, :], ident[:, :])
                mm.then_inc(s_xt, 1)

            def hidden(n):
                e, u = n // 2, n % 2
                pe.wait_ge(s_xtc, n + 1)
                for c in range(FC):
                    if n:
                        pe.wait_ge(s_h1c, (n - 1) * FC + c + 1)
                    pe.matmul(psum[2 + c][:, :], w1[:, e, c * P:(c + 1) * P], xgT[:, u, :], start=True, stop=True).then_inc(s_h1, 1)

            def outputs(n):
                e, u = n // 2, n % 2
                pe.wait_ge(s_h1c, FC * (n + 1))
                if n >= 2:
                    pe.wait_ge(s_yb, n - 1)
                for j in range(HB):
                    for c in range(FC):
                        mm = pe.matmul(psum[1 + 5 * u][:, j * D:(j + 1) * D], hT[:, u, c, j * P:(j + 1) * P], w2[:, e, c, :],
                                       start=(c == 0), stop=(c == FC - 1))
                mm.then_inc(s_y, 1)

            pe.wait_ge(s_sp, 8)
            slots(0)
            slots(1)
            pe.wait_ge(s_weights, WEIGHTS)
            turn_x(0)
            for e in range(E):
                if e + 2 < E:
                    slots(e + 2)
                hidden(2 * e)
                turn_x(2 * e + 1)
                outputs(2 * e)
                hidden(2 * e + 1)
                if e + 1 < E:
                    turn_x(2 * e + 2)
                outputs(2 * e + 1)

        @block.scalar
        def _(act):
            act.wait_ge(s_b1, 1)
            act.activation(b1[:, :, :].rearrange("p e c -> p (e c)"), psum[0][:, 0:E * FC], ACT.Copy).then_inc(s_b1c, 1)
            act.wait_ge(s_nm, 1)
            act.activation(negmax[:, :], psum[2][:, 0:1], ACT.Copy, scale=-1.0).then_inc(s_nmc, 1)
            act.wait_ge(s_nmc, 1)
            act.wait_ge(s_pr, 16)
            act.activation(prob[:, :], prob[:, :], ACT.Exp, bias=negmax[:, :], accum_out=rowsum[:, :]).then_inc(s_e, 1)
            act.wait_ge(s_b1c, 1)

            def copy_x(n):
                act.wait_ge(s_xt, n + 1)
                act.activation(xgT[:, n % 2, :], psum[0][:, :], ACT.Copy).then_inc(s_xtc, 1)

            copy_x(0)
            for n in range(2 * E):
                if n >= 2:
                    act.wait_ge(s_y, n - 1)
                for c in range(FC):
                    act.wait_ge(s_h1, n * FC + c + 1)
                    act.activation(hT[:, n % 2, c, :], psum[2 + c][:, :], ACT.Gelu, bias=b1[:, n // 2, c:c + 1]).then_inc(s_h1c, 1)
                if n + 1 < 2 * E:
                    copy_x(n + 1)

        @block.vector
        def _(dve):
            dve.wait_ge(s_pr, 16)
            dve.wait_ge(s_c, 10)
            dve.tensor_reduce(rowmax[:, :], prob[:, :], AX.X, ALU.max).then_inc(s_rm, 1)
            dve.wait_ge(s_rmT, 1)
            dve.tensor_reduce(m8[:, :], psum[1][0:1, 0:P].rearrange("p (e c) -> p e c", e=E), AX.X, ALU.max).then_inc(s_m8, 1)
            dve.wait_ge(s_m8, 1)
            dve.tensor_copy(mrow[:, :].rearrange("p (e c) -> p e c", e=E), m8[:, :].unsqueeze(2).broadcast_to([1, E, CHUNKS])).then_inc(s_mr, 1)
            dve.wait_ge(s_sum, 1)
            dve.reciprocal(rsum[:, :], psum[3][:, 0:1]).then_inc(s_rs, 1)
            dve.wait_ge(s_rs, 1)
            dve.tensor_scalar(prob[:, :], prob[:, :], rsum[:, :], None, ALU.mult).then_inc(s_p, 1)
            dve.wait_ge(s_p, 1)
            for i in range(BITS // 2):
                thr = take[:, i % 2, 3:4]
                if i == 1:
                    dve.wait_ge(s_tn, 1)
                    dve.tensor_copy(turned[:, 2, :, :, :].rearrange("p e h c -> p h e c"),
                                    psum[7][:, 0:2 * P].rearrange("p (h e c) -> p h e c", h=2, e=E)).then_inc(s_pt, 1)
                dve.tensor_tensor(cand[:, :].bitcast(I32), thr.bitcast(I32).broadcast_to([P, 3]), bits[:, :], ALU.bitwise_or).then_inc(s_cand, 1)
                dve.wait_ge(s_cand, i + 1)
                for k in range(3):
                    dve.tensor_scalar(hits[:, k, :], prob[:, :], cand[:, k:k + 1], 0.0, ALU.is_ge, ALU.add, accum_out=count[:, k:k + 1]).then_inc(s_cnt, 1)
                dve.tensor_scalar(bits[:, :], bits[:, :], 2, None, ALU.logical_shift_right).then_inc(s_bit, 1)
                dve.wait_ge(s_tot, i + 1)
                dve.scalar_tensor_tensor(take[:, i % 2, 0:3], psum[4][:, 0:3], CAP - 0.5, cand[:, :], ALU.is_ge, ALU.mult).then_inc(s_take, 1)
                dve.wait_ge(s_take, i + 1)
                dve.wait_ge(s_bit, i + 1)
                dve.tensor_reduce(take[:, (i + 1) % 2, 3:4], take[:, i % 2, :], AX.X, ALU.max).then_inc(s_thr, 1)
                dve.wait_ge(s_thr, i + 1)
            thr = take[:, (BITS // 2) % 2, 3:4]
            dve.tensor_scalar(above[:, :], prob[:, :], thr, 0.0, ALU.is_gt, ALU.add, accum_out=count[:, 0:1]).then_inc(s_g, 1)
            dve.tensor_scalar(equal[:, :], prob[:, :], thr, 0.0, ALU.is_equal, ALU.add, accum_out=count[:, 1:2]).then_inc(s_g, 1)
            dve.wait_ge(s_g, 2)
            dve.tensor_tensor_scan(rank[:, :], ones[:, :], equal[:, :], 0.0, ALU.mult, ALU.add).then_inc(s_sel, 1)
            dve.wait_ge(s_off, 1)
            dve.tensor_scalar(offs[:, :], psum[5][:, 0:1], -1.0, float(CAP), ALU.mult, ALU.add).then_inc(s_sel, 1)
            dve.wait_ge(s_sel, 2)
            dve.tensor_tensor(need[:, :], offs[:, :], psum[5][:, 1:2], ALU.subtract).then_inc(s_sel, 1)
            dve.wait_ge(s_sel, 3)
            dve.scalar_tensor_tensor(picked[:, :], rank[:, :], need[:, :], equal[:, :], ALU.is_le, ALU.mult).then_inc(s_sel, 1)
            dve.wait_ge(s_sel, 4)
            dve.tensor_tensor(picked[:, :], picked[:, :], above[:, :], ALU.add).then_inc(s_sel, 1)
            dve.wait_ge(s_sel, 5)
            dve.tensor_tensor_scan(rank[:, :], ones[:, :], picked[:, :], 0.0, ALU.mult, ALU.add).then_inc(s_sel, 1)
            dve.wait_ge(s_sel, 6)
            dve.tensor_copy(count[:, 0:1], rank[:, CW - 1:CW]).then_inc(s_g, 1)
            dve.wait_ge(s_off, 2)
            dve.scalar_tensor_tensor(slot[:, :], rank[:, :], psum[6][:, 0:1], picked[:, :], ALU.add, ALU.mult).then_inc(s_sel, 1)
            dve.wait_ge(s_sel, 7)
            dve.tensor_scalar(sloti[:, :], slot[:, :], -1.0, None, ALU.add).then_inc(s_sel, 1)
            dve.wait_ge(s_sel, 8)
            dve.tensor_scalar(hii[:, :], sloti[:, :], 3, None, ALU.arith_shift_right).then_inc(s_sel, 1)
            dve.tensor_scalar(loi[:, :], sloti[:, :], TILES - 1, None, ALU.bitwise_and).then_inc(s_sel, 1)
            dve.wait_ge(s_sel, 10)
            dve.tensor_copy(hl[:, 0, :], hii[:, :]).then_inc(s_hl, 1)
            dve.tensor_copy(hl[:, 1, :], loi[:, :]).then_inc(s_hl, 1)
            for q in range(2):
                dve.wait_ge(s_tn, q + 2)
                dve.tensor_copy(turned[:, q, :, :, :].rearrange("p e h c -> p h e c"),
                                psum[q][:, 0:2 * P].rearrange("p (h e c) -> p h e c", h=2, e=E)).then_inc(s_tnc, 1)
            dve.wait_ge(s_tnc, 2)
            dve.wait_ge(s_sp, 8)

            def hots(e):
                of = lambda q: turned[:, q, e, :, :].rearrange("p h c -> p (h c)")
                if e >= 2:
                    dve.wait_ge(s_ix, e - 1)
                if e:
                    dve.wait_ge(s_rhs, e)
                dve.tensor_tensor(hot_t[:, :, :], of(1).unsqueeze(2).broadcast_to([P, 2 * CHUNKS, TILES]),
                                  iota_t[:, :].unsqueeze(1).broadcast_to([P, 2 * CHUNKS, TILES]), ALU.is_equal).then_inc(s_ht, 1)
                dve.wait_ge(s_ht, e + 1)
                dve.tensor_tensor(rhs[:, e % 2, :, :, :], hot_t[:, :, :].unsqueeze(2).broadcast_to([P, 2 * CHUNKS, PARTS, TILES]),
                                  parts[:, e, :, :].unsqueeze(3).broadcast_to([P, 2 * CHUNKS, PARTS, TILES]), ALU.mult).then_inc(s_rhs, 1)
                for half in range(2):
                    k = slice(half * CHUNKS, (half + 1) * CHUNKS)
                    dve.tensor_tensor(hot_p[:, e % 2, k, :], of(0)[:, k].unsqueeze(2).broadcast_to([P, CHUNKS, P]),
                                      iota_p[:, :].unsqueeze(1).broadcast_to([P, CHUNKS, P]), ALU.is_equal).then_inc(s_hp, 1)

            def told(e):
                dve.wait_ge(s_ix, e + 1)
                dve.tensor_scalar(idhi[:, :], psum[7][:, 0:TILES], float(P), None, ALU.mult).then_inc(s_id, 1)
                dve.tensor_reduce(vals[:, e, :], psum[7][:, 2 * TILES:PARTS * TILES].rearrange("p (q t) -> p t q", t=TILES), AX.X, ALU.add).then_inc(s_ixc, 1)
                dve.wait_ge(s_id, e + 1)
                dve.tensor_tensor(idx[:, e, :], idhi[:, :], psum[7][:, TILES:2 * TILES], ALU.add).then_inc(s_ixc, 1)

            def weighted(n):
                e, u = n // 2, n % 2
                dve.wait_ge(s_y, n + 1)
                if e >= 2:
                    dve.wait_ge(s_sc, 16 * TILES * (e - 1))
                part = y[:, e % 2, u * HB:(u + 1) * HB, :]
                dve.tensor_tensor(part, psum[1 + 5 * u][:, :].rearrange("p (j d) -> p j d", j=HB), b2[:, e:e + 1, :].broadcast_to([P, HB, D]),
                                  ALU.add).then_inc(s_yb, 1)
                dve.wait_ge(s_yb, n + 1)
                dve.tensor_tensor(part, part, vals[:, e, u * HB:(u + 1) * HB].unsqueeze(2).broadcast_to([P, HB, D]), ALU.mult).then_inc(s_yc, 1)

            hots(0)
            hots(1)
            told(0)
            hots(2)
            told(1)
            for e in range(E):
                if e + 2 < E:
                    told(e + 2)
                weighted(2 * e)
                if e + 3 < E:
                    hots(e + 3)
                weighted(2 * e + 1)


def tower_kernel(nc, A, out):
    table = nc.dram_tensor("token_table", (N, D), F32, kind="Internal").ap()
    with ExitStack() as ctx:
        sb = lambda name, shape, dt=F32: ctx.enter_context(nc.sbuf_tensor(name, shape, dt))
        psall = ctx.enter_context(nc.psum_tensor("banks", [P, 8, 512], F32))
        H = sb("H", [P, B, D])
        ident = sb("ident", [P, P])

        def fresh():
            nc.clear_and_free_semaphores(used)
            nc.all_engine_barrier()
            used.clear()

        used = []
        alignment_stage(nc, used, A, H, ident, [psall[:, i, :] for i in range(8)])
        fresh()
        logitsT = sb("logitsT", [E, N])
        w1 = sb("w1", [P, E, F])
        w2 = sb("w2", [P, E, FC, D])
        s_weights = ctx.enter_context(nc.semaphore("s_weights"))
        layers_stage(nc, used, A, H, ident, psall, table, logitsT, w1, w2, s_weights)
        fresh()
        experts_stage(nc, used, A, H, ident, psall, table, logitsT, w1, w2, s_weights, 16 * (1 + E), out)


_OUT = (B, S, D)


def kernel(**inputs):
    import numpy as _np
    import concourse.bacc as _bacc
    from concourse import mybir as _mybir
    from concourse.bass_utils import run_bass_kernel_spmd as _run

    nc = _bacc.Bacc("TRN2", target_bir_lowering=False, num_devices=1)
    arrays, A = {}, {}
    for name, value in inputs.items():
        a = _np.ascontiguousarray(value)
        arrays[f"in_{name}"] = a
        A[name] = nc.dram_tensor(f"in_{name}", a.shape, _mybir.dt.from_np(a.dtype), kind="ExternalInput").ap()
    out = nc.dram_tensor("out_h", _OUT, F32, kind="ExternalOutput").ap()
    tower_kernel(nc, A, out)
    r = _run(nc, [arrays], core_ids=[0])
    return r.results[0]["out_h"]
```

```python
import math
from contextlib import ExitStack

import concourse.bass as bass
from concourse import mybir

F32 = mybir.dt.float32
I32 = mybir.dt.int32
BF16 = mybir.dt.bfloat16
ALU = mybir.AluOpType
ACT = mybir.ActivationFunctionType
AX = mybir.AxisListType

B, S, D = 32, 128, 128
P = 128
V = 22
VP = 32
V3 = 3 * VP
G = 4
NG = B // G
HALF = S // 2
CH = 16
NCH = S // CH

HEADS = 8
DK = D // HEADS
KV_HEADS = (8, 4, 1)
PADK = 32
K1 = 64
E = 8
DECAY = 0.96875
WQ, WK, WV, WO, WALL = 0, HEADS * PADK, 2 * HEADS * PADK, 2 * HEADS * PADK + D, 2 * HEADS * PADK + 2 * D
WEIGHT_SHAPES = {"decay": [P, P], "wkq": [P, P], "wv0": [P, P], "wvo": [P, HEADS, D], "variants": [P, 3, WALL],
                 "wq1": [P, HEADS * K1], "wk1": [P, HEADS * K1], "rw1": [P, 32], "rb1": [32, 1], "rw2": [32, 3], "rb2": [1, 3],
                 "wr": [P, E], "bo": [P, D], "gamma": [P, D], "beta": [P, D]}


def alignment_stage(nc, used, A, H, ident, psum, W):
    w_dram = nc.dram_tensor("w_dram", (2, B, S, S), F32, kind="Internal").ap()
    r_dram = nc.dram_tensor("r_dram", (2, 2 * B, S, HALF), F32, kind="Internal").ap()
    with ExitStack() as ctx:
        sb = lambda name, shape, dt=F32: ctx.enter_context(nc.sbuf_tensor(name, shape, dt))
        sem = lambda name: used.append(nc.alloc_semaphore(name)) or used[-1]
        onehot_x = sb("onehot_x", [P, 2, B * S], BF16)
        onehot_y = sb("onehot_y", [VP, B * S], BF16)
        letter = sb("letter", [V3, 1]); row = sb("row", [V3, 1], I32); block_row = sb("block_row", [V3, 1], I32)
        emb = sb("emb", [V, P])
        wproj = sb("wproj", [P, P])
        bproj = sb("bproj", [P, 1])
        wgap = sb("wgap", [P, 2])
        bgap = sb("bgap", [V, 1])
        embT = sb("embT", [P, V])
        zT = sb("zT", [P, V])
        pair = sb("pair", [V, 3, V])
        pair3 = sb("pair3", [VP, 3, VP], BF16)
        gap = sb("gap", [V, 2])
        gapcol = sb("gapcol", [V, 2, P])
        counts = sb("counts", [V, 2, 4, B])
        gapscore = sb("gapscore", [P, B])
        crow = sb("crow", [P, 1])
        pairY = sb("pairY", [V3, B * S], BF16)
        theta = sb("theta", [P, B, S])
        w_rows = sb("w_rows", [P, 2, B, S])
        w_dp = sb("w_dp", [P, S + 2, HALF])
        tok = w_dp[0:V3, 0:S, :].rearrange("v i j -> v (i j)").bitcast(I32).rearrange("v (k t) -> v k t", k=2)
        hist = sb("hist", [P, S + 2, HALF + 1])
        R = sb("R", [P, HALF])
        bb = sb("bb", [P, HALF])
        aa = sb("aa", [P, HALF])
        rH = sb("rH", [P, 2, HALF])
        xx = sb("xx", [P, HALF])
        gg = sb("gg", [P, 2, HALF])
        qq = sb("qq", [P, HALF])
        ratios = w_rows
        tri = sb("tri", [P, 2, P])
        th1 = sb("th1", [B, S])
        bfin = sb("bfin", [P, HALF])
        last = sb("last", [B, S])
        ones_bs = sb("ones_bs", [B, S])
        path1 = sb("path1", [B, S])
        lnlast = sb("lnlast", [B, S])

        s_tok = [sem(f"s_tok{k}") for k in range(2)]; s_split = sem("s_split"); s_let = sem("s_let"); s_back = sem("s_back"); s_rev = sem("s_rev"); s_pre = sem("s_pre"); s_var0 = sem("s_var0"); s_abs = sem("s_abs")
        s_wt = sem("s_wt"); s_wtc = sem("s_wtc"); s_m0 = sem("s_m0"); s_m0c = sem("s_m0c"); s_y3 = sem("s_y3"); s_w = sem("s_w"); s_const = sem("s_const"); s_pc = sem("s_pc")
        s_embT = sem("s_embT"); s_embTc = sem("s_embTc"); s_z = sem("s_z"); s_zc = sem("s_zc")
        s_pair = sem("s_pair"); s_pairc = sem("s_pairc"); s_gc = sem("s_gc")
        s_hot = sem("s_hot"); s_one = sem("s_one"); s_cnt = sem("s_cnt"); s_A = sem("s_A"); s_Ac = sem("s_Ac")
        s_c = sem("s_c")
        s_y = sem("s_y"); s_yc = sem("s_yc"); s_yA = sem("s_yA")
        s_th = sem("s_th"); s_exp = sem("s_exp"); s_thc = sem("s_thc")
        s_wdp = [sem(f"s_wdp{q}") for q in range(NCH)]
        s_wst = sem("s_wst"); s_wst2 = sem("s_wst2")
        s_rst = [sem(f"s_rst{q}") for q in range(NCH)]
        s_dve = sem("s_dve"); s_b = sem("s_b"); s_a = sem("s_a"); s_rh = sem("s_rh"); s_r = sem("s_r"); s_x = sem("s_x"); s_g = sem("s_g"); s_q = sem("s_q"); s_scan = sem("s_scan"); s_hand = sem("s_hand")
        s_rat = [sem(f"s_rathalf{q}") for q in range(2)]
        s_rat0 = sem("s_rat0"); s_th1 = sem("s_th1"); s_bf = sem("s_bf"); s_last = sem("s_last"); s_lnl = sem("s_lnl")
        s_p1 = sem("s_p1"); s_row1 = [sem(f"s_row1{q}") for q in range(NG // 2)]; s_ln = sem("s_ln"); s_D = sem("s_D"); s_dd = sem("s_dd"); s_h = sem("s_h")
        s_dch = sem("s_dch")
        block = ctx.enter_context(nc.Block())
        spare = onehot_x[:, :, :].rearrange("p k t -> p (k t)").bitcast(F32)
        wv1, wo1, wvT = (spare[:, i * HEADS * D:(i + 1) * HEADS * D].rearrange("p (h n) -> p h n", h=HEADS) for i in range(3))
        wq0, wk0, wqT, wkT = (spare[:, (24 + i) * P:(25 + i) * P] for i in range(4))
        decay, wkq, wvo, variants = W["decay"], W["wkq"], W["wvo"], W["variants"]
        PRE = 16 * (15 + 3 * 2 + 2 * sum(HEADS // n for n in KV_HEADS))

        def load_weights(sp):
            sp.dma_start(wq0, A["L0_attn_W_Q"]).then_inc(s_pre, 16)
            sp.dma_start(wk0, A["L0_attn_W_K"]).then_inc(s_pre, 16)
            sp.dma_start(wv1, A["L1_attn_Wv"].rearrange("d (h n) -> d h n", h=HEADS)).then_inc(s_pre, 16)
            sp.dma_start(wo1, A["L1_attn_Wo"].rearrange("(h p) n -> p h n", h=HEADS)).then_inc(s_pre, 16)
            for name, src in (("wv0", A["L0_attn_W_V"]), ("wq1", A["L1_attn_Wq"]), ("wk1", A["L1_attn_Wk"]), ("rw1", A["L0_ffn_r_w1"]),
                              ("rb1", A["L0_ffn_r_b1"].unsqueeze(1)), ("rw2", A["L0_ffn_r_w2"]), ("rb2", A["L0_ffn_r_b2"].unsqueeze(0)),
                              ("wr", A["L1_ffn_Wr"])):
                sp.dma_start(W[name][:, :], src).then_inc(s_pre, 16)
            for name in ("bo", "gamma", "beta"):
                sp.dma_start(W[name][:, :], A["L1_attn_" + name].unsqueeze(0).broadcast_to([P, D])).then_inc(s_pre, 16)
            sp.wait_ge(s_var0, 1)
            with nc.allow_non_contiguous_dma("a head's columns, set apart"):
                for i, n in enumerate(KV_HEADS):
                    padded = lambda c: variants[:, i, c:c + HEADS * PADK].rearrange("p (h c) -> p h c", c=PADK)[:, :, 0:DK]
                    sp.dma_start(padded(WQ), A[f"L0_ffn_wq{i}"].rearrange("p (h c) -> p h c", c=DK)).then_inc(s_pre, 16)
                    for r in range(HEADS // n):
                        for c, name in ((WK, "wk"), (WV, "wv")):
                            src = A[f"L0_ffn_{name}{i}"].rearrange("p (h c) -> p h c", c=DK)
                            dst = padded(WK) if c == WK else variants[:, i, WV:WV + D].rearrange("p (h c) -> p h c", c=DK)
                            sp.dma_start(dst[:, r::HEADS // n, :], src).then_inc(s_pre, 16)
                    sp.dma_start(variants[:, i, WO:WALL], A[f"L0_ffn_wo{i}"]).then_inc(s_pre, 16)

        tokens = (A["x"], A["itok_BS_0_21"])

        @block.sync
        def _(sp):
            for k, rows in ((1, VP), (0, V3)):
                src = tokens[k].rearrange("b s -> (b s)").unsqueeze(0).broadcast_to([rows, B * S])
                sp.dma_start(tok[0:rows, k, :], src).then_inc(s_tok[k], 16)
            def store(n, rows, signal):
                m, d = 2 * (n // 2), n % 2
                sp.dma_start(w_dram[d, m * G:(m + 2) * G, rows, :].rearrange("b i j -> i b j"), w_rows[rows, d, m * G:(m + 2) * G, :]).then_inc(signal, 16)

            def load(q):
                for half in range(2):
                    r0 = 1 + q * CH + half
                    sp.dma_start(w_dp[half * 64:half * 64 + 64, r0:r0 + CH, :],
                                 w_dram[:, :, q * CH:(q + 1) * CH, half * HALF:(half + 1) * HALF].rearrange("d b i j -> (d b) i j")).then_inc(s_wdp[q], 16)

            for n in range(NG):
                sp.wait_ge(s_exp, 4 * (n // 2) + 3 + n % 2)
                store(n, slice(0, 2 * CH), s_wst)
            sp.wait_ge(s_wst, 16 * NG)
            load(0)
            load(1)
            for n in range(NG):
                store(n, slice(2 * CH, S), s_wst2)
            sp.wait_ge(s_wst2, 16 * NG)
            for q in range(2, NCH):
                load(q)
            sp.wait_ge(s_th, 2 * NG)
            load_weights(sp)
            sp.wait_ge(s_thc, NG)
            sp.dma_start(th1[:, :], theta[0:1, :, :]).then_inc(s_th1, 16)
            for d in range(2):
                sp.dma_start(ratios[0:1, d, :, :], ones_bs[:, :]).then_inc(s_rat0, 16)
            for q in range(NCH + 1):
                for half in range(2):
                    if q < NCH:
                        lo = q * CH + (q == 0)
                        sp.wait_ge(s_scan, (q + 1) * CH + half)
                        src = hist[half * 64:half * 64 + 64, 1 + lo + half:1 + (q + 1) * CH + half, 1:]
                        sp.dma_start(r_dram[half, :, lo:(q + 1) * CH, :], src).then_inc(s_rst[q], 16)
                    if q == NCH - 1:
                        sp.wait_ge(s_bf, 1 + half)
                        sp.dma_start(last[:, half * HALF:(half + 1) * HALF], bfin[half * 64 + 32:half * 64 + 64, :]).then_inc(s_last, 16)
                if q:
                    lo = (q - 1) * CH + (q == 1)
                    sp.wait_ge(s_rst[q - 1], 32)
                    for half in range(2):
                        dst = ratios[lo:q * CH, :, :, half * HALF:(half + 1) * HALF].rearrange("i d b j -> i (d b) j")
                        sp.dma_start(dst, r_dram[half, :, lo:q * CH, :].rearrange("p i j -> i p j")).then_inc(s_rat[half], 16)
            sp.wait_ge(s_p1, 1)
            for m in range(0, NG, 2):
                sp.wait_ge(s_ln, m // 2 + 1)
                sp.dma_start(ratios[0:1, 0, m * G:(m + 2) * G, :], path1[m * G:(m + 2) * G, :]).then_inc(s_row1[m // 2], 16)

        @block.gpsimd
        def _(pool):
            pool.dma_start(emb[:, :], A["L0_tok_W_embed"]).then_inc(s_w, 16)
            pool.dma_start(wproj[:, :], A["L0_tok_W_proj"]).then_inc(s_w, 16)
            pool.dma_start(bproj[:, :], A["L0_tok_b_proj"].unsqueeze(1)).then_inc(s_w, 16)
            with nc.allow_non_contiguous_dma("two short columns"):
                pool.dma_start(wgap[:, :], A["L0_tok_W_gap"].rearrange("(k p) -> p k", k=2)).then_inc(s_w, 16)
            pool.dma_start(bgap[:, :], A["L0_tok_b_gap"].unsqueeze(1).broadcast_to([V, 1])).then_inc(s_w, 16)
            pool.memset(ident[:, :], 0.0).then_inc(s_pc, 1)
            pool.iota(row[:, :], pattern=[[0, 1]], base=0, channel_multiplier=1).then_inc(s_const, 1)
            pool.memset(pair3[:, :, :], 0.0).then_inc(s_const, 1)
            pool.iota(decay[:, :], pattern=[[1, P]], base=0, channel_multiplier=-1, allow_small_or_imprecise_dtypes=True).then_inc(s_const, 1)
            pool.memset(R[:, :], 1.0).then_inc(s_const, 1)
            pool.memset(ones_bs[:, :], 1.0).then_inc(s_const, 1)
            pool.memset(hist[:, :, 0:1], 0.0).then_inc(s_const, 1)
            pool.memset(tri[:, :, :], 0.0).then_inc(s_pc, 1)
            pool.wait_ge(s_pc, 1)
            pool.affine_select(out=ident[:, :], in_=ident[:, :], compare_op=ALU.not_equal, fill=1.0, base=0,
                               pattern=[[-1, P]], channel_multiplier=1).then_inc(s_const, 1)
            pool.wait_ge(s_pc, 2)
            pool.affine_select(out=tri[:, 0, :], in_=tri[:, 0, :], compare_op=ALU.is_gt, fill=1.0, base=0,
                               pattern=[[-1, P]], channel_multiplier=1).then_inc(s_const, 1)
            pool.affine_select(out=tri[:, 1, :], in_=tri[:, 1, :], compare_op=ALU.is_gt, fill=-1.0, base=P,
                               pattern=[[-1, P]], channel_multiplier=-1).then_inc(s_const, 1)
            pool.memset(variants[:, :, :], 0.0).then_inc(s_var0, 1)
            pool.wait_ge(s_hot, 2)
            pool.tensor_copy(onehot_x[0:V3, 1, :].rearrange("v (b s) -> v b s", b=B),
                             onehot_x[0:V3, 0, :].rearrange("v (b s) -> v b s", b=B)[:, :, ::-1]).then_inc(s_rev, 1)
            pool.wait_ge(s_dve, 5)
            pool.tensor_tensor(qq[:, :], w_dp[:, 4, :], R[:, :], ALU.mult).then_inc(s_q, 3)
            for s in range(3, S + 2):
                p = slice(0 if s <= S else 64, P)
                pn = slice(0 if s < S else 64, P)
                if s <= S:
                    pool.wait_ge(s_q, s)
                pool.wait_ge(s_scan, s)
                if s <= S:
                    pool.tensor_tensor(gg[pn, (s + 1) % 2, :], qq[pn, :], hist[pn, s, 0:HALF], ALU.mult).then_inc(s_g, 4 if s == 3 else 1)
                if s == S:
                    pool.wait_ge(s_g, S + 1)
                if s > 3:
                    pool.wait_ge(s_r, s - 1)
                pool.tensor_tensor(xx[p, :], R[p, :], hist[p, s, 0:HALF], ALU.mult).then_inc(s_x, 3 if s == 3 else 1)
                pool.wait_ge(s_x, s)
                pool.wait_ge(s_rh, s)
                pool.tensor_tensor(R[p, :], xx[p, :], rH[p, (s + 1) % 2, :], ALU.mult).then_inc(s_r, 3 if s == 3 else 1)
                pool.wait_ge(s_r, s)
                if s < S:
                    pq = slice(0 if s + 2 <= S else 64, P)
                    if (s + 1) % CH == 0 and s + 1 < S:
                        pool.wait_ge(s_wdp[(s + 1) // CH], 32)
                    pool.tensor_tensor(qq[pq, :], w_dp[pq, s + 2, :], R[pq, :], ALU.mult).then_inc(s_q, 1)
                elif s == S:
                    pool.tensor_tensor(bfin[0:64, :], w_dp[0:64, S, :], R[0:64, :], ALU.mult).then_inc(s_bf, 1)
                    pool.wait_ge(s_bf, 1)
                else:
                    pool.tensor_tensor(bfin[64:128, :], w_dp[64:128, S + 1, :], R[64:128, :], ALU.mult).then_inc(s_bf, 1)

        @block.tensor
        def _(pe):
            pe.wait_ge(s_w, 80)
            pe.wait_ge(s_const, 7)
            pe.transpose(psum[0][:, 0:V], emb[:, :], ident[0:V, 0:V]).then_inc(s_embT, 1)
            pe.wait_ge(s_embTc, 1)
            pe.matmul(psum[1][:, 0:V], wproj[:, :], embT[:, :], start=True, stop=True).then_inc(s_z, 1)
            pe.wait_ge(s_zc, 1)
            pe.matmul(psum[2][0:V, 0:V], zT[:, :], zT[:, :], start=True, stop=True).then_inc(s_pair, 1)
            pe.matmul(psum[3][0:V, 0:2], zT[:, :], wgap[:, :], start=True, stop=True).then_inc(s_pair, 1)
            pe.wait_ge(s_split, 3)
            pe.wait_ge(s_hot, 1)
            for m in range(NG):
                bank = psum[4 + m % 4]
                if m >= 4:
                    pe.wait_ge(s_yc, m - 3)
                pe.matmul(bank[0:V3, :], pair3[:, :, :], onehot_y[:, m * 512:(m + 1) * 512], start=True, stop=True).then_inc(s_y, 1)
            pe.wait_ge(s_gc, 4)
            pe.wait_ge(s_cnt, 2)
            pe.matmul(psum[0][:, 0:B], gapcol[:, 0, :], counts[:, 0, 0, :], start=True, stop=False)
            pe.matmul(psum[0][:, 0:B], gapcol[:, 1, :], counts[:, 1, 0, :], start=False, stop=True).then_inc(s_A, 1)
            pe.matmul(psum[1][:, 0:1], counts[:, 0, :, :].rearrange("v r b -> v (r b)"), gap[:, 0:1], start=True, stop=False)
            pe.matmul(psum[1][:, 0:1], counts[:, 1, :, :].rearrange("v r b -> v (r b)"), gap[:, 1:2], start=False, stop=True).then_inc(s_A, 1)
            pe.wait_ge(s_yc, NG)
            pe.wait_ge(s_rev, 1)
            pe.wait_ge(s_c, 1)
            pe.wait_ge(s_Ac, 1)
            for m in range(NG):
                for d in range(2):
                    n = 2 * m + d
                    bank = psum[n % 8]
                    if n >= 8:
                        pe.wait_ge(s_exp, n - 7)
                    if d == 0 and m >= 4:
                        pe.wait_ge(s_thc, m - 3)
                    for k in range(G):
                        b = m * G + k
                        X = onehot_x[0:V3, d, b * S:(b + 1) * S]
                        Y = pairY[:, b * S:(b + 1) * S]
                        if d:
                            Y = Y[:, ::-1]
                        mm = pe.matmul(bank[:, k * S:(k + 1) * S], X, Y, start=True, stop=True)
                    mm.then_inc(s_th, 1)
            pe.wait_ge(s_exp, 2 * NG)
            pe.wait_ge(s_thc, NG)
            pe.wait_ge(s_pre, PRE)
            pe.transpose(psum[0][:, 0:P], wk0, ident[:, :])
            pe.transpose(psum[0][:, P:2 * P], wq0, ident[:, :]).then_inc(s_wt, 1)
            for n in range(2):
                for h in range(4):
                    mm = pe.transpose(psum[1 + n][:, h * P:(h + 1) * P], wv1[:, 4 * n + h, :], ident[:, :])
                mm.then_inc(s_wt, 1)
            pe.wait_ge(s_wtc, 4)
            pe.matmul(psum[3][:, 0:P], wkT, wqT, start=True, stop=True).then_inc(s_m0, 1)
            for n in range(2):
                for h in range(4):
                    mm = pe.matmul(psum[4 + n][:, h * P:(h + 1) * P], wvT[:, 4 * n + h, :], wo1[:, 4 * n + h, :], start=True, stop=True)
                mm.then_inc(s_m0, 1)
            pe.wait_ge(s_m0c, 3)
            for m in range(NG):
                pe.wait_ge(s_row1[m // 2], 16)
                pe.wait_ge(s_ln, m // 2 + 1)
                pe.matmul(psum[m][:, :], tri[:, 0, :], ratios[:, 0, m * G:(m + 1) * G, :], start=True, stop=False)
                pe.matmul(psum[m][:, :], tri[:, 1, :], ratios[:, 1, m * G:(m + 1) * G, ::-1], start=False, stop=True).then_inc(s_D, 1)

        @block.scalar
        def _(act):
            act.wait_ge(s_embT, 1)
            act.activation(embT[:, :], psum[0][:, 0:V], ACT.Copy).then_inc(s_embTc, 1)
            act.wait_ge(s_z, 1)
            act.activation(zT[:, :], psum[1][:, 0:V], ACT.Identity, bias=bproj[:, :]).then_inc(s_zc, 1)
            for m in range(NG):
                act.wait_ge(s_y, m + 1)
                act.activation(pairY[:, m * 512:(m + 1) * 512], psum[4 + m % 4][0:V3, :], ACT.Copy).then_inc(s_yc, 1)
            act.wait_ge(s_A, 2)
            act.activation(crow[:, :], psum[1][:, 0:1], ACT.Exp, scale=-1.0).then_inc(s_c, 1)
            act.wait_ge(s_abs, 1)
            act.activation(decay[:, :], decay[:, :], ACT.Exp, scale=math.log(DECAY)).then_inc(s_abs, 1)
            for n in range(2 * NG):
                group = slice((n // 2) * G, (n // 2 + 1) * G)
                if n % 2 == 0:
                    act.wait_ge(s_thc, n // 2 + 1)
                    act.activation(w_rows[:, 0, group, :], theta[:, group, :], ACT.Exp).then_inc(s_exp, 1)
                else:
                    act.wait_ge(s_back, n // 2 + 1)
                    act.activation(w_rows[:, 1, group, :], w_rows[:, 1, group, :], ACT.Exp).then_inc(s_exp, 1)
            for s in range(3, S + 2):
                act.wait_ge(s_scan, s - 1)
                act.activation(hist[64:128, s, 0:1], hist[0:64, s - 1, HALF:HALF + 1], ACT.Copy).then_inc(s_hand, 3 if s == 3 else 1)
                if s == 60:
                    act.wait_ge(s_wt, 1)
                    act.activation(wkT, psum[0][:, 0:P], ACT.Copy).then_inc(s_wtc, 1)
                    act.activation(wqT, psum[0][:, P:2 * P], ACT.Copy).then_inc(s_wtc, 1)
                if s in (63, 66):
                    n = (s - 63) // 3
                    act.wait_ge(s_wt, 2 + n)
                    act.activation(wvT[:, 4 * n:4 * n + 4, :], psum[1 + n][:, :], ACT.Copy).then_inc(s_wtc, 1)
                if s == 80:
                    act.wait_ge(s_m0, 1)
                    act.activation(wkq[:, :], psum[3][:, 0:P], ACT.Copy).then_inc(s_m0c, 1)
                if s in (83, 86):
                    n = (s - 83) // 3
                    act.wait_ge(s_m0, 2 + n)
                    act.activation(wvo[:, 4 * n:4 * n + 4, :], psum[4 + n][:, :], ACT.Copy).then_inc(s_m0c, 1)
            act.wait_ge(s_last, 32)
            act.activation(lnlast[:, 1:S], last[:, 1:S], ACT.Ln).then_inc(s_lnl, 1)
            act.wait_ge(s_rat0, 32)
            for half in range(2):
                act.wait_ge(s_rat[half], 16 * NCH)
            for m in range(0, NG, 2):
                some = ratios[:, :, m * G:(m + 2) * G, :]
                act.activation(some, some, ACT.Ln).then_inc(s_ln, 1)
            for m in range(NG):
                act.wait_ge(s_dd, m + 1)
                act.activation(H[:, m * G:(m + 1) * G, :], H[:, m * G:(m + 1) * G, :], ACT.Exp).then_inc(s_h, 1)

        @block.vector
        def _(dve):
            dve.wait_ge(s_const, 1)
            dve.tensor_scalar(block_row[:, :], row[:, :], VP - 1, None, ALU.bitwise_and).then_inc(s_let, 1)
            dve.wait_ge(s_let, 1)
            dve.tensor_copy(letter[:, :], block_row[:, :]).then_inc(s_let, 1)
            dve.wait_ge(s_let, 2)
            for k, onehot in ((1, onehot_y[:, :]), (0, onehot_x[0:V3, 0, :])):
                dve.wait_ge(s_tok[k], 16)
                rows = VP if k else V3
                dve.tensor_scalar(onehot, tok[0:rows, k, :], letter[0:rows, :], None, ALU.is_equal).then_inc(s_hot, 1)
                if k:
                    dve.wait_ge(s_pair, 1)
                    dve.wait_ge(s_const, 2)
                    dve.tensor_copy(pair[:, 0, :], psum[2][0:V, 0:V]).then_inc(s_y3, 1)
                    for q in range(3):
                        dve.wait_ge(s_y3, q + 1)
                        dve.tensor_copy(pair3[0:V, q, 0:V], pair[:, q, :]).then_inc(s_split, 1)
                        if q < 2:
                            dve.wait_ge(s_split, q + 1)
                            dve.tensor_tensor(pair[:, q + 1, :], pair[:, q, :], pair3[0:V, q, 0:V], ALU.subtract).then_inc(s_y3, 1)
            dve.wait_ge(s_const, 3)
            dve.scalar_tensor_tensor(decay[:, :], decay[:, :], -1.0, decay[:, :], ALU.mult, ALU.max).then_inc(s_abs, 1)
            dve.wait_ge(s_w, 80)
            dve.wait_ge(s_hot, 2)
            for k in range(2):
                dve.tensor_reduce(counts[:, k, 0, :], (onehot_y[0:V, :] if k else onehot_x[0:V, 0, :]).rearrange("v (b s) -> v b s", b=B), AX.X, ALU.add).then_inc(s_dch, 1)
            dve.wait_ge(s_dch, 2)
            for k in range(2):
                dve.tensor_copy(counts[:, k, 1:4, :], counts[:, k, 0:1, :].broadcast_to([V, 3, B])).then_inc(s_cnt, 1)
            dve.wait_ge(s_pair, 2)
            dve.tensor_scalar(gap[:, 0:1], psum[3][0:V, 0:1], bgap[:, :], 1.0 / S, ALU.add, ALU.mult).then_inc(s_gc, 1)
            dve.tensor_scalar(gap[:, 1:2], psum[3][0:V, 1:2], 1.0 / S, None, ALU.mult).then_inc(s_gc, 1)
            dve.wait_ge(s_gc, 2)
            for k in range(2):
                dve.tensor_copy(gapcol[:, k, :], gap[:, k:k + 1].broadcast_to([V, P])).then_inc(s_gc, 1)
            dve.wait_ge(s_A, 1)
            dve.tensor_copy(gapscore[:, :], psum[0][:, 0:B]).then_inc(s_Ac, 1)
            dve.wait_ge(s_Ac, 1)
            for n in range(2 * NG):
                m = n // 2
                dve.wait_ge(s_th, n + 1)
                dst, signal = (w_rows[:, 1, m * G:(m + 1) * G, :], s_back) if n % 2 else (theta[:, m * G:(m + 1) * G, :], s_thc)
                dve.tensor_tensor(dst, psum[n % 8].rearrange("p (k s) -> p k s", k=G),
                                  gapscore[:, m * G:(m + 1) * G].unsqueeze(2).broadcast_to([P, G, S]), ALU.add).then_inc(signal, 1)

            dve.wait_ge(s_c, 1)
            dve.wait_ge(s_wdp[0], 32)
            dve.wait_ge(s_const, 9)
            dve.reciprocal(R[0:64, :], w_dp[0:64, 1, :]).then_inc(s_dve, 1)
            dve.wait_ge(s_dve, 1)
            dve.memset(R[0:64, 0:1], 0.0).then_inc(s_dve, 1)
            dve.wait_ge(s_dve, 2)
            dve.tensor_tensor(bb[0:64, :], w_dp[0:64, 2, :], R[0:64, :], ALU.mult).then_inc(s_b, 2)
            dve.wait_ge(s_b, 2)
            dve.scalar_tensor_tensor(aa[0:64, :], bb[0:64, :], crow[0:64, :], w_dp[0:64, 2, :], ALU.mult, ALU.add).then_inc(s_a, 2)
            dve.wait_ge(s_a, 2)
            dve.tensor_tensor_scan(hist[0:64, 2, 1:HALF + 1], bb[0:64, :], aa[0:64, :], 0.0, ALU.mult, ALU.add).then_inc(s_scan, 2)
            dve.wait_ge(s_scan, 2)
            dve.reciprocal(rH[0:64, 0, :], hist[0:64, 2, 1:HALF + 1]).then_inc(s_rh, 2)
            dve.wait_ge(s_rh, 2)
            dve.tensor_tensor(xx[0:64, :], rH[0:64, 0, :], hist[0:64, 2, 0:HALF], ALU.mult).then_inc(s_dve, 1)
            dve.wait_ge(s_dve, 3)
            dve.tensor_tensor(R[0:64, :], R[0:64, :], xx[0:64, :], ALU.mult).then_inc(s_dve, 1)
            dve.reciprocal(R[64:128, :], w_dp[64:128, 2, :]).then_inc(s_dve, 1)
            dve.wait_ge(s_dve, 5)
            for s in range(3, S + 2):
                p = slice(0 if s <= S else 64, P)
                w, h = w_dp[p, s, :], hist[p, s, 1:HALF + 1]
                if (s - 1) % CH == 0 and s <= S:
                    dve.wait_ge(s_wdp[(s - 1) // CH], 32)
                if s == 3:
                    dve.tensor_tensor(bb[p, :], w, R[p, :], ALU.mult).then_inc(s_b, 1)
                else:
                    dve.wait_ge(s_rh, s - 1)
                    dve.wait_ge(s_g, s)
                    dve.tensor_tensor(bb[p, :], gg[p, s % 2, :], rH[p, s % 2, :], ALU.mult).then_inc(s_b, 1)
                dve.wait_ge(s_b, s)
                dve.scalar_tensor_tensor(aa[p, :], bb[p, :], crow[p, :], w, ALU.mult, ALU.add).then_inc(s_a, 1)
                dve.wait_ge(s_a, s)
                if s > 3:
                    dve.wait_ge(s_hand, s)
                else:
                    dve.wait_ge(s_hand, 3)
                dve.tensor_tensor_scan(h, bb[p, :], aa[p, :], hist[p, s, 0:1], ALU.mult, ALU.add).then_inc(s_scan, 1)
                dve.wait_ge(s_scan, s)
                dve.reciprocal(rH[p, (s + 1) % 2, :], h).then_inc(s_rh, 1)

            dve.wait_ge(s_lnl, 1)
            dve.wait_ge(s_bf, 2)
            dve.tensor_tensor_scan(path1[:, 1:S], ones_bs[:, 1:S], lnlast[:, 1:S][:, ::-1], 0.0, ALU.mult, ALU.add).then_inc(s_dch, 1)
            dve.memset(path1[:, 0:1], 0.0).then_inc(s_dch, 1)
            dve.wait_ge(s_dch, 4)
            dve.wait_ge(s_th1, 16)
            dve.tensor_tensor(path1[:, :], path1[:, :], th1[:, :], ALU.add).then_inc(s_p1, 1)
            for m in range(NG):
                dve.wait_ge(s_D, m + 1)
                dve.tensor_tensor(H[:, m * G:(m + 1) * G, :], psum[m].rearrange("p (k s) -> p k s", k=G), theta[:, m * G:(m + 1) * G, :],
                                  ALU.subtract).then_inc(s_dd, 1)


def layers_stage(nc, used, A, H, ident, psall, W, table, logitsT, w1, w2, s_weights):
    psum = [psall[:, i, :] for i in range(8)]
    with ExitStack() as ctx:
        sb = lambda name, shape, dt=F32: ctx.enter_context(nc.sbuf_tensor(name, shape, dt))
        sem = lambda name: used.append(nc.alloc_semaphore(name)) or used[-1]
        decay, wkq, wv0, wvo, variants = W["decay"], W["wkq"], W["wv0"], W["wvo"], W["variants"]
        wq1, wk1, rw1, rb1, rw2, rb2, wr = W["wq1"], W["wk1"], W["rw1"], W["rb1"], W["rw2"], W["rb2"], W["wr"]
        bo, gamma, beta = W["bo"], W["gamma"], W["beta"]
        chosen = sb("chosen", [P, G, WALL])
        power = sb("power", [P, G])
        stats = sb("stats", [P, 5, G, 6]); mv = sb("mv", [P, 5, G, 2]); ve = sb("ve", [P, 5, G]); rstd = sb("rstd", [P, 5, G])
        xh = [sb(f"xh{i}", [P, G, D]) for i in range(4)]
        xT = [sb(f"xT{i}", [P, G, S]) for i in range(4)]
        pT = sb("pT", [P, G, S]); v0 = sb("v0", [P, G, D])
        sd = sb("sd", [P, G, S]); th = sb("th", [P, G, S]); act0 = sb("act0", [P, G, S])
        msum = sb("msum", [P, G]); r1 = sb("r1", [32, G]); lg = sb("lg", [1, G, 3]); c1 = sb("c1", [1, G]); mx1 = sb("mx1", [1, G])
        c2 = sb("c2", [1, G]); sel = sb("sel", [1, G], I32)
        qk = sb("qk", [P, G, 4, S]); v17 = sb("v17", [P, G, HEADS, DK + 1])
        smax = sb("smax", [P, 2, 2, HEADS]); bias = sb("bias", [P, 2, 2, HEADS])
        ex = [sb(f"ex{i}", [P, 2, HEADS, S]) for i in range(2)]
        exT = sb("exT", [P, HEADS, S])
        rden = sb("rden", [P, HEADS]); o0 = sb("o0", [P, G, D]); oT = sb("oT", [P, G, S])
        qT1 = sb("qT1", [P, 4, G * S]); kT1 = sb("kT1", [P, 4, G * S]); vo = sb("vo", [P, G, HEADS, D])
        masked = sb("masked", [P, 2, HEADS, S]); den = sb("den", [P, 2, HEADS]); rden1 = sb("rden1", [P, 2, HEADS])
        y1 = sb("y1", [P, G, D]); y2 = sb("y2", [P, G, D])

        s_in = sem("s_in"); s_one = sem("s2_one")
        s_bn = [sem(f"s_bn{i}") for i in range(5)]; s_mv = [sem(f"s_mv{i}") for i in range(5)]
        s_ve = [sem(f"s_ve{i}") for i in range(5)]; s_rstd = [sem(f"s_rstd{i}") for i in range(5)]
        s_xh = [sem(f"s_xh{i}") for i in range(5)]
        s_xT = [sem(f"s_xT{i}") for i in range(4)]; s_xTc = [sem(f"s_xTc{i}") for i in range(4)]
        s_p = sem("s_p"); s_pT = sem("s_pT"); s_v0 = sem("s_v0"); s_v0c = sem("s_v0c"); s_s0 = sem("s_s0"); s_sd = sem("s_sd")
        s_th = sem("s2_th"); s_act0 = sem("s_act0"); s_o = sem("s_o"); s_h = [sem(f"s_h{i}") for i in range(3)]
        s_ms = sem("s_ms"); s_r1 = sem("s_r1"); s_r1c = sem("s_r1c"); s_lg = sem("s_lg"); s_rt = sem("s_rt"); s_sel = sem("s_sel")
        s_ch = sem("s_ch"); s_chw = sem("s_chw"); s_qk = sem("s_qk"); s_qkc = sem("s_qkc"); s_v = sem("s_v"); s_vc = sem("s_vc")
        s_half = sem("s_half"); s_sc = [sem(f"s_sc{i}") for i in range(2)]; s_mx = [sem(f"s_mx{i}") for i in range(2)]
        s_bias = [sem(f"s_bias{i}") for i in range(2)]
        s_ex = [sem(f"s_ex{i}") for i in range(2)]; s_eT = [sem(f"s_eT{i}") for i in range(2)]
        s_eTa = [sem(f"s_eTa{i}") for i in range(2)]; s_eTv = [sem(f"s_eTv{i}") for i in range(2)]
        s_av = [sem(f"s_av{i}") for i in range(2)]
        s_rd = sem("s_rd"); s_o0 = sem("s_o0"); s_oT = sem("s_oT"); s_oTc = sem("s_oTc"); s_wo = sem("s_wo")
        s_q1 = sem("s_q1"); s_q1a = sem("s_q1a"); s_q1v = sem("s_q1v"); s_vo = sem("s_vo"); s_voa = sem("s_voa"); s_vov = sem("s_vov")
        s_zero = sem("s_zero"); s_rd1 = sem("s_rd1"); s_nrm = sem("s_nrm")
        s_xb = sem("s_xb"); s_y = sem("s_y2"); s_gm = sem("s_gm"); s_lt = sem("s_lt"); s_ltc = sem("s_ltc"); s_tab = sem("s_tab")
        block = ctx.enter_context(nc.Block())
        rows = lambda g, k: H[:, bass.ds(g * G + k, 1), :].squeeze(1)
        group = lambda g: H[:, bass.ds(g * G, G), :]
        bank = lambda i: psum[i].rearrange("p (k s) -> p k s", k=G)
        first = lambda g: isinstance(g, int) and g == 0

        def wait_alone(eng, signal, value):
            if not isinstance(value, int):
                value = eng.to_reg(value)
            eng.wait_ge(s_in, IN)
            eng.wait_ge(signal, value)

        def turns(eng, body, last):
            for t in range(3):
                body(t, True, t >= 1, t >= 2, False, True)
            with eng.Fori(3, NG - 1) as t:
                body(t, True, True, True, True, True)
            for t in range(NG - 1, NG + 1):
                body(t, t < NG, True, True, True, False)
            for t in range(NG + 1, NG + 3):
                last(t, t < NG + 2)

        IN = 1

        @block.sync
        def _(sp):
            sp.dma_start(w1[:, :, :], A["L1_ffn_W1"].rearrange("e d f -> d e f")).then_inc(s_weights, 16)
            for e in range(E):
                sp.dma_start(w2[:, e, :, :], A["L1_ffn_W2"][e].rearrange("(c p) d -> p c d", p=P)).then_inc(s_weights, 16)
            sp.wait_ge(s_in, IN)

            def body(t, a1, a2, b, c, ahead):
                if a1:
                    wait_alone(sp, s_sel, t + 1)
                    picks = [sp.value_load(sel[0:1, k:k + 1], min_val=0, max_val=2) for k in range(G)]
                    if a2:
                        sp.wait_ge(s_v, t)
                    for k in range(G):
                        sp.dma_start(chosen[:, k, 0:WO], variants[:, bass.ds(picks[k], 1), 0:WO].squeeze(1)).then_inc(s_ch, 16)
                    if a2:
                        sp.wait_ge(s_wo, t)
                    for k in range(G):
                        sp.dma_start(chosen[:, k, WO:WALL], variants[:, bass.ds(picks[k], 1), WO:WALL].squeeze(1)).then_inc(s_chw, 16)
                if c:
                    g = t - 3
                    sp.wait_ge(s_xh[3], g * G + G)
                    sp.dma_start(table[bass.ds(g * G * S, G * S), :].rearrange("(k s) d -> s k d", k=G), xh[3][:, :, :]).then_inc(s_tab, 16)

            turns(sp, body, lambda t, b: body(t, False, False, b, True, False))
            sp.wait_ge(s_tab, 16 * NG)

        @block.gpsimd
        def _(pool):
            pool.memset(power[:, :], -0.5).then_inc(s_in, 1)
            pool.memset(v17[:, :, :, DK:DK + 1], 1.0).then_inc(s_one, 1)
            pool.wait_ge(s_in, IN)

            def ln_rstd(g, i, eps):
                wait_alone(pool, s_mv[i], g * G + G)
                pool.tensor_scalar(ve[:, i, :], mv[:, i, :, 1], eps, None, ALU.add).then_inc(s_ve[i], 1)
                pool.wait_ge(s_ve[i], g + 1)
                pool.tensor_tensor(rstd[:, i, :], ve[:, i, :], power[:, :], ALU.pow).then_inc(s_rstd[i], 1)

            def share(g, k):
                pool.wait_ge(s_rd1, g * G + k + 1)
                pool.tensor_tensor(ex[1][:, k % 2, :, :], ex[1][:, k % 2, :, :],
                                   rden1[:, k % 2, :].unsqueeze(2).broadcast_to([P, HEADS, S]), ALU.mult).then_inc(s_nrm, 1)

            def affine(g):
                pool.wait_ge(s_xh[4], g * G + G)
                pool.tensor_tensor(y2[:, :, :], y2[:, :, :], gamma[:, :].unsqueeze(1).broadcast_to([P, G, D]), ALU.mult).then_inc(s_gm, 1)
                pool.wait_ge(s_gm, 2 * g + 1)
                pool.tensor_tensor(y2[:, :, :], y2[:, :, :], beta[:, :].unsqueeze(1).broadcast_to([P, G, D]), ALU.add).then_inc(s_gm, 1)

            def residual(g):
                pool.wait_ge(s_xh[2], g * G + G)
                pool.tensor_tensor(y1[:, :, :], xh[2][:, :, :], bo[:, :].unsqueeze(1).broadcast_to([P, G, D]), ALU.add).then_inc(s_xb, 1)

            ln_rstd(0, 0, 1e-5)

            def body(t, a1, a2, b, c, ahead):
                g2, g3, g4 = t - 1, t - 2, t - 3
                if b:
                    ln_rstd(g3, 2, 1e-5)
                if c:
                    ln_rstd(g4, 4, 1e-6)
                    affine(g4)
                    ln_rstd(g4, 3, 1e-5)
                if b:
                    share(g3, 0)
                if a1:
                    ln_rstd(t, 1, 1e-5)
                if b:
                    residual(g3)
                    share(g3, 1)
                    share(g3, 2)
                if ahead:
                    ln_rstd(t + 1, 0, 1e-5)
                if b:
                    share(g3, 3)

            def last(t, b):
                c, g3, g4 = True, t - 2, t - 3
                if b:
                    ln_rstd(g3, 2, 1e-5)
                if c:
                    ln_rstd(g4, 4, 1e-6)
                    affine(g4)
                if b:
                    residual(g3)
                    share(g3, 0)
                if c:
                    ln_rstd(g4, 3, 1e-5)
                if b:
                    share(g3, 1)
                    share(g3, 2)
                    share(g3, 3)

            turns(pool, body, last)

        @block.tensor
        def _(pe):
            pe.wait_ge(s_in, IN)

            def turn_x(g, i, b):
                pe.wait_ge(s_xh[i], g * G + G)
                for k in range(G):
                    mm = pe.transpose(psum[b][:, k * S:(k + 1) * S], xh[i][:, k, :], ident[:, :])
                mm.then_inc(s_xT[i], 1)

            def turn_ex(g, i, k):
                pe.wait_ge(s_ex[0] if i == 0 else s_nrm, g * G + k + 1)
                for n in range(HEADS):
                    mm = pe.transpose(psum[2 + n // 4][:, (n % 4) * S:(n % 4 + 1) * S], ex[i][:, k % 2, n, :], ident[:, :])
                mm.then_inc(s_eT[i], 1)

            def a1_xT(t):
                turn_x(t, 0, 0)

            def a1_p(t):
                pe.wait_ge(s_xTc[0], t + 1)
                pe.matmul(psum[0], wkq[:, :], xT[0][:, :, :], start=True, stop=True).then_inc(s_p, 1)

            def a1_v(t):
                pe.wait_ge(s_pT, t + 1)
                for k in range(G):
                    mm = pe.matmul(psum[0][:, k * D:(k + 1) * D], xT[0][:, k, :], wv0[:, :], start=True, stop=True)
                mm.then_inc(s_v0, 1)

            def a1_s(t):
                pe.wait_ge(s_v0c, t + 1)
                for k in range(G):
                    mm = pe.matmul(psum[0][:, k * S:(k + 1) * S], pT[:, k, :], xT[0][:, k, :], start=True, stop=True)
                mm.then_inc(s_s0, 1)

            def a1_o(t):
                pe.wait_ge(s_act0, t + 1)
                for k in range(G):
                    mm = pe.matmul(psum[0][:, k * D:(k + 1) * D], act0[:, k, :], v0[:, k, :], start=True, stop=True)
                mm.then_inc(s_o, 1)

            def a1_xT2(t):
                turn_x(t, 1, 0)

            def a1_r1(t):
                pe.wait_ge(s_ms, t + 1)
                pe.matmul(psum[0][0:32, 0:G], rw1[:, :], msum[:, :], start=True, stop=True).then_inc(s_r1, 1)

            def a1_lg(t):
                wait_alone(pe, s_r1c, t + 1)
                for k in range(G):
                    mm = pe.matmul(psum[0][0:1, 3 * k:3 * k + 3], r1[:, k:k + 1], rw2[:, :], start=True, stop=True)
                mm.then_inc(s_lg, 1)

            def a2_v(g):
                for k in range(G):
                    mm = pe.matmul(psum[1][:, k * D:(k + 1) * D], xT[1][:, k, :], chosen[:, k, WV:WO], start=True, stop=True)
                mm.then_inc(s_v, 1)

            def a2_qk(g):
                pe.wait_ge(s_ch, (g + 1) * 16 * G)
                pe.wait_ge(s_xTc[1], g + 1)
                for k in range(G):
                    if k >= 2:
                        pe.wait_ge(s_qkc, g * G + k - 1)
                    for c in range(4):
                        mm = pe.matmul(psum[4 + k % 2][:, c * S:(c + 1) * S], chosen[:, k, c * P:(c + 1) * P], xT[1][:, k, :], start=True, stop=True)
                    mm.then_inc(s_qk, 1)

            def a2_scores(g, k, pair):
                n = g * G + k
                if pair == 0:
                    pe.wait_ge(s_qkc, g * G + G)
                    if k:
                        pe.wait_ge(s_ex[0], n)
                else:
                    pe.wait_ge(s_half, n + 1)
                for c in range(2):
                    for r in range(2 * pair, 2 * pair + 2):
                        q = slice(r * PADK, (r + 1) * PADK)
                        col = (2 * pair + c) * S
                        mm = pe.matmul(psum[4 + r % 2][:, col:col + S], qk[q, k, c, :], qk[q, k, 2 + c, :], start=True, stop=True)
                mm.then_inc(s_sc[0] if pair else s_half, 1)

            def a2_weigh(g, k):
                n = g * G + k
                pe.wait_ge(s_vc, g + 1)
                pe.wait_ge(s_eTa[0], n + 1)
                pe.wait_ge(s_eTv[0], n + 1)
                for m in range(HEADS):
                    h = 4 * (m % 2) + m // 4 + 2 * (m % 4 // 2)
                    mm = pe.matmul(psum[1][:, h * (DK + 1):(h + 1) * (DK + 1)], exT[:, m, :], v17[:, k, h, :], start=True, stop=True)
                mm.then_inc(s_av[0], 1)

            def a2_oT(g):
                pe.wait_ge(s_o0, g * G + G)
                pe.wait_ge(s_ex[0], g * G + G)
                for k in range(G):
                    mm = pe.transpose(psum[4][:, k * S:(k + 1) * S], o0[:, k, :], ident[:, :])
                mm.then_inc(s_oT, 1)

            def a2_wo(g):
                pe.wait_ge(s_oTc, g + 1)
                pe.wait_ge(s_chw, (g + 1) * 16 * G)
                for k in range(G):
                    mm = pe.matmul(psum[5][:, k * D:(k + 1) * D], oT[:, k, :], chosen[:, k, WO:WALL], start=True, stop=True)
                mm.then_inc(s_wo, 1)

            def b_qk(g, part):
                for c in range(4 * part, 4 * part + 4):
                    if c == 0:
                        pe.wait_ge(s_xTc[2], g + 1)
                    if 2 <= c < 6:
                        pe.wait_ge(s_q1a, g * 4 + c - 1)
                    if c >= 6:
                        pe.wait_ge(s_q1v, g * 4 + c - 5)
                    w = wq1 if c < 4 else wk1
                    pe.matmul(psum[7 - c % 2], w[:, (c % 4) * P:(c % 4 + 1) * P], xT[2][:, :, :], start=True, stop=True).then_inc(s_q1, 1)

            def b_values(g, n):
                pe.matmul(psum[1], xT[2][:, n // 2, :], wvo[:, 4 * (n % 2):4 * (n % 2) + 4, :], start=True, stop=True).then_inc(s_vo, 1)

            def b_scores(g, k):
                if k:
                    pe.wait_ge(s_mx[1], HEADS * (g * G + k))
                else:
                    pe.wait_ge(s_q1v, g * 4 + 4)
                for h in range(HEADS):
                    r = slice((h % 2) * K1, (h % 2 + 1) * K1)
                    mm = pe.matmul(psum[6 + h % 2][:, (h // 2) * S:(h // 2 + 1) * S], qT1[r, h // 2, k * S:(k + 1) * S],
                                   kT1[r, h // 2, k * S:(k + 1) * S], start=True, stop=True)
                mm.then_inc(s_sc[1], 1)

            def b_weigh(g, k):
                n = g * G + k
                pe.wait_ge(s_eTa[1], n + 1)
                pe.wait_ge(s_eTv[1], n + 1)
                for m in range(HEADS):
                    mm = pe.matmul(psum[1][:, 0:D], exT[:, m, :], vo[:, k, 2 * (m % 4) + m // 4, :], start=(m == 0), stop=(m == HEADS - 1))
                mm.then_inc(s_av[1], 1)

            def c_logits(g):
                pe.wait_ge(s_xTc[3], g + 1)
                pe.matmul(psum[0][0:E, :], wr[:, :], xT[3][:, :, :], start=True, stop=True).then_inc(s_lt, 1)

            def body(t, a1, a2, b, c, ahead):
                g2, g3, g4 = t - 1, t - 2, t - 3
                if c:
                    turn_ex(g4, 1, 3)
                if a2:
                    if not first(g2):
                        pe.wait_ge(s_h[1], g2)
                    a2_qk(g2)
                if c:
                    pe.wait_ge(s_y, g4 * G + 3)
                    b_weigh(g4, 3)
                if a1:
                    if not first(t):
                        pe.wait_ge(s_rt, 5 * t - 4)
                    if c and not first(g4):
                        pe.wait_ge(s_ltc, g4)
                    a1_xT(t)
                if b:
                    turn_x(g3, 2, 6)
                if a2:
                    if c:
                        pe.wait_ge(s_y, g4 * G + 4)
                    a2_v(g2)
                if b:
                    b_qk(g3, 0)
                if a2:
                    a2_scores(g2, 0, 0)
                    a2_scores(g2, 0, 1)
                if a1:
                    a1_p(t)
                if b:
                    b_qk(g3, 1)
                if a1:
                    a1_v(t)
                if a2:
                    turn_ex(g2, 0, 0)
                if b:
                    b_scores(g3, 0)
                    if a2:
                        pe.wait_ge(s_vc, g2 + 1)
                    else:
                        pe.wait_ge(s_y, g4 * G + 4)
                    b_values(g3, 0)
                if a1:
                    a1_s(t)
                if a2:
                    a2_scores(g2, 1, 0)
                    if b:
                        pe.wait_ge(s_voa, g3 * G + 1)
                    else:
                        pe.wait_ge(s_vc, g2 + 1)
                    a2_weigh(g2, 0)
                    a2_scores(g2, 1, 1)
                if b:
                    if a2:
                        pe.wait_ge(s_o0, g2 * G + 1)
                    else:
                        pe.wait_ge(s_voa, g3 * G + 1)
                    b_values(g3, 1)
                    pe.wait_ge(s_vov, g3 * G + 1)
                    b_values(g3, 2)
                if a1:
                    a1_o(t)
                if a2:
                    turn_ex(g2, 0, 1)
                if b:
                    b_scores(g3, 1)
                if a2:
                    a2_scores(g2, 2, 0)
                    if b:
                        pe.wait_ge(s_voa, g3 * G + 2)
                    else:
                        pe.wait_ge(s_o0, g2 * G + 1)
                    a2_weigh(g2, 1)
                    a2_scores(g2, 2, 1)
                if b:
                    if a2:
                        pe.wait_ge(s_o0, g2 * G + 2)
                    else:
                        pe.wait_ge(s_voa, g3 * G + 2)
                    b_values(g3, 3)
                    turn_ex(g3, 1, 0)
                if c:
                    if a1:
                        pe.wait_ge(s_h[0], t + 1)
                    elif isinstance(t, int) and t == NG:
                        pe.wait_ge(s_rt, 5 * NG - 4)
                    if not a1 and not first(g4):
                        pe.wait_ge(s_ltc, g4)
                    turn_x(g4, 3, 0)
                if b:
                    pe.wait_ge(s_vov, g3 * G + 2)
                    b_values(g3, 4)
                if c:
                    c_logits(g4)
                if b:
                    pe.wait_ge(s_voa, g3 * G + 3)
                    b_weigh(g3, 0)
                if a2:
                    turn_ex(g2, 0, 2)
                if b:
                    b_scores(g3, 2)
                if a2:
                    a2_scores(g2, 3, 0)
                    if b:
                        pe.wait_ge(s_y, g3 * G + 1)
                    else:
                        pe.wait_ge(s_o0, g2 * G + 2)
                    a2_weigh(g2, 2)
                if a1:
                    if c:
                        pe.wait_ge(s_ltc, g4 + 1)
                    a1_xT2(t)
                if a2:
                    a2_scores(g2, 3, 1)
                if b:
                    if a2:
                        pe.wait_ge(s_o0, g2 * G + 3)
                    else:
                        pe.wait_ge(s_y, g3 * G + 1)
                    b_values(g3, 5)
                    turn_ex(g3, 1, 1)
                    pe.wait_ge(s_vov, g3 * G + 3)
                    b_values(g3, 6)
                if a1:
                    a1_r1(t)
                if b:
                    pe.wait_ge(s_voa, g3 * G + 4)
                    b_weigh(g3, 1)
                if a2:
                    turn_ex(g2, 0, 3)
                if b:
                    pe.wait_ge(s_y, g3 * G + 2)
                    b_values(g3, 7)
                if a1:
                    a1_lg(t)
                if b:
                    b_scores(g3, 3)
                if a2:
                    if b:
                        pe.wait_ge(s_vov, g3 * G + 4)
                    else:
                        pe.wait_ge(s_o0, g2 * G + 3)
                    a2_weigh(g2, 3)
                if b:
                    turn_ex(g3, 1, 2)
                if a2:
                    a2_oT(g2)
                if b:
                    if a2:
                        pe.wait_ge(s_o0, g2 * G + 4)
                    else:
                        pe.wait_ge(s_vov, g3 * G + 4)
                    b_weigh(g3, 2)
                if a2:
                    a2_wo(g2)

            def last(t, b):
                c, g3, g4 = True, t - 2, t - 3
                if c:
                    turn_ex(g4, 1, 3)
                    pe.wait_ge(s_y, g4 * G + 3)
                    b_weigh(g4, 3)
                if b:
                    turn_x(g3, 2, 6)
                    b_qk(g3, 0)
                    b_qk(g3, 1)
                    b_scores(g3, 0)
                    if c:
                        pe.wait_ge(s_y, g4 * G + 4)
                    b_values(g3, 0)
                    pe.wait_ge(s_voa, g3 * G + 1)
                    b_values(g3, 1)
                    pe.wait_ge(s_vov, g3 * G + 1)
                    b_values(g3, 2)
                    b_scores(g3, 1)
                    pe.wait_ge(s_voa, g3 * G + 2)
                    b_values(g3, 3)
                    pe.wait_ge(s_vov, g3 * G + 2)
                    b_values(g3, 4)
                    pe.wait_ge(s_voa, g3 * G + 3)
                    b_values(g3, 5)
                    b_scores(g3, 2)
                    turn_ex(g3, 1, 0)
                    pe.wait_ge(s_vov, g3 * G + 3)
                    b_values(g3, 6)
                    pe.wait_ge(s_voa, g3 * G + 4)
                    b_weigh(g3, 0)
                    pe.wait_ge(s_y, g3 * G + 1)
                    b_values(g3, 7)
                    b_scores(g3, 3)
                if c:
                    pe.wait_ge(s_ltc, g4)
                    turn_x(g4, 3, 0)
                if b:
                    turn_ex(g3, 1, 1)
                if c:
                    c_logits(g4)
                if b:
                    pe.wait_ge(s_vov, g3 * G + 4)
                    b_weigh(g3, 1)
                    turn_ex(g3, 1, 2)
                    pe.wait_ge(s_y, g3 * G + 2)
                    b_weigh(g3, 2)

            turns(pe, body, last)

        @block.scalar
        def _(act):
            act.wait_ge(s_in, IN)

            def copy_x(g, i, b):
                act.wait_ge(s_xT[i], g + 1)
                act.activation(xT[i][:, :, :], bank(b), ACT.Copy).then_inc(s_xTc[i], 1)

            def copy_ex(g, i, k):
                act.wait_ge(s_eT[i], g * G + k + 1)
                act.activation(exT[:, 0:4, :], psum[2], ACT.Copy).then_inc(s_eTa[i], 1)

            def a2_copy_qk(g, k):
                act.wait_ge(s_qk, g * G + k + 1)
                act.activation(qk[:, k, :, :], bank(4 + k % 2), ACT.Copy).then_inc(s_qkc, 1)

            def b_copy_q(g, n):
                act.wait_ge(s_q1, g * 8 + n + 1)
                act.activation(qT1[:, n, :], psum[7 - n % 2], ACT.Copy).then_inc(s_q1a, 1)

            def a1_copy_p(t):
                act.wait_ge(s_p, t + 1)
                act.activation(pT[:, :, :], bank(0), ACT.Copy).then_inc(s_pT, 1)

            def a1_copy_v(t):
                act.wait_ge(s_v0, t + 1)
                act.activation(v0[:, :, :], bank(0), ACT.Copy, scale=0.5).then_inc(s_v0c, 1)

            def a1_tanh(t):
                act.wait_ge(s_sd, t + 1)
                act.activation(th[:, :, :], sd[:, :, :], ACT.Tanh, scale=0.5).then_inc(s_th, 1)

            def a1_relu(t):
                act.wait_ge(s_r1, t + 1)
                act.activation(r1[:, :], psum[0][0:32, 0:G], ACT.Relu, bias=rb1[:, :], scale=1.0 / S).then_inc(s_r1c, 1)

            def a2_copy_o(g):
                act.wait_ge(s_oT, g + 1)
                act.activation(oT[:, :, :], bank(4), ACT.Copy).then_inc(s_oTc, 1)

            def c_copy_logits(g):
                act.wait_ge(s_lt, g + 1)
                act.activation(logitsT[:, bass.ds(g * G * S, G * S)], psum[0][0:E, :], ACT.Copy).then_inc(s_ltc, 1)

            def a2_exps(g, k):
                n = g * G + k
                act.wait_ge(s_bias[0], n + 1)
                if k >= 2 or not first(g):
                    act.wait_ge(s_eT[0], n - 1)
                for m in range(HEADS):
                    ins = act.activation(ex[0][:, k % 2, m, :], psum[4 + m // 4][:, (m % 4) * S:(m % 4 + 1) * S], ACT.Exp,
                                         bias=bias[:, 0, k % 2, m:m + 1], scale=1.0 / math.sqrt(DK))
                ins.then_inc(s_ex[0], 1)

            def b_exps(g, k):
                n = g * G + k
                act.wait_ge(s_bias[1], n + 1)
                if k >= 2 or not first(g):
                    act.wait_ge(s_eT[1], n - 1)
                for m in range(HEADS):
                    ins = act.activation(ex[1][:, k % 2, m, :], masked[:, k % 2, m, :], ACT.Exp, bias=bias[:, 1, k % 2, m:m + 1],
                                         scale=1.0 / math.sqrt(K1), accum_out=den[:, k % 2, m:m + 1])
                ins.then_inc(s_ex[1], 1)

            def b_values(g, n):
                act.wait_ge(s_vo, g * 2 * G + n + 1)
                act.activation(vo[:, n // 2, 0:4, :], bank(1), ACT.Copy).then_inc(s_voa, 1)

            def body(t, a1, a2, b, c, ahead):
                g2, g3, g4 = t - 1, t - 2, t - 3
                if a2:
                    a2_copy_qk(g2, 0)
                    a2_copy_qk(g2, 1)
                if c:
                    copy_ex(g4, 1, 3)
                if a2:
                    a2_copy_qk(g2, 2)
                if b:
                    copy_x(g3, 2, 6)
                    b_copy_q(g3, 0)
                    b_copy_q(g3, 1)
                if a2:
                    a2_copy_qk(g2, 3)
                if a1:
                    copy_x(t, 0, 0)
                if b:
                    b_copy_q(g3, 2)
                    b_copy_q(g3, 3)
                if a2:
                    a2_exps(g2, 0)
                if a1:
                    a1_copy_p(t)
                    a1_copy_v(t)
                if a2:
                    copy_ex(g2, 0, 0)
                if b:
                    b_values(g3, 0)
                    b_exps(g3, 0)
                if a1:
                    a1_tanh(t)
                if a2:
                    a2_exps(g2, 1)
                if b:
                    b_values(g3, 2)
                if a2:
                    copy_ex(g2, 0, 1)
                    a2_exps(g2, 2)
                if c:
                    copy_x(g4, 3, 0)
                if b:
                    copy_ex(g3, 1, 0)
                    b_values(g3, 4)
                    b_exps(g3, 1)
                if c:
                    c_copy_logits(g4)
                if a2:
                    copy_ex(g2, 0, 2)
                if b:
                    b_exps(g3, 2)
                if a2:
                    a2_exps(g2, 3)
                if a1:
                    copy_x(t, 1, 0)
                if b:
                    copy_ex(g3, 1, 1)
                    b_values(g3, 6)
                if a1:
                    a1_relu(t)
                if a2:
                    copy_ex(g2, 0, 3)
                if b:
                    copy_ex(g3, 1, 2)
                    b_exps(g3, 3)
                if a2:
                    a2_copy_o(g2)

            def last(t, b):
                c, g3, g4 = True, t - 2, t - 3
                if c:
                    copy_ex(g4, 1, 3)
                if b:
                    copy_x(g3, 2, 6)
                    b_copy_q(g3, 0)
                    b_copy_q(g3, 1)
                    b_copy_q(g3, 2)
                    b_copy_q(g3, 3)
                    b_values(g3, 0)
                    b_values(g3, 2)
                    b_exps(g3, 0)
                    b_values(g3, 4)
                    b_exps(g3, 1)
                    copy_ex(g3, 1, 0)
                    b_values(g3, 6)
                    b_exps(g3, 2)
                if c:
                    copy_x(g4, 3, 0)
                if b:
                    copy_ex(g3, 1, 1)
                if c:
                    c_copy_logits(g4)
                if b:
                    b_exps(g3, 3)
                    copy_ex(g3, 1, 2)

            turns(act, body, last)

        @block.vector
        def _(dve):
            dve.wait_ge(s_in, IN)
            dve.wait_ge(s_one, 1)

            def ln_stats(g, i, src):
                for k in range(G):
                    dve.bn_stats(stats[:, i, k, :], src(k)).then_inc(s_bn[i], 1)
                for k in range(G):
                    wait_alone(dve, s_bn[i], g * G + k + 1)
                    dve.bn_aggr(mv[:, i, k, :], stats[:, i, k, :]).then_inc(s_mv[i], 1)

            def ln_apply(g, i, src, dst):
                dve.wait_ge(s_rstd[i], g + 1)
                for k in range(G):
                    dve.tensor_scalar(dst(k), src(k), mv[:, i, k, 0:1], rstd[:, i, k:k + 1], ALU.subtract, ALU.mult).then_inc(s_xh[i], 1)

            def add_h(g, i, part):
                dve.tensor_tensor(group(g), group(g), part, ALU.add).then_inc(s_h[i], 1)

            def copy_ex(g, i, k):
                dve.wait_ge(s_eT[i], g * G + k + 1)
                dve.tensor_copy(exT[:, 4:8, :].rearrange("p h s -> p (h s)"), psum[3]).then_inc(s_eTv[i], 1)

            def a1_decay(t):
                dve.wait_ge(s_s0, t + 1)
                dve.tensor_tensor(sd[:, :, :], bank(0), decay[:, :].unsqueeze(1).broadcast_to([P, G, S]), ALU.mult).then_inc(s_sd, 1)

            def a1_silu(t):
                dve.wait_ge(s_th, t + 1)
                dve.scalar_tensor_tensor(act0[:, :, :], th[:, :, :], 1.0, sd[:, :, :], ALU.add, ALU.mult).then_inc(s_act0, 1)

            def a1_route(t):
                dve.wait_ge(s_lg, t + 1)
                dve.tensor_tensor(lg[:, :, :], psum[0][0:1, 0:3 * G].rearrange("p (k c) -> p k c", k=G),
                                  rb2[:, :].unsqueeze(1).broadcast_to([1, G, 3]), ALU.add).then_inc(s_rt, 1)
                dve.wait_ge(s_rt, t * 5 + 1)
                dve.tensor_tensor(c1[:, :], lg[:, :, 1], lg[:, :, 0], ALU.is_gt).then_inc(s_rt, 1)
                dve.tensor_tensor(mx1[:, :], lg[:, :, 1], lg[:, :, 0], ALU.max).then_inc(s_rt, 1)
                dve.wait_ge(s_rt, t * 5 + 3)
                dve.tensor_tensor(c2[:, :], lg[:, :, 2], mx1[:, :], ALU.is_gt).then_inc(s_rt, 2)
                dve.wait_ge(s_rt, t * 5 + 5)
                dve.scalar_tensor_tensor(sel[:, :], c2[:, :], 2.0, c1[:, :], ALU.mult, ALU.max).then_inc(s_sel, 1)

            def a2_max(g, k):
                n = g * G + k
                dve.wait_ge(s_sc[0], n + 1)
                dve.tensor_reduce(smax[:, 0, k % 2, :], psall[:, 4:6, :].rearrange("p b (c s) -> p (b c) s", c=4), AX.X, ALU.max).then_inc(s_mx[0], 1)
                dve.wait_ge(s_mx[0], n + 1)
                dve.tensor_scalar(bias[:, 0, k % 2, :], smax[:, 0, k % 2, :], -1.0 / math.sqrt(DK), None, ALU.mult).then_inc(s_bias[0], 1)

            def a2_norm(g, k):
                n = g * G + k
                av = psum[1][:, 0:HEADS * (DK + 1)].rearrange("p (h c) -> p h c", h=HEADS)
                wait_alone(dve, s_av[0], n + 1)
                dve.reciprocal(rden[:, :], av[:, :, DK]).then_inc(s_rd, 1)
                dve.wait_ge(s_rd, n + 1)
                dve.tensor_tensor(o0[:, k, :].rearrange("p (h c) -> p h c", h=HEADS), av[:, :, 0:DK],
                                  rden[:, :].unsqueeze(2).broadcast_to([P, HEADS, DK]), ALU.mult).then_inc(s_o0, 1)

            def b_values(g, n):
                dve.wait_ge(s_vo, g * 2 * G + n + 1)
                dve.tensor_copy(vo[:, n // 2, 4:8, :].rearrange("p h d -> p (h d)"), psum[1]).then_inc(s_vov, 1)

            def b_mask(g, k):
                n = g * G + k
                if k >= 2 or not first(g):
                    dve.wait_ge(s_ex[1], n - 1)
                wait_alone(dve, s_sc[1], n + 1)
                for c in range(2):
                    dve.tensor_scalar(masked[:, k % 2, 4 * c:4 * c + 4, :].rearrange("p h s -> p (h s)"), psum[6 + c], 0.0,
                                      -1e9 * math.sqrt(K1), ALU.is_equal, ALU.mult).then_inc(s_zero, 1)
                for m in range(HEADS):
                    if m % 4 == 0:
                        wait_alone(dve, s_zero, 2 * n + 1 + m // 4)
                    dve.tensor_tensor_reduce(out=masked[:, k % 2, m, :], in0=psum[6 + m // 4][:, (m % 4) * S:(m % 4 + 1) * S], in1=masked[:, k % 2, m, :],
                                             scale=1.0, scalar=-3.0e38, op0=ALU.add, op1=ALU.max,
                                             accum_out=smax[:, 1, k % 2, m:m + 1]).then_inc(s_mx[1], 1)
                dve.wait_ge(s_mx[1], HEADS * (n + 1))
                dve.tensor_scalar(bias[:, 1, k % 2, :], smax[:, 1, k % 2, :], -1.0 / math.sqrt(K1), None, ALU.mult).then_inc(s_bias[1], 1)

            def b_den(g, k):
                wait_alone(dve, s_ex[1], g * G + k + 1)
                dve.reciprocal(rden1[:, k % 2, :], den[:, k % 2, :]).then_inc(s_rd1, 1)

            def b_add(g, k):
                dve.wait_ge(s_av[1], g * G + k + 1)
                dve.tensor_tensor(y1[:, k, :], y1[:, k, :], psum[1][:, 0:D], ALU.add).then_inc(s_y, 1)

            def a2_copy_v(g):
                dve.wait_ge(s_v, g + 1)
                dve.tensor_copy(v17[:, :, :, 0:DK], psum[1].rearrange("p (k h c) -> p k h c", k=G, h=HEADS)).then_inc(s_vc, 1)

            def b_copy_k(g, n):
                dve.wait_ge(s_q1, g * 8 + n + 5)
                dve.tensor_copy(kT1[:, n, :], psum[7 - n % 2]).then_inc(s_q1v, 1)

            def a1_add(t):
                dve.wait_ge(s_o, t + 1)
                add_h(t, 0, bank(0))

            def a1_mean(t):
                dve.wait_ge(s_xTc[1], t + 1)
                dve.tensor_reduce(msum[:, :], xT[1][:, :, :], AX.X, ALU.add).then_inc(s_ms, 1)

            def a2_add(g):
                dve.wait_ge(s_wo, g + 1)
                add_h(g, 1, bank(5))

            row = lambda g: lambda k: rows(g, k)
            buf = lambda x: lambda k: x[:, k, :]
            ln_stats(0, 0, row(0))
            ln_apply(0, 0, row(0), buf(xh[0]))

            def body(t, a1, a2, b, c, ahead):
                g2, g3, g4 = t - 1, t - 2, t - 3
                if b:
                    wait_alone(dve, s_h[1], g3 + 1)
                    ln_stats(g3, 2, row(g3))
                if c:
                    copy_ex(g4, 1, 3)
                if b:
                    ln_apply(g3, 2, row(g3), buf(xh[2]))
                if c:
                    b_add(g4, 3)
                    wait_alone(dve, s_y, G * (g4 + 1))
                    ln_stats(g4, 4, buf(y1))
                if a2:
                    a2_max(g2, 0)
                if b:
                    b_copy_k(g3, 0)
                if a2:
                    a2_copy_v(g2)
                if b:
                    b_copy_k(g3, 1)
                if c:
                    ln_apply(g4, 4, buf(y1), buf(y2))
                if b:
                    b_copy_k(g3, 2)
                    b_copy_k(g3, 3)
                if a2:
                    copy_ex(g2, 0, 0)
                if b:
                    b_mask(g3, 0)
                if a2:
                    a2_norm(g2, 0)
                if a1:
                    a1_decay(t)
                if b:
                    b_values(g3, 1)
                if a2:
                    a2_max(g2, 1)
                if a1:
                    a1_silu(t)
                if c:
                    dve.wait_ge(s_gm, 2 * g4 + 2)
                    add_h(g4, 2, y2[:, :, :])
                if a2:
                    copy_ex(g2, 0, 1)
                if a1:
                    a1_add(t)
                if c:
                    wait_alone(dve, s_h[2], g4 + 1)
                    ln_stats(g4, 3, row(g4))
                if b:
                    b_den(g3, 0)
                    b_mask(g3, 1)
                if a2:
                    a2_norm(g2, 1)
                    a2_max(g2, 2)
                if c:
                    if not first(g4):
                        dve.wait_ge(s_tab, 16 * g4)
                    ln_apply(g4, 3, row(g4), buf(xh[3]))
                if b:
                    b_values(g3, 3)
                if a1:
                    wait_alone(dve, s_h[0], t + 1)
                    ln_stats(t, 1, row(t))
                if b:
                    copy_ex(g3, 1, 0)
                if a2:
                    copy_ex(g2, 0, 2)
                if a1:
                    ln_apply(t, 1, row(t), buf(xh[1]))
                if b:
                    dve.wait_ge(s_xb, g3 + 1)
                    b_add(g3, 0)
                    b_den(g3, 1)
                    b_mask(g3, 2)
                if a2:
                    a2_norm(g2, 2)
                    a2_max(g2, 3)
                if b:
                    b_values(g3, 5)
                    copy_ex(g3, 1, 1)
                if a1:
                    a1_mean(t)
                if b:
                    b_add(g3, 1)
                if a2:
                    copy_ex(g2, 0, 3)
                if a1:
                    a1_route(t)
                if b:
                    b_values(g3, 7)
                    b_den(g3, 2)
                    b_mask(g3, 3)
                if a2:
                    a2_norm(g2, 3)
                if b:
                    copy_ex(g3, 1, 2)
                if ahead:
                    ln_stats(t + 1, 0, row(t + 1))
                if b:
                    b_den(g3, 3)
                    b_add(g3, 2)
                if a2:
                    a2_add(g2)
                if ahead:
                    ln_apply(t + 1, 0, row(t + 1), buf(xh[0]))

            def last(t, b):
                c, g3, g4 = True, t - 2, t - 3
                if c:
                    copy_ex(g4, 1, 3)
                if b:
                    wait_alone(dve, s_h[1], g3 + 1)
                    ln_stats(g3, 2, row(g3))
                if c:
                    b_add(g4, 3)
                if b:
                    ln_apply(g3, 2, row(g3), buf(xh[2]))
                if c:
                    wait_alone(dve, s_y, G * (g4 + 1))
                    ln_stats(g4, 4, buf(y1))
                if b:
                    b_copy_k(g3, 0)
                    b_copy_k(g3, 1)
                    b_copy_k(g3, 2)
                    b_copy_k(g3, 3)
                if c:
                    ln_apply(g4, 4, buf(y1), buf(y2))
                if b:
                    b_mask(g3, 0)
                    b_values(g3, 1)
                    b_values(g3, 3)
                    b_mask(g3, 1)
                    b_den(g3, 0)
                    b_values(g3, 5)
                    copy_ex(g3, 1, 0)
                    b_mask(g3, 2)
                    b_den(g3, 1)
                if c:
                    dve.wait_ge(s_gm, 2 * g4 + 2)
                    add_h(g4, 2, y2[:, :, :])
                if b:
                    dve.wait_ge(s_xb, g3 + 1)
                    b_add(g3, 0)
                if c:
                    wait_alone(dve, s_h[2], g4 + 1)
                    ln_stats(g4, 3, row(g4))
                if b:
                    b_mask(g3, 3)
                if c:
                    dve.wait_ge(s_tab, 16 * g4)
                    ln_apply(g4, 3, row(g4), buf(xh[3]))
                if b:
                    b_den(g3, 2)
                    b_values(g3, 7)
                    copy_ex(g3, 1, 1)
                    b_add(g3, 1)
                    copy_ex(g3, 1, 2)
                    b_den(g3, 3)
                    b_add(g3, 2)

            turns(dve, body, last)


U32 = mybir.dt.uint32
N = B * S
CAP = 1024
F = 512
FC = F // P
CHUNKS = P // E
CW = N // CHUNKS
TILES = CAP // P
PARTS = 5
HB = 4


def experts_stage(nc, used, A, H, ident, psall, table, logitsT, w1, w2, s_weights, WEIGHTS, out):
    psum = [psall[:, i, :] for i in range(8)]
    logits_dram = nc.dram_tensor("logits_dram", (E, N), F32, kind="Internal").ap()
    out_rows = out.rearrange("b s d -> (b s) d")
    with ExitStack() as ctx:
        sb = lambda name, shape, dt=F32: ctx.enter_context(nc.sbuf_tensor(name, shape, dt))
        sem = lambda name: used.append(nc.alloc_semaphore(name)) or used[-1]
        b1rows = sb("b1rows", [E * FC, P]); b1 = sb("b1", [P, E, FC]); b2 = sb("b2", [P, E, D])
        prob = sb("prob", [P, CW]); rowmax = sb("rowmax", [P, 1]); m8 = sb("m8", [1, E]); mrow = sb("mrow", [1, P])
        one1 = sb("one1", [1, 1]); negmax = sb("negmax", [P, 1]); rowsum = sb("rowsum", [P, 1]); rsum = sb("rsum", [P, 1])
        same = sb("same", [P, E, CHUNKS]); before = sb("before", [P, E, CHUNKS])
        cand = sb("cand", [P, 3]); bits = sb("bits", [P, 3], I32); take = sb("take", [P, 2, 4])
        count = sb("count", [P, 3]); hits = sb("hits", [P, 3, CW], BF16)
        above = sb("above", [P, CW]); equal = sb("equal", [P, CW]); rank = sb("rank", [P, CW]); ones = sb("ones", [P, CW])
        need = sb("need", [P, 1]); offs = sb("offs", [P, 1]); picked = sb("picked", [P, CW]); slot = sb("slot", [P, CW])
        sloti = sb("sloti", [P, CW], I32); hii = sb("hii", [P, CW], I32); loi = sb("loi", [P, CW], I32)
        hl = sb("hl", [P, 2, CW])
        turned = sb("turned", [P, 3, E, 2, CHUNKS])
        left = sb("left", [P, 2, E, 2, CHUNKS])
        iota_p = sb("iota_p", [P, P]); iota_t = sb("iota_t", [P, TILES]); chunk = sb("chunk", [P, CHUNKS, 2]); lane = sb("lane", [P, 1])
        parts = sb("parts", [P, E, 2 * CHUNKS, PARTS], BF16)
        hot_t = sb("hot_t", [P, 2 * CHUNKS, TILES], BF16); rhs = sb("rhs", [P, 2, 2 * CHUNKS, PARTS, TILES], BF16)
        hot_p = sb("hot_p", [P, 2, 2 * CHUNKS, P], BF16)
        idhi = sb("idhi", [P, TILES]); idx = sb("idx", [P, E, TILES], U32); vals = sb("vals", [P, E, TILES])
        xg = sb("xg", [P, 3, TILES, D]); xgT = sb("xgT", [P, 2, HB * P]); hT = sb("hT", [P, 2, FC, HB * P])
        y = sb("y", [P, 2, TILES, D])

        s_lo = sem("s3_lo"); s_pr = sem("s3_pr"); s_b = sem("s3_b"); s_c = sem("s3_c"); s_cc = sem("s3_cc")
        s_rm = sem("s3_rm"); s_rmT = sem("s3_rmT"); s_m8 = sem("s3_m8"); s_mr = sem("s3_mr"); s_nm = sem("s3_nm"); s_nmc = sem("s3_nmc")
        s_e = sem("s3_e"); s_sum = sem("s3_sum"); s_rs = sem("s3_rs"); s_p = sem("s3_p")
        s_thr = sem("s3_thr"); s_cand = sem("s3_cand"); s_cnt = sem("s3_cnt"); s_tot = sem("s3_tot"); s_take = sem("s3_take"); s_bit = sem("s3_bit")
        s_sel = sem("s3_sel"); s_g = sem("s3_g"); s_off = sem("s3_off"); s_hl = sem("s3_hl"); s_tn = sem("s3_tn"); s_tnc = sem("s3_tnc")
        s_ht = sem("s3_ht"); s_rhs = sem("s3_rhs"); s_hp = sem("s3_hp"); s_ix = sem("s3_ix"); s_id = sem("s3_id"); s_ixc = sem("s3_ixc"); s_b1 = sem("s3_b1"); s_b1c = sem("s3_b1c")
        s_out0 = sem("s3_out0"); s_ga = [sem(f"s3_ga{i}") for i in range(3)]; s_pt = sem("s3_pt"); s_sp = sem("s3_sp"); s_sc = sem("s3_sc")
        s_xt = sem("s3_xt"); s_xtc = sem("s3_xtc"); s_h1 = sem("s3_h1"); s_h1c = sem("s3_h1c"); s_y = sem("s3_y"); s_yb = sem("s3_yb"); s_yc = sem("s3_yc")
        block = ctx.enter_context(nc.Block())
        BITS = 30
        flat = lambda t: t.rearrange("p a b -> p (a b)")

        @block.sync
        def _(sp):
            sp.dma_start(logits_dram, logitsT[:, :]).then_inc(s_lo, 16)
            sp.wait_ge(s_lo, 16)
            sp.dma_start(prob[:, :], logits_dram.rearrange("e (c f) -> (e c) f", f=CW)).then_inc(s_pr, 16)
            sp.wait_ge(s_pr, 16)
            sp.dma_start(b1rows[:, :], A["L1_ffn_b1"].rearrange("e (c f) -> (e c) f", f=P)).then_inc(s_b, 16)
            sp.dma_start(b2[:, :, :], A["L1_ffn_b2"].unsqueeze(0).broadcast_to([P, E, D])).then_inc(s_b, 16)
            sp.dma_start(out.rearrange("b s d -> s b d"), H[:, :, :]).then_inc(s_out0, 16)

        @block.gpsimd
        def _(pool):
            pool.memset(ones[:, :], 1.0).then_inc(s_c, 1)
            pool.memset(flat(same[:, :, :]), 1.0).then_inc(s_cc, 1)
            pool.memset(take[:, 0, 3:4], 0.0).then_inc(s_c, 1)
            for k in range(3):
                pool.memset(bits[:, k:k + 1], (k + 1) << (BITS - 2)).then_inc(s_c, 1)
            pool.memset(one1[:, :], 1.0).then_inc(s_c, 1)
            pool.iota(iota_p[:, :], pattern=[[1, P]], base=0, channel_multiplier=0, allow_small_or_imprecise_dtypes=True).then_inc(s_c, 1)
            pool.iota(iota_t[:, :], pattern=[[1, TILES]], base=0, channel_multiplier=0, allow_small_or_imprecise_dtypes=True).then_inc(s_c, 1)
            pool.iota(chunk[:, :, :], pattern=[[2, CHUNKS], [1, 2]], base=0, channel_multiplier=0, allow_small_or_imprecise_dtypes=True).then_inc(s_c, 1)
            pool.iota(lane[:, :], pattern=[[0, 1]], base=0, channel_multiplier=1, allow_small_or_imprecise_dtypes=True).then_inc(s_c, 1)
            pool.wait_ge(s_cc, 1)
            pool.affine_select(out=same[:, :, :], in_=same[:, :, :], compare_op=ALU.is_ge, fill=0.0, base=0,
                               pattern=[[-CHUNKS, E], [0, CHUNKS]], channel_multiplier=1).then_inc(s_cc, 1)
            pool.wait_ge(s_cc, 2)
            pool.affine_select(out=same[:, :, :], in_=same[:, :, :], compare_op=ALU.is_ge, fill=0.0, base=CHUNKS - 1,
                               pattern=[[CHUNKS, E], [0, CHUNKS]], channel_multiplier=-1).then_inc(s_cc, 1)
            pool.wait_ge(s_cc, 3)
            pool.affine_select(out=flat(before[:, :, :]), in_=flat(same[:, :, :]), compare_op=ALU.is_gt, fill=0.0, base=0,
                               pattern=[[1, P]], channel_multiplier=-1).then_inc(s_cc, 1)

            pool.wait_ge(s_c, 10)
            by = lambda q: parts[:, :, :, q]
            for half in range(2):
                pool.tensor_copy(parts[:, :, half * CHUNKS:(half + 1) * CHUNKS, 0],
                                 chunk[:, :, half].unsqueeze(1).broadcast_to([P, E, CHUNKS])).then_inc(s_sp, 1)
            pool.tensor_copy(by(1), lane[:, :].unsqueeze(2).broadcast_to([P, E, 2 * CHUNKS])).then_inc(s_sp, 1)
            rest = turned[:, 2, :, :, :].rearrange("p e h c -> p e (h c)")
            pool.wait_ge(s_pt, 1)
            for q in range(3):
                pool.tensor_copy(by(2 + q), rest).then_inc(s_sp, 1)
                if q < 2:
                    pool.wait_ge(s_sp, 4 + 2 * q)
                    less = left[:, q, :, :, :].rearrange("p e h c -> p e (h c)")
                    pool.tensor_tensor(less, rest, by(2 + q), ALU.subtract).then_inc(s_sp, 1)
                    pool.wait_ge(s_sp, 5 + 2 * q)
                    rest = less

            def gather(e):
                pool.wait_ge(s_ixc, 2 * e + 2)
                if e >= 3:
                    pool.wait_ge(s_xt, 2 * (e - 2))
                for j in range(TILES):
                    pool.indirect_dma_start(out=xg[:, e % 3, j, :], out_offset=None, in_=table,
                                            in_offset=bass.IndirectOffsetOnAxis(ap=idx[:, e, j:j + 1], axis=0)).then_inc(s_ga[e % 3], 16)

            def scatter(e):
                pool.wait_ge(s_out0, 16)
                if e:
                    pool.wait_ge(s_sc, 16 * TILES * e)
                for j in range(TILES):
                    if j % HB == 0:
                        pool.wait_ge(s_yc, 2 * e + j // HB + 1)
                    pool.indirect_dma_start(out=out_rows, out_offset=bass.IndirectOffsetOnAxis(ap=idx[:, e, j:j + 1], axis=0),
                                            in_=y[:, e % 2, j, :], in_offset=None, compute_op=ALU.add).then_inc(s_sc, 16)

            gather(0)
            gather(1)
            for e in range(E):
                if e + 2 < E:
                    gather(e + 2)
                scatter(e)
            pool.wait_ge(s_sc, 16 * TILES * E)

        @block.tensor
        def _(pe):
            pe.wait_ge(s_rm, 1)
            pe.transpose(psum[1][0:1, 0:P], rowmax[:, :], ident[:, :]).then_inc(s_rmT, 1)
            pe.wait_ge(s_mr, 1)
            pe.matmul(psum[2][:, 0:1], mrow[:, :], one1[:, :], start=True, stop=True).then_inc(s_nm, 1)
            pe.wait_ge(s_cc, 4)
            pe.wait_ge(s_e, 1)
            pe.matmul(psum[3][:, 0:1], flat(same[:, :, :]), rowsum[:, :], start=True, stop=True).then_inc(s_sum, 1)
            pe.wait_ge(s_p, 1)
            for half in range(2):
                mm = pe.transpose(psum[7][:, half * P:(half + 1) * P], prob[:, half * P:(half + 1) * P], ident[:, :])
            mm.then_inc(s_tn, 1)
            for i in range(BITS // 2):
                pe.wait_ge(s_cnt, 3 * (i + 1))
                pe.matmul(psum[4][:, 0:3], flat(same[:, :, :]), count[:, :], start=True, stop=True).then_inc(s_tot, 1)
            pe.wait_ge(s_b, 32)
            pe.transpose(psum[3][:, P:P + E * FC], b1rows[:, :], ident[0:E * FC, 0:E * FC]).then_inc(s_b1, 1)
            pe.wait_ge(s_g, 2)
            pe.matmul(psum[5][:, 0:1], flat(same[:, :, :]), count[:, 0:1], start=True, stop=True)
            pe.matmul(psum[5][:, 1:2], flat(before[:, :, :]), count[:, 1:2], start=True, stop=True).then_inc(s_off, 1)
            pe.wait_ge(s_g, 3)
            pe.matmul(psum[6][:, 0:1], flat(before[:, :, :]), count[:, 0:1], start=True, stop=True).then_inc(s_off, 1)
            pe.wait_ge(s_hl, 2)
            for q, t in enumerate((hl[:, 0, :], hl[:, 1, :])):
                for half in range(2):
                    mm = pe.transpose(psum[q][:, half * P:(half + 1) * P], t[:, half * P:(half + 1) * P], ident[:, :])
                mm.then_inc(s_tn, 1)

            def slots(e):
                pe.wait_ge(s_rhs, e + 1)
                if e:
                    pe.wait_ge(s_ixc, 2 * e)
                for c in range(2 * CHUNKS):
                    if c % CHUNKS == 0:
                        pe.wait_ge(s_hp, 2 * e + c // CHUNKS + 1)
                    mm = pe.matmul(psum[7][:, 0:PARTS * TILES], hot_p[:, e % 2, c, :], rhs[:, e % 2, c, :, :],
                                   start=(c == 0), stop=(c == 2 * CHUNKS - 1))
                mm.then_inc(s_ix, 1)

            def turn_x(n):
                e, u = n // 2, n % 2
                pe.wait_ge(s_ga[e % 3], 16 * TILES * (e // 3 + 1))
                if n:
                    pe.wait_ge(s_xtc, n)
                for j in range(HB):
                    mm = pe.transpose(psum[0][:, j * P:(j + 1) * P], xg[:, e % 3, u * HB + j, :], ident[:, :])
                mm.then_inc(s_xt, 1)

            def hidden(n):
                e, u = n // 2, n % 2
                pe.wait_ge(s_xtc, n + 1)
                for c in range(FC):
                    if n:
                        pe.wait_ge(s_h1c, (n - 1) * FC + c + 1)
                    pe.matmul(psum[2 + c][:, :], w1[:, e, c * P:(c + 1) * P], xgT[:, u, :], start=True, stop=True).then_inc(s_h1, 1)

            def outputs(n):
                e, u = n // 2, n % 2
                if n >= 2:
                    pe.wait_ge(s_yb, n - 1)
                for j in range(HB):
                    for c in range(FC):
                        if j == 0:
                            pe.wait_ge(s_h1c, FC * n + c + 1)
                        mm = pe.matmul(psum[1 + 5 * u][:, j * D:(j + 1) * D], hT[:, u, c, j * P:(j + 1) * P], w2[:, e, c, :],
                                       start=(c == 0), stop=(c == FC - 1))
                mm.then_inc(s_y, 1)

            pe.wait_ge(s_sp, 8)
            slots(0)
            slots(1)
            pe.wait_ge(s_weights, WEIGHTS)
            turn_x(0)
            for e in range(E):
                if e + 2 < E:
                    slots(e + 2)
                hidden(2 * e)
                turn_x(2 * e + 1)
                outputs(2 * e)
                hidden(2 * e + 1)
                if e + 1 < E:
                    turn_x(2 * e + 2)
                outputs(2 * e + 1)

        @block.scalar
        def _(act):
            act.wait_ge(s_nm, 1)
            act.activation(negmax[:, :], psum[2][:, 0:1], ACT.Copy, scale=-1.0).then_inc(s_nmc, 1)
            act.wait_ge(s_nmc, 1)
            act.wait_ge(s_pr, 16)
            act.activation(prob[:, :], prob[:, :], ACT.Exp, bias=negmax[:, :], accum_out=rowsum[:, :]).then_inc(s_e, 1)
            act.wait_ge(s_b1, 1)
            act.activation(b1[:, :, :].rearrange("p e c -> p (e c)"), psum[3][:, P:P + E * FC], ACT.Copy).then_inc(s_b1c, 1)
            act.wait_ge(s_b1c, 1)

            def copy_x(n):
                act.wait_ge(s_xt, n + 1)
                act.activation(xgT[:, n % 2, :], psum[0][:, :], ACT.Copy).then_inc(s_xtc, 1)

            copy_x(0)
            for n in range(2 * E):
                if n >= 2:
                    act.wait_ge(s_y, n - 1)
                for c in range(FC):
                    act.wait_ge(s_h1, n * FC + c + 1)
                    act.activation(hT[:, n % 2, c, :], psum[2 + c][:, :], ACT.Gelu, bias=b1[:, n // 2, c:c + 1]).then_inc(s_h1c, 1)
                if n + 1 < 2 * E:
                    copy_x(n + 1)

        @block.vector
        def _(dve):
            dve.wait_ge(s_pr, 16)
            dve.wait_ge(s_c, 10)
            dve.tensor_reduce(rowmax[:, :], prob[:, :], AX.X, ALU.max).then_inc(s_rm, 1)
            dve.wait_ge(s_rmT, 1)
            dve.tensor_reduce(m8[:, :], psum[1][0:1, 0:P].rearrange("p (e c) -> p e c", e=E), AX.X, ALU.max).then_inc(s_m8, 1)
            dve.wait_ge(s_m8, 1)
            dve.tensor_copy(mrow[:, :].rearrange("p (e c) -> p e c", e=E), m8[:, :].unsqueeze(2).broadcast_to([1, E, CHUNKS])).then_inc(s_mr, 1)
            dve.wait_ge(s_sum, 1)
            dve.reciprocal(rsum[:, :], psum[3][:, 0:1]).then_inc(s_rs, 1)
            dve.wait_ge(s_rs, 1)
            dve.tensor_scalar(prob[:, :], prob[:, :], rsum[:, :], None, ALU.mult).then_inc(s_p, 1)
            dve.wait_ge(s_p, 1)
            for i in range(BITS // 2):
                thr = take[:, i % 2, 3:4]
                if i == 1:
                    dve.wait_ge(s_tn, 1)
                    dve.tensor_copy(turned[:, 2, :, :, :].rearrange("p e h c -> p h e c"),
                                    psum[7][:, 0:2 * P].rearrange("p (h e c) -> p h e c", h=2, e=E)).then_inc(s_pt, 1)
                dve.tensor_tensor(cand[:, :].bitcast(I32), thr.bitcast(I32).broadcast_to([P, 3]), bits[:, :], ALU.bitwise_or).then_inc(s_cand, 1)
                dve.wait_ge(s_cand, i + 1)
                for k in range(3):
                    dve.tensor_scalar(hits[:, k, :], prob[:, :], cand[:, k:k + 1], 0.0, ALU.is_ge, ALU.add, accum_out=count[:, k:k + 1]).then_inc(s_cnt, 1)
                dve.tensor_scalar(bits[:, :], bits[:, :], 2, None, ALU.logical_shift_right).then_inc(s_bit, 1)
                dve.wait_ge(s_tot, i + 1)
                dve.scalar_tensor_tensor(take[:, i % 2, 0:3], psum[4][:, 0:3], CAP - 0.5, cand[:, :], ALU.is_ge, ALU.mult).then_inc(s_take, 1)
                dve.wait_ge(s_take, i + 1)
                dve.wait_ge(s_bit, i + 1)
                dve.tensor_reduce(take[:, (i + 1) % 2, 3:4], take[:, i % 2, :], AX.X, ALU.max).then_inc(s_thr, 1)
                dve.wait_ge(s_thr, i + 1)
            thr = take[:, (BITS // 2) % 2, 3:4]
            dve.tensor_scalar(above[:, :], prob[:, :], thr, 0.0, ALU.is_gt, ALU.add, accum_out=count[:, 0:1]).then_inc(s_g, 1)
            dve.tensor_scalar(equal[:, :], prob[:, :], thr, 0.0, ALU.is_equal, ALU.add, accum_out=count[:, 1:2]).then_inc(s_g, 1)
            dve.wait_ge(s_g, 2)
            dve.tensor_tensor_scan(rank[:, :], ones[:, :], equal[:, :], 0.0, ALU.mult, ALU.add).then_inc(s_sel, 1)
            dve.wait_ge(s_off, 1)
            dve.tensor_scalar(offs[:, :], psum[5][:, 0:1], -1.0, float(CAP), ALU.mult, ALU.add).then_inc(s_sel, 1)
            dve.wait_ge(s_sel, 2)
            dve.tensor_tensor(need[:, :], offs[:, :], psum[5][:, 1:2], ALU.subtract).then_inc(s_sel, 1)
            dve.wait_ge(s_sel, 3)
            dve.scalar_tensor_tensor(picked[:, :], rank[:, :], need[:, :], equal[:, :], ALU.is_le, ALU.mult).then_inc(s_sel, 1)
            dve.wait_ge(s_sel, 4)
            dve.tensor_tensor(picked[:, :], picked[:, :], above[:, :], ALU.add).then_inc(s_sel, 1)
            dve.wait_ge(s_sel, 5)
            dve.tensor_tensor_scan(rank[:, :], ones[:, :], picked[:, :], 0.0, ALU.mult, ALU.add).then_inc(s_sel, 1)
            dve.wait_ge(s_sel, 6)
            dve.tensor_copy(count[:, 0:1], rank[:, CW - 1:CW]).then_inc(s_g, 1)
            dve.wait_ge(s_off, 2)
            dve.scalar_tensor_tensor(slot[:, :], rank[:, :], psum[6][:, 0:1], picked[:, :], ALU.add, ALU.mult).then_inc(s_sel, 1)
            dve.wait_ge(s_sel, 7)
            dve.tensor_scalar(sloti[:, :], slot[:, :], -1.0, None, ALU.add).then_inc(s_sel, 1)
            dve.wait_ge(s_sel, 8)
            dve.tensor_scalar(hii[:, :], sloti[:, :], 3, None, ALU.arith_shift_right).then_inc(s_sel, 1)
            dve.tensor_scalar(loi[:, :], sloti[:, :], TILES - 1, None, ALU.bitwise_and).then_inc(s_sel, 1)
            dve.wait_ge(s_sel, 10)
            dve.tensor_copy(hl[:, 0, :], hii[:, :]).then_inc(s_hl, 1)
            dve.tensor_copy(hl[:, 1, :], loi[:, :]).then_inc(s_hl, 1)
            for q in range(2):
                dve.wait_ge(s_tn, q + 2)
                dve.tensor_copy(turned[:, q, :, :, :].rearrange("p e h c -> p h e c"),
                                psum[q][:, 0:2 * P].rearrange("p (h e c) -> p h e c", h=2, e=E)).then_inc(s_tnc, 1)
            dve.wait_ge(s_tnc, 2)
            dve.wait_ge(s_sp, 8)

            of = lambda q, e: turned[:, q, e, :, :].rearrange("p h c -> p (h c)")

            def tiles(e):
                if e >= 2:
                    dve.wait_ge(s_ix, e - 1)
                if e:
                    dve.wait_ge(s_rhs, e)
                dve.tensor_tensor(hot_t[:, :, :], of(1, e).unsqueeze(2).broadcast_to([P, 2 * CHUNKS, TILES]),
                                  iota_t[:, :].unsqueeze(1).broadcast_to([P, 2 * CHUNKS, TILES]), ALU.is_equal).then_inc(s_ht, 1)
                dve.wait_ge(s_ht, e + 1)
                dve.tensor_tensor(rhs[:, e % 2, :, :, :], hot_t[:, :, :].unsqueeze(2).broadcast_to([P, 2 * CHUNKS, PARTS, TILES]),
                                  parts[:, e, :, :].unsqueeze(3).broadcast_to([P, 2 * CHUNKS, PARTS, TILES]), ALU.mult).then_inc(s_rhs, 1)

            def lanes(e):
                for half in range(2):
                    k = slice(half * CHUNKS, (half + 1) * CHUNKS)
                    dve.tensor_tensor(hot_p[:, e % 2, k, :], of(0, e)[:, k].unsqueeze(2).broadcast_to([P, CHUNKS, P]),
                                      iota_p[:, :].unsqueeze(1).broadcast_to([P, CHUNKS, P]), ALU.is_equal).then_inc(s_hp, 1)

            def told(e):
                dve.wait_ge(s_ix, e + 1)
                dve.tensor_scalar(idhi[:, :], psum[7][:, 0:TILES], float(P), None, ALU.mult).then_inc(s_id, 1)
                dve.tensor_reduce(vals[:, e, :], psum[7][:, 2 * TILES:PARTS * TILES].rearrange("p (q t) -> p t q", t=TILES), AX.X, ALU.add).then_inc(s_ixc, 1)
                dve.wait_ge(s_id, e + 1)
                dve.tensor_tensor(idx[:, e, :], idhi[:, :], psum[7][:, TILES:2 * TILES], ALU.add).then_inc(s_ixc, 1)

            def weighted(n):
                e, u = n // 2, n % 2
                dve.wait_ge(s_y, n + 1)
                if e >= 2:
                    dve.wait_ge(s_sc, 16 * TILES * (e - 1))
                part = y[:, e % 2, u * HB:(u + 1) * HB, :]
                dve.tensor_tensor(part, psum[1 + 5 * u][:, :].rearrange("p (j d) -> p j d", j=HB), b2[:, e:e + 1, :].broadcast_to([P, HB, D]),
                                  ALU.add).then_inc(s_yb, 1)
                dve.wait_ge(s_yb, n + 1)
                dve.tensor_tensor(part, part, vals[:, e, u * HB:(u + 1) * HB].unsqueeze(2).broadcast_to([P, HB, D]), ALU.mult).then_inc(s_yc, 1)

            tiles(0)
            lanes(0)
            tiles(1)
            told(0)
            lanes(1)
            tiles(2)
            told(1)
            lanes(2)
            for e in range(E):
                if e + 2 < E:
                    told(e + 2)
                weighted(2 * e)
                if e + 3 < E:
                    tiles(e + 3)
                    lanes(e + 3)
                weighted(2 * e + 1)


def tower_kernel(nc, A, out):
    table = nc.dram_tensor("token_table", (N, D), F32, kind="Internal").ap()
    with ExitStack() as ctx:
        sb = lambda name, shape, dt=F32: ctx.enter_context(nc.sbuf_tensor(name, shape, dt))
        psall = ctx.enter_context(nc.psum_tensor("banks", [P, 8, 512], F32))
        H = sb("H", [P, B, D])
        ident = sb("ident", [P, P])

        def fresh():
            nc.clear_and_free_semaphores(used)
            nc.all_engine_barrier()
            used.clear()

        W = {name: sb(name, shape) for name, shape in WEIGHT_SHAPES.items()}
        used = []
        alignment_stage(nc, used, A, H, ident, [psall[:, i, :] for i in range(8)], W)
        fresh()
        logitsT = sb("logitsT", [E, N])
        w1 = sb("w1", [P, E, F])
        w2 = sb("w2", [P, E, FC, D])
        s_weights = ctx.enter_context(nc.semaphore("s_weights"))
        layers_stage(nc, used, A, H, ident, psall, W, table, logitsT, w1, w2, s_weights)
        fresh()
        experts_stage(nc, used, A, H, ident, psall, table, logitsT, w1, w2, s_weights, 16 * (1 + E), out)


_OUT = (B, S, D)


def kernel(**inputs):
    import numpy as _np
    import concourse.bacc as _bacc
    from concourse import mybir as _mybir
    from concourse.bass_utils import run_bass_kernel_spmd as _run

    nc = _bacc.Bacc("TRN2", target_bir_lowering=False, num_devices=1)
    arrays, A = {}, {}
    for name, value in inputs.items():
        a = _np.ascontiguousarray(value)
        arrays[f"in_{name}"] = a
        A[name] = nc.dram_tensor(f"in_{name}", a.shape, _mybir.dt.from_np(a.dtype), kind="ExternalInput").ap()
    out = nc.dram_tensor("out_h", _OUT, F32, kind="ExternalOutput").ap()
    tower_kernel(nc, A, out)
    r = _run(nc, [arrays], core_ids=[0])
    return r.results[0]["out_h"]
```
